# Optimizing a Trainium2 kernel written in Bass

```python
import numpy as np
import jax
import jax.numpy as jnp

def _softmax(x, axis=-1):
    return jax.nn.softmax(x, axis=axis)
def _gelu(x):
    return jax.nn.gelu(x, approximate=True)
def _silu(x):
    return jax.nn.silu(x)
def _sigmoid(x):
    return jax.nn.sigmoid(x)
def _layernorm(x, axis=-1, eps=1e-5):
    m = jnp.mean(x, axis=axis, keepdims=True)
    v = jnp.var(x, axis=axis, keepdims=True)
    return (x - m) / jnp.sqrt(v + eps)
def _scatter_add(tgt, idx, src, axis=0):
    return tgt.at[idx].add(src)
def _segment_sum(src, seg, n):
    return jax.ops.segment_sum(src, seg, n)

kernel_name = 'mk_dlrm_tower_d1_rec_747c1c'

def setup_inputs(seed: int = 0):
    np.random.seed(seed)
    _w = jnp.asarray
    def _rec_inputs():
        import jax
        import jax.numpy as jnp
        _tk = jax.random.key(seed)
        ids = jnp.stack([jax.random.randint(jax.random.fold_in(_tk, 200 + f), (1024,), 0, v, jnp.int32) for f, v in enumerate([10000, 100000, 100000, 1000])], axis=1)
        tbl_0 = 0.05 * jax.random.normal(jax.random.fold_in(_tk, 500 + 0), (10000, 4), jnp.float32)
        tbl_1 = 0.05 * jax.random.normal(jax.random.fold_in(_tk, 500 + 1), (100000, 4), jnp.float32)
        tbl_2 = 0.05 * jax.random.normal(jax.random.fold_in(_tk, 500 + 2), (100000, 4), jnp.float32)
        tbl_3 = 0.05 * jax.random.normal(jax.random.fold_in(_tk, 500 + 3), (1000, 4), jnp.float32)
        _rk = jax.random.fold_in(_tk, 7)
        r_x = 7.22013e-05 + 1.00017 * jax.random.normal(jax.random.fold_in(_rk, 101), (1024, 2048), jnp.float32)
        W_top1 = 0.0197642 * jax.random.normal(jax.random.fold_in(_tk, 801), (2560, 512), jnp.float32)
        W_top2 = 0.0441942 * jax.random.normal(jax.random.fold_in(_tk, 802), (512, 256), jnp.float32)
        W_top3 = 0.0625 * jax.random.normal(jax.random.fold_in(_tk, 803), (256, 1), jnp.float32)
        b_top1 = jnp.zeros((512,), jnp.float32)
        b_top2 = jnp.zeros((256,), jnp.float32)
        return r_x, ids, tbl_0, tbl_1, tbl_2, tbl_3, W_top1, b_top1, W_top2, b_top2, W_top3
    r_x, ids, tbl_0, tbl_1, tbl_2, tbl_3, W_top1, b_top1, W_top2, b_top2, W_top3 = _rec_inputs()
    def _L0_rec_setup():
        import jax, jax.numpy as jnp
        import numpy as np
        B, IN, HID, D, N, OUT = (4096, 2048, 2048, 512, 4, 512)
        H = 8
        HD = D // H

        def _ln(x, g, b):
            m = x.mean(-1, keepdims=True)
            v = ((x - m) ** 2).mean(-1, keepdims=True)
            return (x - m) / jnp.sqrt(v + 1e-05) * g + b
        key = jax.random.key(seed)
        ks = jax.random.split(key, 32)

        def nrm(k, shape, scale=0.02):
            return jax.random.normal(k, shape, jnp.float32) * scale
        inp = {}
        inp['x'] = jax.random.normal(ks[0], (B, IN), jnp.float32)
        inp['strength'] = jax.random.uniform(ks[1], (B, N, N), jnp.float32)
        for t, i in (('er', 2), ('ei', 4)):
            inp[t + '_W1'] = nrm(ks[i], (HID, IN))
            inp[t + '_b1'] = jnp.zeros((HID,), jnp.float32)
            inp[t + '_g1'] = jnp.ones((HID,), jnp.float32)
            inp[t + '_be1'] = jnp.zeros((HID,), jnp.float32)
            inp[t + '_W2'] = nrm(ks[i + 1], (N * D, HID))
            inp[t + '_b2'] = jnp.zeros((N * D,), jnp.float32)
        names = ['Wq_r', 'Wq_i', 'Wk_r', 'Wk_i', 'Wv_r', 'Wv_i', 'Wo_r', 'Wo_i']
        for j, nm in enumerate(names):
            inp[nm] = nrm(ks[6 + j], (D, D))
            inp['b' + nm[1:]] = jnp.zeros((D,), jnp.float32)
        inp['int_Wr'] = jnp.tile(jnp.eye(D, dtype=jnp.float32)[None], (N, 1, 1))
        inp['int_Wi'] = jnp.zeros((N, D, D), jnp.float32)
        inp['meas_Mr'] = nrm(ks[20], (OUT, D), 1.0 / np.sqrt(D))
        inp['meas_Mi'] = nrm(ks[21], (OUT, D), 1.0 / np.sqrt(D))
        inp['post_W'] = nrm(ks[22], (OUT, OUT))
        inp['post_b'] = jnp.zeros((OUT,), jnp.float32)
        inp['post_g'] = jnp.ones((OUT,), jnp.float32)
        inp['post_be'] = jnp.zeros((OUT,), jnp.float32)
        return inp
    _L0_rec_all = _L0_rec_setup()
    _L0_rec_in = {k: v for k, v in _L0_rec_all.items() if k in ('er_W1', 'er_b1', 'er_g1', 'er_be1', 'er_W2', 'er_b2', 'ei_W1', 'ei_b1', 'ei_g1', 'ei_be1', 'ei_W2', 'ei_b2', 'Wq_r', 'bq_r', 'Wq_i', 'bq_i', 'Wk_r', 'bk_r', 'Wk_i', 'bk_i', 'Wv_r', 'bv_r', 'Wv_i', 'bv_i', 'Wo_r', 'bo_r', 'Wo_i', 'bo_i', 'int_Wr', 'int_Wi', 'meas_Mr', 'meas_Mi', 'post_W', 'post_b', 'post_g', 'post_be', )}
    del _L0_rec_all

    return {
        "r_x": r_x,
        "ids": ids,
        "tbl_0": tbl_0,
        "tbl_1": tbl_1,
        "tbl_2": tbl_2,
        "tbl_3": tbl_3,
        "W_top1": W_top1,
        "b_top1": b_top1,
        "W_top2": W_top2,
        "b_top2": b_top2,
        "W_top3": W_top3,
        "L0_rec_er_W1": _L0_rec_in["er_W1"],
        "L0_rec_er_b1": _L0_rec_in["er_b1"],
        "L0_rec_er_g1": _L0_rec_in["er_g1"],
        "L0_rec_er_be1": _L0_rec_in["er_be1"],
        "L0_rec_er_W2": _L0_rec_in["er_W2"],
        "L0_rec_er_b2": _L0_rec_in["er_b2"],
        "L0_rec_ei_W1": _L0_rec_in["ei_W1"],
        "L0_rec_ei_b1": _L0_rec_in["ei_b1"],
        "L0_rec_ei_g1": _L0_rec_in["ei_g1"],
        "L0_rec_ei_be1": _L0_rec_in["ei_be1"],
        "L0_rec_ei_W2": _L0_rec_in["ei_W2"],
        "L0_rec_ei_b2": _L0_rec_in["ei_b2"],
        "L0_rec_Wq_r": _L0_rec_in["Wq_r"],
        "L0_rec_bq_r": _L0_rec_in["bq_r"],
        "L0_rec_Wq_i": _L0_rec_in["Wq_i"],
        "L0_rec_bq_i": _L0_rec_in["bq_i"],
        "L0_rec_Wk_r": _L0_rec_in["Wk_r"],
        "L0_rec_bk_r": _L0_rec_in["bk_r"],
        "L0_rec_Wk_i": _L0_rec_in["Wk_i"],
        "L0_rec_bk_i": _L0_rec_in["bk_i"],
        "L0_rec_Wv_r": _L0_rec_in["Wv_r"],
        "L0_rec_bv_r": _L0_rec_in["bv_r"],
        "L0_rec_Wv_i": _L0_rec_in["Wv_i"],
        "L0_rec_bv_i": _L0_rec_in["bv_i"],
        "L0_rec_Wo_r": _L0_rec_in["Wo_r"],
        "L0_rec_bo_r": _L0_rec_in["bo_r"],
        "L0_rec_Wo_i": _L0_rec_in["Wo_i"],
        "L0_rec_bo_i": _L0_rec_in["bo_i"],
        "L0_rec_int_Wr": _L0_rec_in["int_Wr"],
        "L0_rec_int_Wi": _L0_rec_in["int_Wi"],
        "L0_rec_meas_Mr": _L0_rec_in["meas_Mr"],
        "L0_rec_meas_Mi": _L0_rec_in["meas_Mi"],
        "L0_rec_post_W": _L0_rec_in["post_W"],
        "L0_rec_post_b": _L0_rec_in["post_b"],
        "L0_rec_post_g": _L0_rec_in["post_g"],
        "L0_rec_post_be": _L0_rec_in["post_be"],
    }

def reference(r_x, ids, tbl_0, tbl_1, tbl_2, tbl_3, W_top1, b_top1, W_top2, b_top2, W_top3, L0_rec_er_W1, L0_rec_er_b1, L0_rec_er_g1, L0_rec_er_be1, L0_rec_er_W2, L0_rec_er_b2, L0_rec_ei_W1, L0_rec_ei_b1, L0_rec_ei_g1, L0_rec_ei_be1, L0_rec_ei_W2, L0_rec_ei_b2, L0_rec_Wq_r, L0_rec_bq_r, L0_rec_Wq_i, L0_rec_bq_i, L0_rec_Wk_r, L0_rec_bk_r, L0_rec_Wk_i, L0_rec_bk_i, L0_rec_Wv_r, L0_rec_bv_r, L0_rec_Wv_i, L0_rec_bv_i, L0_rec_Wo_r, L0_rec_bo_r, L0_rec_Wo_i, L0_rec_bo_i, L0_rec_int_Wr, L0_rec_int_Wi, L0_rec_meas_Mr, L0_rec_meas_Mi, L0_rec_post_W, L0_rec_post_b, L0_rec_post_g, L0_rec_post_be):
    import jax
    import jax.numpy as jnp
    def _L0_rec_ref(x, strength, er_W1, er_b1, er_g1, er_be1, er_W2, er_b2, ei_W1, ei_b1, ei_g1, ei_be1, ei_W2, ei_b2, Wq_r, bq_r, Wq_i, bq_i, Wk_r, bk_r, Wk_i, bk_i, Wv_r, bv_r, Wv_i, bv_i, Wo_r, bo_r, Wo_i, bo_i, int_Wr, int_Wi, meas_Mr, meas_Mi, post_W, post_b, post_g, post_be):
        import jax, jax.numpy as jnp
        import numpy as np
        B, IN, HID, D, N, OUT = (4096, 2048, 2048, 512, 4, 512)
        H = 8
        HD = D // H

        def _ln(x, g, b):
            m = x.mean(-1, keepdims=True)
            v = ((x - m) ** 2).mean(-1, keepdims=True)
            return (x - m) / jnp.sqrt(v + 1e-05) * g + b
        Bsz = x.shape[0]

        def enc(W1, b1, g, be, W2, b2):
            h = jax.nn.gelu(_ln(x @ W1.T + b1, g, be), approximate=False)
            return (h @ W2.T + b2).reshape(Bsz, N, D)
        sr = enc(er_W1, er_b1, er_g1, er_be1, er_W2, er_b2)
        si = enc(ei_W1, ei_b1, ei_g1, ei_be1, ei_W2, ei_b2)

        def heads(t):
            return t.reshape(Bsz, N, H, HD).transpose(0, 2, 1, 3)
        qr = heads(sr @ Wq_r.T + bq_r)
        qi = heads(si @ Wq_i.T + bq_i)
        kr = heads(sr @ Wk_r.T + bk_r)
        ki = heads(si @ Wk_i.T + bk_i)
        vr = heads(sr @ Wv_r.T + bv_r)
        vi = heads(si @ Wv_i.T + bv_i)
        ar = jnp.einsum('bhnd,bhmd->bhnm', qr, kr) + jnp.einsum('bhnd,bhmd->bhnm', qi, ki)
        ai = jnp.einsum('bhnd,bhmd->bhnm', qi, kr) - jnp.einsum('bhnd,bhmd->bhnm', qr, ki)
        mag = jnp.sqrt(ar ** 2 + ai ** 2 + 1e-08) * HD ** (-0.5)
        w = jax.nn.softmax(mag, axis=-1)
        out_r = jnp.einsum('bhnm,bhmd->bhnd', w, vr).transpose(0, 2, 1, 3).reshape(Bsz, N, D)
        out_i = jnp.einsum('bhnm,bhmd->bhnd', w, vi).transpose(0, 2, 1, 3).reshape(Bsz, N, D)
        attn_r = out_r @ Wo_r.T + bo_r
        attn_i = out_i @ Wo_i.T + bo_i
        R = jnp.einsum('bnd,ned->bne', attn_r, int_Wr) - jnp.einsum('bnd,ned->bne', attn_i, int_Wi)
        I = jnp.einsum('bnd,ned->bne', attn_r, int_Wi) + jnp.einsum('bnd,ned->bne', attn_i, int_Wr)
        Ri, Ii = (R[:, :, None, :], I[:, :, None, :])
        Rj, Ij = (R[:, None, :, :], I[:, None, :, :])
        phase = jnp.arctan2(Ii * Rj - Ri * Ij, Ri * Rj + Ii * Ij)
        f = jnp.cos(phase) * strength[..., None]
        sup_r = jnp.einsum('bijd,bjd->bd', f, R)
        sup_i = jnp.einsum('bijd,bjd->bd', f, I)
        norm = jnp.sqrt(jnp.sum(sup_r ** 2 + sup_i ** 2, axis=-1, keepdims=True) + 1e-08)
        sup_r = sup_r / norm
        sup_i = sup_i / norm
        mr = sup_r @ meas_Mr.T - sup_i @ meas_Mi.T
        mi = sup_r @ meas_Mi.T + sup_i @ meas_Mr.T
        amp = jnp.sqrt(mr ** 2 + mi ** 2)
        out = jax.nn.gelu(_ln(amp @ post_W.T + post_b, post_g, post_be), approximate=False)
        return out

    e = jnp.stack([tbl_0[ids[:, 0]], tbl_1[ids[:, 1]], tbl_2[ids[:, 2]], tbl_3[ids[:, 3]]], axis=1)
    z = _L0_rec_ref(r_x, e, L0_rec_er_W1, L0_rec_er_b1, L0_rec_er_g1, L0_rec_er_be1, L0_rec_er_W2, L0_rec_er_b2, L0_rec_ei_W1, L0_rec_ei_b1, L0_rec_ei_g1, L0_rec_ei_be1, L0_rec_ei_W2, L0_rec_ei_b2, L0_rec_Wq_r, L0_rec_bq_r, L0_rec_Wq_i, L0_rec_bq_i, L0_rec_Wk_r, L0_rec_bk_r, L0_rec_Wk_i, L0_rec_bk_i, L0_rec_Wv_r, L0_rec_bv_r, L0_rec_Wv_i, L0_rec_bv_i, L0_rec_Wo_r, L0_rec_bo_r, L0_rec_Wo_i, L0_rec_bo_i, L0_rec_int_Wr, L0_rec_int_Wi, L0_rec_meas_Mr, L0_rec_meas_Mi, L0_rec_post_W, L0_rec_post_b, L0_rec_post_g, L0_rec_post_be)
    z = z.reshape(z.shape[0], -1)
    h = jnp.concatenate([z, r_x], axis=1)
    h = jnp.maximum(h @ W_top1 + b_top1, 0.0)
    h = jnp.maximum(h @ W_top2 + b_top2, 0.0)
    y = h @ W_top3
    return y


_drawn_inputs = setup_inputs


def setup_inputs(seed=0):
    import zlib

    import numpy as np

    out = dict(_drawn_inputs(seed))
    spreads = {'b_top1': (0.0, 0.1),
     'b_top2': (0.0, 0.1),
     'L0_rec_er_b1': (0.0, 0.8),
     'L0_rec_er_g1': (1.0, 0.6),
     'L0_rec_er_be1': (0.0, 0.8),
     'L0_rec_er_b2': (0.0, 0.8),
     'L0_rec_ei_b1': (0.0, 0.8),
     'L0_rec_ei_g1': (1.0, 0.6),
     'L0_rec_ei_be1': (0.0, 0.8),
     'L0_rec_ei_b2': (0.0, 0.8),
     'L0_rec_bq_r': (0.0, 0.8),
     'L0_rec_bq_i': (0.0, 0.8),
     'L0_rec_bk_r': (0.0, 0.8),
     'L0_rec_bk_i': (0.0, 0.8),
     'L0_rec_bv_r': (0.0, 0.1),
     'L0_rec_bv_i': (0.0, 0.1),
     'L0_rec_bo_r': (0.0, 0.1),
     'L0_rec_bo_i': (0.0, 0.1),
     'L0_rec_int_Wi': (0.0, 0.1),
     'L0_rec_post_b': (0.0, 0.1),
     'L0_rec_post_g': (1.0, 0.2),
     'L0_rec_post_be': (0.0, 0.1)}
    factors = {'L0_rec_Wq_r': 8.0, 'L0_rec_Wq_i': 8.0, 'L0_rec_Wk_r': 8.0, 'L0_rec_Wk_i': 8.0}
    for name, (base, spread) in spreads.items():
        noise = np.random.default_rng([zlib.crc32(name.encode()), seed]).standard_normal(out[name].shape)
        drawn = base * np.exp(spread * noise) if base else spread * noise
        out[name] = jnp.asarray(drawn.astype(out[name].dtype))
    for name, factor in factors.items():
        out[name] = (out[name] * factor).astype(out[name].dtype)
    return out
```

```python
import concourse.bass as bass
from concourse import mybir
from contextlib import ExitStack

F32 = mybir.dt.float32
F32R = mybir.dt.float32r
I32 = mybir.dt.int32
ALU = mybir.AluOpType
ACT = mybir.ActivationFunctionType
AX = mybir.AxisListType

P = 128
B = 1024
BT = B // P
IN = 2048
HID = 2048
D = 512
N = 4
HEADS = 8
HD = D // HEADS
OUT = 512
KT = IN // P
DC = D // P
CH = 512
NCH = 2 * HID // CH + 1
ECH = HID // CH
LN_EPS = 1e-5


def split_product(nc, out, stat, move, start, stop):
    (sh, sl), (mh, ml) = stat, move
    nc.tensor.matmul(out, sh, mh, start=start, stop=False)
    nc.tensor.matmul(out, sh, ml, start=False, stop=False)
    return nc.tensor.matmul(out, sl, mh, start=False, stop=stop)


class Sems:

    def __init__(self, nc, keep, ctx, phase):
        self.nc, self.keep, self.ctx, self.phase, self.engines_own = nc, keep, ctx, phase, []

    def one(self, name):
        self.engines_own.append(self.ctx.enter_context(self.nc.semaphore(f"{self.phase}_{name}")))
        return self.engines_own[-1]

    def dma(self, name):
        return self.keep.enter_context(self.nc.semaphore(f"{self.phase}_{name}"))

    def ring(self, name, n):
        return [self.dma(f"{name}{i}") for i in range(n)]

    def block(self):
        self.ctx.callback(self.clear)
        return self.ctx.enter_context(self.nc.Block(no_gpsimd_drain=True))

    def clear(self):
        with self.nc.Block(no_gpsimd_drain=True) as block:
            @block.sync
            def _(sp):
                for sem in self.engines_own:
                    sp.sem_clear(sem)


def products_with_x(nc, keep, xT, wA, bA, h_dram, stats):
    PAIR, PAIRS = 2, KT // 2
    RAW, SPL, XRAW, HO = 4, 2, 2, BT
    AHEAD = 1
    with ExitStack() as ctx:
        def sb(name, shape, dt=F32):
            return ctx.enter_context(nc.sbuf_tensor(name, shape, dt))
        x_raw = sb("x_raw", [P, XRAW, B])
        x_hi = sb("x_hi", [P, KT, B], F32R)
        x_lo = sb("x_lo", [P, KT, B], F32R)
        w_raw = sb("wA_raw", [P, RAW, PAIR * CH])
        w_hi = sb("wA_hi", [P, SPL, PAIR * CH], F32R)
        w_lo = sb("wA_lo", [P, SPL, PAIR * CH], F32R)
        bias = sb("bA_all", [P, NCH * CH])
        h_out = sb("h_out", [P, HO, CH])
        acc = [ctx.enter_context(nc.psum_tensor(f"accA{t}", [P, CH], F32)) for t in range(BT)]
        s = Sems(nc, keep, ctx, "A")
        x_loaded = s.ring("x_loaded", XRAW)
        w_loaded = s.ring("w_loaded", RAW)
        bias_loaded = s.dma("bias_loaded")
        x_hi_ready, x_split = s.one("x_hi_ready"), s.one("x_split")
        w_hi_ready, w_split = s.one("w_hi_ready"), s.one("w_split")
        w_used = s.one("w_used")
        acc_ready, acc_taken = s.one("acc_ready"), s.one("acc_taken")
        stats_done = s.one("stats_done")
        h_stored = s.ring("h_stored", HO)
        block = s.block()

        @block.sync
        def _(sp):
            def load_w(c, j):
                if not (isinstance(c, int) and c * PAIRS + j < RAW):
                    sp.wait_ge(w_split, c * PAIRS + j - RAW + 1)
                sp.dma_start(w_raw[:, j % RAW, :], wA[c, j]).then_inc(w_loaded[j % RAW], 16)

            for j in range(PAIRS):
                for k in range(PAIR * j, PAIR * j + PAIR):
                    if k >= XRAW:
                        sp.wait_ge(x_split, k - XRAW + 1)
                    sp.dma_start(x_raw[:, k % XRAW, :], xT[k]).then_inc(x_loaded[k % XRAW], 16)
                load_w(0, j)
            sp.dma_start(bias[:, :], bA.to_broadcast([P, NCH * CH])).then_inc(bias_loaded, 16)
            with sp.Fori(1, NCH) as c:
                for j in range(PAIRS):
                    load_w(c, j)

        @block.scalar
        def _(act):
            def split_w(c, j):
                act.wait_ge(w_loaded[j % RAW], (c * (PAIRS // RAW) + j // RAW + 1) * 16)
                if j >= SPL:
                    act.wait_ge(w_used, c * (PAIRS - 1) + j - SPL + 1)
                elif not (isinstance(c, int) and c == 0):
                    if j == SPL - 1:
                        act.wait_ge(acc_ready, c * BT)
                    else:
                        act.wait_ge(w_used, c * (PAIRS - 1) + j - SPL + 2)
                nc.scalar.activation(w_hi[:, j % SPL, :], w_raw[:, j % RAW, :], ACT.Copy).then_inc(w_hi_ready, 1)

            for j in range(PAIRS):
                for k in range(PAIR * j, PAIR * j + PAIR):
                    act.wait_ge(x_loaded[k % XRAW], (k // XRAW + 1) * 16)
                    nc.scalar.activation(x_hi[:, k, :], x_raw[:, k % XRAW, :], ACT.Copy).then_inc(x_hi_ready, 1)
                split_w(0, j)
            with act.Fori(1, NCH) as c:
                for j in range(PAIRS):
                    split_w(c, j)

        @block.vector
        def _(dve):
            def split_w(c, j):
                dve.wait_ge(w_hi_ready, c * PAIRS + j + 1)
                nc.vector.tensor_tensor(w_lo[:, j % SPL, :], w_raw[:, j % RAW, :],
                                        w_hi[:, j % SPL, :].bitcast(F32), ALU.subtract).then_inc(w_split, 1)

            def take(c):
                for t in range(BT):
                    dve.wait_ge(acc_ready, c * BT + t + 1)
                    if not (isinstance(c, int) and c == 0):
                        dve.wait_ge(h_stored[t], c * 16)
                    nc.vector.tensor_tensor(h_out[:, t, :], acc[t][:, :], bias[:, bass.ts(c, CH)],
                                            ALU.add).then_inc(acc_taken, 1)
                for t in range(BT):
                    dve.wait_ge(acc_taken, c * BT + t + 1)
                    nc.vector.bn_stats(stats[:, c, t, :], h_out[:, t, :]).then_inc(stats_done, 1)

            for j in range(PAIRS):
                for k in range(PAIR * j, PAIR * j + PAIR):
                    dve.wait_ge(x_hi_ready, k + 1)
                    nc.vector.tensor_tensor(x_lo[:, k, :], x_raw[:, k % XRAW, :],
                                            x_hi[:, k, :].bitcast(F32), ALU.subtract).then_inc(x_split, 1)
                split_w(0, j)
            for j in range(AHEAD):
                split_w(1, j)
            dve.wait_ge(bias_loaded, 16)
            take(0)
            for j in range(AHEAD, PAIRS):
                split_w(1, j)
            with dve.Fori(2, NCH) as c:
                for j in range(AHEAD):
                    split_w(c, j)
                take(c - 1)
                for j in range(AHEAD, PAIRS):
                    split_w(c, j)
            take(NCH - 1)

        @block.tensor
        def _(pe):
            def chunk(c):
                first = isinstance(c, int)
                for j in range(PAIRS):
                    if first:
                        pe.wait_ge(x_split, PAIR * (j + 1))
                    pe.wait_ge(w_split, c * PAIRS + j + 1)
                    for kk in range(PAIR):
                        k = PAIR * j + kk
                        cols = slice(kk * CH, (kk + 1) * CH)
                        for t in range(BT):
                            if k == 0 and not first:
                                pe.wait_ge(acc_taken, (c - 1) * BT + t + 1)
                            rows = slice(t * P, (t + 1) * P)
                            last = split_product(
                                nc, acc[t][:, :], (x_hi[:, k, rows], x_lo[:, k, rows]),
                                (w_hi[:, j % SPL, cols], w_lo[:, j % SPL, cols]), k == 0, k == KT - 1)
                            if k == KT - 1:
                                last.then_inc(acc_ready, 1)
                    if j < PAIRS - 1:
                        last.then_inc(w_used, 1)

            chunk(0)
            with pe.Fori(1, NCH) as c:
                chunk(c)

        @block.gpsimd
        def _(pool):
            def store(c):
                for t in range(BT):
                    pool.wait_ge(acc_taken, c * BT + t + 1)
                    pool.dma_start(h_dram[c, t], h_out[:, t, :]).then_inc(h_stored[t], 16)

            with pool.Fori(0, NCH) as c:
                store(c)
            for t in range(BT):
                pool.wait_ge(h_stored[t], 16 * NCH)
            pool.wait_ge(stats_done, NCH * BT)


def second_products(nc, keep, e, h_dram, w2, b2, norm2, stats, ident, s_dram):
    QK = 4
    QS = KT // QK
    HALF = B // 2
    HT = BT // 2
    with ExitStack() as ctx:
        def sb(name, shape, dt=F32):
            return ctx.enter_context(nc.sbuf_tensor(f"{name}_{e}", shape, dt))
        g_hi = sb("g_hi", [P, KT, B], F32R)
        g_lo = sb("g_lo", [P, KT, B], F32R)
        h_raw = sb("h_raw", [P, 2, HT, CH])
        gelu = sb("gelu", [P, 2, HALF])
        w_raw = sb("w2_raw", [P, QS, QK * P])
        w_hi = sb("w2_hi", [P, QS, QK * P], F32R)
        w_lo = sb("w2_lo", [P, QS, QK * P], F32R)
        s_out = sb("s_out", [P, 4, HALF])
        par = sb("norm2", [P, 2, KT])
        bias = sb("b2", [P, KT])
        mv = sb("mv", [P, BT, 2])
        rstd = sb("rstd", [P, 3, BT])
        tr = [ctx.enter_context(nc.psum_tensor(f"turn{e}{i}", [P, HALF], F32)) for i in range(4)]
        acc = [ctx.enter_context(nc.psum_tensor(f"accS{e}{i}", [P, HALF], F32)) for i in range(4)]
        s = Sems(nc, keep, ctx, f"E{e}")
        par_loaded = s.dma("par_loaded")
        h_loaded = s.ring("h_loaded", 2)
        w_loaded = s.ring("w_loaded", QS)
        var_ready, std_ready, mv_ready = s.one("var_ready"), s.one("std_ready"), s.one("mv_ready")
        normed, turned = s.one("normed"), s.one("turned")
        gelu_ready, g_hi_ready, g_split = s.one("gelu_ready"), s.one("g_hi_ready"), s.one("g_split")
        w_hi_ready, w_split, w_used = s.one("w_hi_ready"), s.one("w_split"), s.one("w_used")
        acc_ready, s_ready = s.one("acc_ready"), s.one("s_ready")
        s_stored = s.ring("s_stored", 4)
        block = s.block()

        @block.sync
        def _(sp):
            def load_w(n, u, q):
                if not (isinstance(n, int) and u == 0):
                    sp.wait_ge(w_split, (n * DC + u - 1) * QS + q + 1)
                sp.dma_start(w_raw[:, q, :], w2[e, n, u, q]).then_inc(w_loaded[q], 16)

            for i in range(2 * ECH):
                c, half = i // 2, i % 2
                if i >= 2:
                    sp.wait_ge(turned, (i - 1) * QK)
                sp.dma_start(h_raw[:, half, :, :], h_dram[e * ECH + c, half * HT:(half + 1) * HT]
                             .rearrange("t p f -> p t f")).then_inc(h_loaded[half], 16)
                if i == 0:
                    sp.dma_start(par[:, :, :], norm2[e]).then_inc(par_loaded, 16)
                    sp.dma_start(bias[:, :], b2[e]).then_inc(par_loaded, 16)
                if i == 1:
                    for q in range(QS):
                        load_w(0, 0, q)
            for u in range(1, DC):
                for q in range(QS):
                    load_w(0, u, q)
            with sp.Fori(1, N) as n:
                for u in range(DC):
                    for q in range(QS):
                        load_w(n, u, q)

        @block.scalar
        def _(act):
            def split_w(n, u, q):
                act.wait_ge(w_loaded[q], (n * DC + u + 1) * 16)
                if not (isinstance(n, int) and u == 0):
                    if q < QS - 1:
                        act.wait_ge(w_used, (n * DC + u - 1) * (QS - 1) + q + 1)
                    else:
                        act.wait_ge(acc_ready, (n * DC + u) * 2)
                nc.scalar.activation(w_hi[:, q, :], w_raw[:, q, :], ACT.Copy).then_inc(w_hi_ready, 1)

            act.wait_ge(var_ready, 1)
            nc.scalar.activation(rstd[:, 0, :], rstd[:, 1, :], ACT.Sqrt).then_inc(std_ready, 1)
            act.wait_ge(par_loaded, 32)
            for i in range(2 * ECH):
                c, half = i // 2, i % 2
                for kk in range(QK):
                    k, m = c * QK + kk, i * QK + kk
                    act.wait_ge(turned, m + 1)
                    if m >= 2:
                        act.wait_ge(g_split, m - 1)
                    nc.scalar.activation(gelu[:, m % 2, :], tr[m % 4][:, :], ACT.Gelu,
                                         bias=par[:, 1, k:k + 1], scale=par[:, 0, k:k + 1]).then_inc(gelu_ready, 1)
                if half == 0:
                    split_w(0, 0, c)
            for u in range(1, DC):
                for q in range(QS):
                    split_w(0, u, q)
            with act.Fori(1, N) as n:
                for u in range(DC):
                    for q in range(QS):
                        split_w(n, u, q)

        @block.vector
        def _(dve):
            def split_w(n, u, q):
                dve.wait_ge(w_hi_ready, (n * DC + u) * QS + q + 1)
                nc.vector.tensor_tensor(w_lo[:, q, :], w_raw[:, q, :], w_hi[:, q, :].bitcast(F32),
                                        ALU.subtract).then_inc(w_split, 1)

            def take(n, u):
                for half in range(2):
                    slot = 2 * (u % 2) + half
                    dve.wait_ge(acc_ready, (n * DC + u) * 2 + half + 1)
                    if not (isinstance(n, int) and u < 2):
                        dve.wait_ge(s_stored[slot], (n * 2 + u // 2) * 16)
                    nc.vector.tensor_scalar(s_out[:, slot, :], acc[slot][:, :],
                                            bias[:, bass.ds(n * DC + u, 1)], None, ALU.add).then_inc(s_ready, 1)

            for t in range(BT):
                last = nc.vector.bn_aggr(mv[:, t, :], stats[:, e * ECH:(e + 1) * ECH, t, :])
            last.then_inc(mv_ready, 1)
            dve.wait_ge(mv_ready, 1)
            nc.vector.tensor_scalar(rstd[:, 1, :], mv[:, :, 1], LN_EPS, None, ALU.add).then_inc(var_ready, 1)
            dve.wait_ge(std_ready, 1)
            nc.vector.reciprocal(rstd[:, 2, :], rstd[:, 0, :]).then_inc(mv_ready, 1)
            dve.wait_ge(mv_ready, 2)

            def norm(i):
                half = i % 2
                dve.wait_ge(h_loaded[half], (i // 2 + 1) * 16)
                for t in range(HT):
                    row = half * HT + t
                    nc.vector.tensor_scalar(h_raw[:, half, t, :], h_raw[:, half, t, :], mv[:, row, 0:1],
                                            rstd[:, 2, row:row + 1], ALU.subtract, ALU.mult).then_inc(normed, 1)

            norm(0)
            for i in range(2 * ECH):
                c, half = i // 2, i % 2
                if i + 1 < 2 * ECH:
                    norm(i + 1)
                for kk in range(QK):
                    k, m = c * QK + kk, i * QK + kk
                    rows = slice(half * HALF, (half + 1) * HALF)
                    dve.wait_ge(gelu_ready, m + 1)
                    nc.vector.tensor_copy(g_hi[:, k, rows], gelu[:, m % 2, :]).then_inc(g_hi_ready, 1)
                    dve.wait_ge(g_hi_ready, m + 1)
                    nc.vector.tensor_tensor(g_lo[:, k, rows], gelu[:, m % 2, :], g_hi[:, k, rows].bitcast(F32),
                                            ALU.subtract).then_inc(g_split, 1)
                if half == 0:
                    split_w(0, 0, c)
            dve.wait_ge(par_loaded, 32)
            for u in range(1, DC):
                for q in range(QS):
                    split_w(0, u, q)
                take(0, u - 1)
            with dve.Fori(1, N) as n:
                for u in range(DC):
                    for q in range(QS):
                        split_w(n, u, q)
                    if u == 0:
                        take(n - 1, DC - 1)
                    else:
                        take(n, u - 1)
            take(N - 1, DC - 1)

        @block.tensor
        def _(pe):
            def turn(i):
                half = i % 2
                pe.wait_ge(normed, (i + 1) * HT)
                for kk in range(QK):
                    m = i * QK + kk
                    if m >= 4:
                        pe.wait_ge(gelu_ready, m - 3)
                    for t in range(HT):
                        last = nc.tensor.transpose(tr[m % 4][:, t * P:(t + 1) * P],
                                                   h_raw[:, half, t, kk * P:(kk + 1) * P], ident[:, :])
                    last.then_inc(turned, 1)

            def products(n, u, q):
                pe.wait_ge(w_split, (n * DC + u) * QS + q + 1)
                for kk in range(QK):
                    k = q * QK + kk
                    cols = slice(kk * P, (kk + 1) * P)
                    for half in range(2):
                        if k == 0 and not (isinstance(n, int) and u < 2):
                            pe.wait_ge(s_ready, (n * DC + u - 2) * 2 + half + 1)
                        rows = slice(half * HALF, (half + 1) * HALF)
                        last = split_product(nc, acc[2 * (u % 2) + half][:, :],
                                             (w_hi[:, q, cols], w_lo[:, q, cols]),
                                             (g_hi[:, k, rows], g_lo[:, k, rows]), k == 0, k == KT - 1)
                        if k == KT - 1 and half == 0:
                            last.then_inc(acc_ready, 1)
                if q < QS - 1:
                    last.then_inc(w_used, 1)
                else:
                    last.then_inc(acc_ready, 1)

            for c in range(ECH):
                turn(2 * c)
                turn(2 * c + 1)
                if c >= 1:
                    pe.wait_ge(g_split, c * 2 * QK)
                    products(0, 0, c - 1)
            pe.wait_ge(g_split, ECH * 2 * QK)
            products(0, 0, QS - 1)
            for u in range(1, DC):
                for q in range(QS):
                    products(0, u, q)
            with pe.Fori(1, N) as n:
                for u in range(DC):
                    for q in range(QS):
                        products(n, u, q)

        @block.gpsimd
        def _(pool):
            def store(n):
                for u in range(DC):
                    for half in range(2):
                        slot = 2 * (u % 2) + half
                        pool.wait_ge(s_ready, (n * DC + u) * 2 + half + 1)
                        pool.dma_start(
                            s_dram[half * HT:(half + 1) * HT, n, :, e, u].rearrange("t p b -> p t b"),
                            s_out[:, slot, :].rearrange("p (t b) -> p t b", b=P)).then_inc(s_stored[slot], 16)
            with pool.Fori(0, N) as n:
                store(n)
            for slot in range(4):
                pool.wait_ge(s_stored[slot], 16 * 2 * N)


def scores(nc, keep, s_dram, wqk, bqk, power):
    MATS = 4
    W = N * N * HEADS
    SLOTS = 3
    with ExitStack() as ctx:
        def sb(name, shape, dt=F32):
            return ctx.enter_context(nc.sbuf_tensor(name, shape, dt))
        w_hi = sb("wqk_hi", [P, MATS, DC, D], F32R)
        w_lo = sb("wqk_lo", [P, MATS, DC, D], F32R)
        bias = sb("bqk_parts", [P, MATS, D], F32R)
        picks = sb("picks", [P, P], F32R)
        s_raw = sb("sB_raw", [P, 2, 2, DC * P])
        s_hi = sb("sB_hi", [P, 2, 2, DC * P], F32R)
        s_lo = sb("sB_lo", [P, 2, 2, DC * P], F32R)
        q = sb("q_parts", [P, N, 3, D])
        k = sb("k_parts", [P, 2, N, 3, D])
        prod = sb("prod", [P, SLOTS, N, D])
        part = sb("part", [P, 2, 3, W])
        both = sb("both", [P, 2, 2, W])
        picks_raw = sb("picks_raw", [P, P])
        w_raw = k[:, 1].rearrange("p n i d -> p (n i d)")[:, 0:2 * DC * D].rearrange("p (s x) -> p s x", s=2)
        b_raw = q[:, :, 0, :]
        acc = [[ctx.enter_context(nc.psum_tensor(f"accB{i}{m}", [P, D], F32)) for m in range(MATS)] for i in range(2)]
        s = Sems(nc, keep, ctx, "B")
        w_loaded, bias_loaded = s.ring("w_loaded", 2), s.dma("bias_loaded")
        w_hi_ready, w_split = s.one("w_hi_ready"), s.one("w_split")
        zeroed, bias_ready = s.one("zeroed"), s.one("bias_ready")
        s_loaded = s.ring("s_loaded", 2)
        s_hi_ready, s_split = s.one("s_hi_ready"), s.one("s_split")
        acc_ready, copied, k_ready, q_ready = s.one("acc_ready"), s.one("copied"), s.one("k_ready"), s.one("q_ready")
        multiplied, summed = s.one("multiplied"), s.one("summed")
        small = s.one("small")
        PRODS = 3 * N
        SMALL = 5
        block = s.block()

        def first(t, n=0, m=0):
            return isinstance(t, int) and t * N + n < m

        @block.sync
        def _(sp):
            def load_s(t, n):
                if not first(t, n, 2):
                    sp.wait_ge(s_split, t * N + n - 1)
                sp.dma_start(s_raw[:, n % 2, :, :].rearrange("p e x -> p (e x)"), s_dram[t, n]).then_inc(s_loaded[n % 2], 16)

            sp.wait_ge(zeroed, 2)
            for r in (0, 32):
                sp.dma_start(b_raw[r:r + 1, :, :], bqk).then_inc(bias_loaded, 16)
            for m in range(2):
                sp.dma_start(w_raw[:, m, :], wqk[m]).then_inc(w_loaded[m], 16)
            load_s(0, 0)
            for m in range(2, MATS):
                sp.wait_ge(w_split, m - 1)
                sp.dma_start(w_raw[:, m % 2, :], wqk[m]).then_inc(w_loaded[m % 2], 16)
            for n in range(1, N):
                load_s(0, n)
            for n in range(N):
                load_s(1, n)
            with sp.Fori(2, BT) as t:
                for n in range(N):
                    load_s(t, n)

        @block.scalar
        def _(act):
            def split_s(t, n):
                act.wait_ge(s_loaded[n % 2], (t * 2 + n // 2 + 1) * 16)
                if not first(t, n, 2):
                    act.wait_ge(acc_ready, (t * N + n - 1) * MATS)
                nc.scalar.activation(s_hi[:, n % 2, :, :], s_raw[:, n % 2, :, :], ACT.Copy).then_inc(s_hi_ready, 1)

            def copy(t, u, n):
                if not first(t, 0, 1):
                    act.wait_ge(multiplied, (t - 1) * PRODS + 3 * (n + 1))
                for m, to in enumerate((q[:, n, 0, :], q[:, n, 1, :], k[:, u, n, 0, :])):
                    act.wait_ge(acc_ready, (t * N + n) * MATS + m + 1)
                    nc.scalar.activation(to, acc[n % 2][m][:, :], ACT.Copy).then_inc(copied, 1)

            for m in range(MATS):
                act.wait_ge(w_loaded[m % 2], 16 * (m // 2 + 1))
                nc.scalar.activation(w_hi[:, m, :, :], w_raw[:, m % 2, :], ACT.Copy).then_inc(w_hi_ready, 1)
                if m == 0:
                    split_s(0, 0)
            act.wait_ge(bias_ready, 3)

            def tile(t, u):
                for n in range(N):
                    if n < N - 1:
                        split_s(t, n + 1)
                    elif not (isinstance(t, int) and t == BT - 1):
                        split_s(t + 1, 0)
                    copy(t, u, n)

            tile(0, 0)
            tile(1, 1)
            with act.Fori(1, BT // 2 - 1) as i:
                tile(i * 2, 0)
                tile(i * 2 + 1, 1)
            tile(BT - 2, 0)
            tile(BT - 1, 1)

        @block.gpsimd
        def _(pool):
            nc.gpsimd.memset(b_raw, 0.0).then_inc(zeroed, 1)
            nc.gpsimd.memset(picks_raw[:, :], 0.0).then_inc(zeroed, 1)
            pool.wait_ge(zeroed, 2)
            for r in (0, 32):
                nc.gpsimd.memset(picks_raw[r:r + 1, :], 1.0).then_inc(zeroed, 1)
            pool.wait_ge(zeroed, 4)

            def split_s(t, n):
                pool.wait_ge(s_hi_ready, t * N + n + 1)
                nc.gpsimd.tensor_tensor(s_lo[:, n % 2, :, :], s_raw[:, n % 2, :, :],
                                        s_hi[:, n % 2, :, :].bitcast(F32), ALU.subtract).then_inc(s_split, 1)

            def add_q(t, n):
                pool.wait_ge(copied, (t * N + n) * 3 + 2)
                nc.gpsimd.tensor_tensor(q[:, n, 2, :], q[:, n, 0, :], q[:, n, 1, :], ALU.add).then_inc(q_ready, 1)

            def combine(t, u):
                pool.wait_ge(summed, (t + 1) * PRODS)
                m1, m2, m3 = (part[:, u, i, :] for i in range(3))
                re, im = both[:, u, 0, :], both[:, u, 1, :]
                nc.gpsimd.tensor_tensor(re, m1, m3, ALU.add).then_inc(small, 1)
                nc.gpsimd.tensor_tensor(im, m1, m2, ALU.subtract).then_inc(small, 1)
                pool.wait_ge(small, t * SMALL + 2)
                nc.gpsimd.tensor_tensor(re, re, re, ALU.mult).then_inc(small, 1)
                nc.gpsimd.tensor_tensor(im, im, im, ALU.mult).then_inc(small, 1)
                pool.wait_ge(small, t * SMALL + 4)
                nc.gpsimd.tensor_tensor(power[:, t, :], re, im, ALU.add).then_inc(small, 1)

            split_s(0, 0)

            def tile(t, u):
                for n in range(N):
                    if n < N - 1:
                        split_s(t, n + 1)
                    elif not (isinstance(t, int) and t == BT - 1):
                        split_s(t + 1, 0)
                    add_q(t, n)
                    if n == N - 1 and not first(t, 0, 1):
                        combine(t - 1, 1 - u)

            tile(0, 0)
            tile(1, 1)
            with pool.Fori(1, BT // 2 - 1) as i:
                tile(i * 2, 0)
                tile(i * 2 + 1, 1)
            tile(BT - 2, 0)
            tile(BT - 1, 1)
            combine(BT - 1, 1)
            pool.wait_ge(small, BT * SMALL)

        @block.vector
        def _(dve):
            dve.wait_ge(zeroed, 4)
            nc.vector.tensor_copy(picks[:, :], picks_raw[:, :]).then_inc(bias_ready, 1)
            dve.wait_ge(bias_loaded, 32)
            nc.vector.tensor_copy(bias[:, :, :], b_raw).then_inc(bias_ready, 1)
            dve.wait_ge(bias_ready, 2)
            nc.vector.tensor_tensor(bias[32:33, :, :], b_raw[32:33], bias[32:33, :, :].bitcast(F32),
                                    ALU.subtract).then_inc(bias_ready, 1)
            for m in range(MATS):
                dve.wait_ge(w_hi_ready, m + 1)
                nc.vector.tensor_tensor(w_lo[:, m, :, :].rearrange("p c d -> p (c d)"), w_raw[:, m % 2, :],
                                        w_hi[:, m, :, :].rearrange("p c d -> p (c d)").bitcast(F32),
                                        ALU.subtract).then_inc(w_split, 1)

            def finish_k(t, u, n):
                dve.wait_ge(copied, (t * N + n + 1) * 3)
                dve.wait_ge(acc_ready, (t * N + n + 1) * MATS)
                ki = acc[n % 2][3][:, :]
                nc.vector.tensor_tensor(k[:, u, n, 1, :], ki, k[:, u, n, 0, :], ALU.add)
                nc.vector.tensor_tensor(k[:, u, n, 2, :], ki, k[:, u, n, 0, :], ALU.subtract).then_inc(k_ready, 1)

            def tile(t, u, more):
                dve.wait_ge(k_ready, (t + 1) * N)
                pairs = ((2, 0), (0, 1), (1, 2))

                def add_up(r):
                    n, i = r // 3, r % 3
                    dve.wait_ge(multiplied, t * PRODS + r + 1)
                    nc.vector.tensor_reduce(part[:, u, i, n * N * HEADS:(n + 1) * N * HEADS],
                                            prod[:, r % SLOTS, :, :].rearrange("p m (h d) -> p (m h) d", d=HD),
                                            AX.X, ALU.add).then_inc(summed, 1)

                for n in range(N):
                    dve.wait_ge(q_ready, t * N + n + 1)
                    for i, (a, b) in enumerate(pairs):
                        r = 3 * n + i
                        if not first(t, 0, 1) or r >= SLOTS:
                            dve.wait_ge(summed, t * PRODS + r - SLOTS + 1)
                        nc.vector.tensor_tensor(prod[:, r % SLOTS, :, :], k[:, u, :, b, :],
                                                q[:, n, a, :].unsqueeze(1).to_broadcast([P, N, D]),
                                                ALU.mult).then_inc(multiplied, 1)
                        if r:
                            add_up(r - 1)
                    if n == N - 1:
                        add_up(PRODS - 1)
                    if more:
                        finish_k(t + 1, 1 - u, n)

            for n in range(N):
                finish_k(0, 0, n)
            tile(0, 0, True)
            tile(1, 1, True)
            with dve.Fori(1, BT // 2 - 1) as i:
                tile(i * 2, 0, True)
                tile(i * 2 + 1, 1, True)
            tile(BT - 2, 0, True)
            tile(BT - 1, 1, False)

        @block.tensor
        def _(pe):
            pe.wait_ge(bias_ready, 3)

            def tile(t):
                for n in range(N):
                    pe.wait_ge(s_split, t * N + n + 1)
                    if not first(t, n, 2):
                        pe.wait_ge(copied, (t * N + n - 1) * 3)
                        pe.wait_ge(k_ready, t * N + n - 1)
                    for m in range(MATS):
                        e = m % 2
                        if first(t, n, 1):
                            pe.wait_ge(w_split, m + 1)
                        out = acc[n % 2][m][:, :]
                        nc.tensor.matmul(out, picks[:, :], bias[:, m, :], start=True, stop=False)
                        for c in range(DC):
                            x = slice(c * P, (c + 1) * P)
                            last = split_product(nc, out, (s_hi[:, n % 2, e, x], s_lo[:, n % 2, e, x]),
                                                 (w_hi[:, m, c, :], w_lo[:, m, c, :]), False, c == DC - 1)
                        last.then_inc(acc_ready, 1)

            tile(0)
            with pe.Fori(1, BT) as t:
                tile(t)


def mix_values(nc, keep, power, s_dram, wvo, bv, bo, ident, a_dram):
    MATS = 4
    W = N * N * HEADS
    with ExitStack() as ctx:
        def sb(name, shape, dt=F32):
            return ctx.enter_context(nc.sbuf_tensor(name, shape, dt))
        w_hi = sb("wvo_hi", [P, MATS, DC, D], F32R)
        w_lo = sb("wvo_lo", [P, MATS, DC, D], F32R)
        s_raw = sb("sV_raw", [P, 2, 2, DC * P])
        s_hi = sb("sV_hi", [P, 2, 2, DC * P], F32R)
        s_lo = sb("sV_lo", [P, 2, 2, DC * P], F32R)
        bias_v = sb("bv_all", [P, 2, D])
        bias_o = sb("bo_cols", [P, 2, DC])
        v = sb("v_rows", [P, 2, 2, N, D])
        prod = sb("prodV", [P, 2, N, D])
        o = sb("mixed", [P, 2, N, D])
        ot_hi = sb("ot_hi", [P, DC, N * P], F32R)
        ot_lo = sb("ot_lo", [P, DC, N * P], F32R)
        a_out = sb("a_out", [P, 2, N, DC, P])
        top = sb("softmax_top", [P, BT, N, HEADS])
        w_raw = v[:, 1].rearrange("p e n d -> p (e n d)").rearrange("p (s x) -> p s x", s=2)
        vb = [[ctx.enter_context(nc.psum_tensor(f"accV{i}{e}", [P, D], F32)) for e in range(2)] for i in range(2)]
        tr = [ctx.enter_context(nc.psum_tensor(f"turnV{i}", [P, N * P], F32)) for i in range(2)]
        ob = [ctx.enter_context(nc.psum_tensor(f"accO{i}", [P, N * P], F32)) for i in range(2)]
        s = Sems(nc, keep, ctx, "V")
        w_loaded, bias_loaded = s.ring("w_loaded", 2), s.dma("bias_loaded")
        w_hi_ready, w_split = s.one("w_hi_ready"), s.one("w_split")
        s_loaded = s.ring("s_loaded", 2)
        s_hi_ready, s_split = s.one("s_hi_ready"), s.one("s_split")
        soft, root, exped, prob_ready = s.one("soft"), s.one("root"), s.one("exped"), s.one("prob_ready")
        v_ready, v_taken = s.one("v_ready"), s.one("v_taken")
        multiplied, halved, o_ready = s.one("multiplied"), s.one("halved"), s.one("o_ready")
        turned, ot_hi_ready, ot_split = s.one("turned"), s.one("ot_hi_ready"), s.one("ot_split")
        out_ready, out_taken = s.one("out_ready"), s.one("out_taken")
        stored = s.ring("stored", 2)
        block = s.block()

        def first(t, n=0, m=0):
            return isinstance(t, int) and t * N + n < m

        @block.sync
        def _(sp):
            def load_s(t, n):
                if not first(t, n, 2):
                    sp.wait_ge(s_split, t * N + n - 1)
                sp.dma_start(s_raw[:, n % 2, :, :].rearrange("p e x -> p (e x)"), s_dram[t, n]).then_inc(s_loaded[n % 2], 16)

            for m in range(2):
                sp.dma_start(w_raw[:, m, :], wvo[m]).then_inc(w_loaded[m], 16)
            load_s(0, 0)
            sp.dma_start(bias_v[:, :, :], bv.to_broadcast([P, 2, D])).then_inc(bias_loaded, 16)
            sp.dma_start(bias_o[:, :, :], bo).then_inc(bias_loaded, 16)
            for m in range(2, MATS):
                sp.wait_ge(w_split, m - 1)
                sp.dma_start(w_raw[:, m % 2, :], wvo[m]).then_inc(w_loaded[m % 2], 16)
            for n in range(1, N):
                load_s(0, n)
            with sp.Fori(1, BT) as t:
                for n in range(N):
                    load_s(t, n)

        @block.scalar
        def _(act):
            def split_s(t, n):
                act.wait_ge(s_loaded[n % 2], (t * 2 + n // 2 + 1) * 16)
                if not first(t, n, 2):
                    act.wait_ge(v_ready, (t * N + n - 1) * 2)
                nc.scalar.activation(s_hi[:, n % 2, :, :], s_raw[:, n % 2, :, :], ACT.Copy).then_inc(s_hi_ready, 1)

            def split_w(m):
                act.wait_ge(w_loaded[m % 2], 16 * (m // 2 + 1))
                nc.scalar.activation(w_hi[:, m, :, :], w_raw[:, m % 2, :], ACT.Copy).then_inc(w_hi_ready, 1)

            def split_o(t, e):
                for c in range(DC):
                    r = (t * 2 + e) * DC + c
                    act.wait_ge(turned, r + 1)
                    if not (isinstance(t, int) and t == 0 and e == 0):
                        act.wait_ge(out_ready, (t * 2 + e) * DC)
                    nc.scalar.activation(ot_hi[:, c, :], tr[c % 2][:, :], ACT.Copy).then_inc(ot_hi_ready, 1)

            def take_out(t, e):
                if not (isinstance(t, int) and t == 0):
                    act.wait_ge(stored[e], t * 16)
                for c in range(DC):
                    act.wait_ge(out_ready, (t * 2 + e) * DC + c + 1)
                    nc.scalar.activation(a_out[:, e, :, c, :], ob[c % 2][:, :].rearrange("p (n b) -> p n b", b=P),
                                         ACT.Identity, bias=bias_o[:, e, c:c + 1]).then_inc(out_taken, 1)

            split_w(0)
            split_s(0, 0)
            split_w(1)
            act.wait_ge(soft, 1)
            nc.scalar.activation(power[:, :, :], power[:, :, :], ACT.Sqrt).then_inc(root, 1)
            split_w(2)
            act.wait_ge(soft, 3)
            nc.scalar.activation(power[:, :, :], power[:, :, :], ACT.Exp, scale=HD ** -0.5).then_inc(exped, 1)
            split_w(3)
            for n in range(1, N):
                split_s(0, n)
            act.wait_ge(bias_loaded, 32)

            def step(t, splits):
                for e in range(2):
                    for half in range(2):
                        if 2 * e + half < splits:
                            split_s(t + 1 + e, 2 * (1 - e) + half)
                        if half == 0:
                            split_o(t, e)
                        else:
                            take_out(t, e)

            split_s(1, 0)
            split_s(1, 1)
            step(0, 4)
            with act.Fori(1, BT - 2) as t:
                step(t, 4)
            step(BT - 2, 2)
            step(BT - 1, 0)

        @block.gpsimd
        def _(pool):
            def split_s(t, n):
                pool.wait_ge(s_hi_ready, t * N + n + 1)
                nc.gpsimd.tensor_tensor(s_lo[:, n % 2, :, :], s_raw[:, n % 2, :, :],
                                        s_hi[:, n % 2, :, :].bitcast(F32), ALU.subtract).then_inc(s_split, 1)

            def store(t, e):
                pool.wait_ge(out_taken, (t * 2 + e + 1) * DC)
                pool.dma_start(a_dram[t, :, :, e].rearrange("n p c b -> p n (c b)"),
                               a_out[:, e].rearrange("p n c b -> p n (c b)")).then_inc(stored[e], 16)

            for n in range(N):
                split_s(0, n)
            split_s(1, 0)
            split_s(1, 1)

            def step(t, splits):
                for e in range(2):
                    for half in range(2):
                        if 2 * e + half < splits:
                            split_s(t + 1 + e, 2 * (1 - e) + half)
                    store(t, e)

            step(0, 4)
            with pool.Fori(1, BT - 2) as t:
                step(t, 4)
            step(BT - 2, 2)
            step(BT - 1, 0)
            for e in range(2):
                pool.wait_ge(stored[e], 16 * BT)

        @block.vector
        def _(dve):
            def split_w(m):
                dve.wait_ge(w_hi_ready, m + 1)
                nc.vector.tensor_tensor(w_lo[:, m, :, :].rearrange("p c d -> p (c d)"), w_raw[:, m % 2, :],
                                        w_hi[:, m, :, :].rearrange("p c d -> p (c d)").bitcast(F32),
                                        ALU.subtract).then_inc(w_split, 1)

            def take_v(t, u, n):
                for e in range(2):
                    dve.wait_ge(v_ready, (t * N + n) * 2 + e + 1)
                    nc.vector.tensor_tensor(v[:, u, e, n, :], vb[n % 2][e][:, :], bias_v[:, e, :],
                                            ALU.add).then_inc(v_taken, 1)

            def mix(t, u, e, n):
                r = (t * 2 + e) * N + n
                slot = n % 2
                if not (isinstance(t, int) and t == 0 and e == 0 and n < 2):
                    dve.wait_ge(o_ready, r - 1)
                if not (isinstance(t, int) and t == 0):
                    dve.wait_ge(turned, (t * 2 + e - 1) * DC)
                prob = power[:, bass.ds(t, 1), n * N * HEADS:(n + 1) * N * HEADS]
                nc.vector.tensor_tensor(
                    prod[:, slot, :, :].rearrange("p m (h d) -> p (m h) d", d=HD),
                    v[:, u, e, :, :].rearrange("p m (h d) -> p (m h) d", d=HD),
                    prob.rearrange("p t x -> p (t x)").unsqueeze(2).to_broadcast([P, N * HEADS, HD]),
                    ALU.mult).then_inc(multiplied, 1)
                dve.wait_ge(multiplied, r + 1)
                nc.vector.tensor_tensor(prod[:, slot, 0:2, :], prod[:, slot, 0:2, :], prod[:, slot, 2:4, :],
                                        ALU.add).then_inc(halved, 1)
                dve.wait_ge(halved, r + 1)
                nc.vector.tensor_tensor(o[:, e, n, :], prod[:, slot, 0, :], prod[:, slot, 1, :],
                                        ALU.add).then_inc(o_ready, 1)

            def split_o(t, e):
                for c in range(DC):
                    dve.wait_ge(ot_hi_ready, (t * 2 + e) * DC + c + 1)
                    nc.vector.tensor_tensor(ot_lo[:, c, :], tr[c % 2][:, :], ot_hi[:, c, :].bitcast(F32),
                                            ALU.subtract).then_inc(ot_split, 1)

            def step(t, u, more):
                dve.wait_ge(v_taken, (t + 1) * N * 2)
                for e in range(2):
                    for n in range(N):
                        mix(t, u, e, n)
                    for n in range(2 * e, 2 * e + 2):
                        if more:
                            take_v(t + 1, 1 - u, n)
                    split_o(t, e)

            split_w(0)
            nc.vector.tensor_scalar(power[:, :, :], power[:, :, :], 1e-8, None, ALU.add).then_inc(soft, 1)
            split_w(1)
            dve.wait_ge(root, 1)
            by_m = power[:, :, :].rearrange("p t (n m h) -> p (t n) h m", n=N, m=N)
            plain = power[:, :, :].rearrange("p t (n m h) -> p (t n) m h", n=N, m=N)
            heads = top[:, :, :, :].rearrange("p t n h -> p (t n) h")
            over_m = heads.unsqueeze(2).to_broadcast([P, BT * N, N, HEADS])
            nc.vector.tensor_reduce(heads, by_m, AX.X, ALU.max).then_inc(soft, 1)
            dve.wait_ge(soft, 2)
            nc.vector.tensor_tensor(plain, plain, over_m, ALU.subtract).then_inc(soft, 1)
            split_w(2)
            dve.wait_ge(exped, 1)
            nc.vector.tensor_reduce(heads, by_m, AX.X, ALU.add).then_inc(soft, 1)
            dve.wait_ge(soft, 4)
            nc.vector.reciprocal(heads, heads).then_inc(soft, 1)
            dve.wait_ge(soft, 5)
            nc.vector.tensor_tensor(plain, plain, over_m, ALU.mult).then_inc(prob_ready, 1)
            split_w(3)
            dve.wait_ge(bias_loaded, 32)
            for n in range(N):
                take_v(0, 0, n)
            dve.wait_ge(prob_ready, 1)
            step(0, 0, True)
            step(1, 1, True)
            with dve.Fori(1, BT // 2 - 1) as i:
                step(i * 2, 0, True)
                step(i * 2 + 1, 1, True)
            step(BT - 2, 0, True)
            step(BT - 1, 1, False)

        @block.tensor
        def _(pe):
            def values(t, n):
                pe.wait_ge(s_split, t * N + n + 1)
                for e in range(2):
                    if first(t, n, 1):
                        pe.wait_ge(w_split, e + 1)
                    if not first(t, n, 2):
                        pe.wait_ge(v_taken, (t * N + n - 2) * 2 + e + 1)
                    for c in range(DC):
                        x = slice(c * P, (c + 1) * P)
                        last = split_product(nc, vb[n % 2][e][:, :], (s_hi[:, n % 2, e, x], s_lo[:, n % 2, e, x]),
                                             (w_hi[:, e, c, :], w_lo[:, e, c, :]), c == 0, c == DC - 1)
                    last.then_inc(v_ready, 1)

            def project(t, e):
                pe.wait_ge(o_ready, (t * 2 + e + 1) * N)
                for c in range(DC):
                    if not (isinstance(t, int) and t == 0 and e == 0 and c < 2):
                        pe.wait_ge(ot_split, (t * 2 + e) * DC + c - 1)
                    for n in range(N):
                        last = nc.tensor.transpose(tr[c % 2][:, n * P:(n + 1) * P],
                                                   o[:, e, n, c * P:(c + 1) * P], ident[:, :])
                    last.then_inc(turned, 1)
                for to in range(DC):
                    if not (isinstance(t, int) and t == 0 and e == 0 and to < 2):
                        pe.wait_ge(out_taken, (t * 2 + e) * DC + to - 1)
                    for c in range(DC):
                        if to == 0:
                            pe.wait_ge(ot_split, (t * 2 + e) * DC + c + 1)
                        cols = slice(to * P, (to + 1) * P)
                        last = split_product(nc, ob[to % 2][:, :], (w_hi[:, 2 + e, c, cols], w_lo[:, 2 + e, c, cols]),
                                             (ot_hi[:, c, :], ot_lo[:, c, :]), c == 0, c == DC - 1)
                    last.then_inc(out_ready, 1)

            def step(t):
                for e in range(2):
                    values(t + 1, 2 * e)
                    values(t + 1, 2 * e + 1)
                    project(t, e)

            for n in range(N):
                values(0, n)
            pe.wait_ge(w_split, MATS)
            step(0)
            with pe.Fori(1, BT - 1) as t:
                step(t)
            for e in range(2):
                project(BT - 1, e)



def mix_states(nc, keep, a_dram, wint, ri_dram):
    SETS = 3
    RING = 4
    PAIR = 2
    with ExitStack() as ctx:
        def sb(name, shape, dt=F32):
            return ctx.enter_context(nc.sbuf_tensor(name, shape, dt))
        w_raw = sb("wint_raw", [P, 2, DC * D])
        w_hi = sb("wint_hi", [P, PAIR, SETS, DC * D], F32R)
        w_lo = sb("wint_lo", [P, PAIR, SETS, DC * D], F32R)
        a_raw = sb("a_raw", [P, RING, 2 * DC * P])
        a_hi = sb("a_hi", [P, RING, 2 * DC * P], F32R)
        a_lo = sb("a_lo", [P, RING, 2 * DC * P], F32R)
        out = sb("ri_out", [P, RING, 2, D])
        acc = [[ctx.enter_context(nc.psum_tensor(f"accR{i}{j}", [P, D], F32)) for j in range(2)] for i in range(RING)]
        s = Sems(nc, keep, ctx, "M")
        w_loaded, a_loaded = s.ring("w_loaded", 2), s.ring("a_loaded", RING)
        w_hi_ready, w_split, w_ready = s.one("w_hi_ready"), s.one("w_split"), s.one("w_ready")
        a_hi_ready, a_split = s.one("a_hi_ready"), s.one("a_split")
        r_ready, i_ready = s.one("r_ready"), s.one("i_ready")
        r_taken, i_taken = s.one("r_taken"), s.one("i_taken")
        stored = s.ring("stored", RING)
        RAW_FREE, A_FREE, SET_FREE = 2, RING, PAIR * BT
        STORED = 16
        block = s.block()

        def state(i, u):
            return i * PAIR + u

        @block.sync
        def _(sp):
            sp.sem_inc(w_split, RAW_FREE)
            sp.sem_inc(a_split, A_FREE)
            with sp.Fori(0, N // PAIR) as i:
                for u in range(PAIR):
                    n = state(i, u)
                    for j in range(2):
                        sp.wait_ge(w_split, n * 2 + j + 1)
                        sp.dma_start(w_raw[:, j, :], wint[n, j]).then_inc(w_loaded[j], 16)
                    for t in range(BT):
                        sp.wait_ge(a_split, n * BT + t + 1)
                        sp.dma_start(a_raw[:, t % RING, :], a_dram[t, n]).then_inc(a_loaded[t % RING], 16)

        @block.scalar
        def _(act):
            def split_w(n, u):
                act.wait_ge(i_ready, SET_FREE + (n - PAIR + 1) * BT)
                for j in range(2):
                    act.wait_ge(w_loaded[j], (n + 1) * 16)
                    nc.scalar.activation(w_hi[:, u, j, :], w_raw[:, j, :], ACT.Copy).then_inc(w_hi_ready, 1)
                act.wait_ge(w_hi_ready, n * 2 + 2)
                nc.scalar.activation(w_hi[:, u, 2, :], w_hi[:, u, 1, :].bitcast(F32), ACT.Copy, scale=-1.0).then_inc(w_ready, 1)
                act.wait_ge(w_split, RAW_FREE + n * 2 + 2)
                nc.scalar.activation(w_lo[:, u, 2, :], w_lo[:, u, 1, :].bitcast(F32), ACT.Copy, scale=-1.0).then_inc(w_ready, 1)

            def split_a(n, t):
                act.wait_ge(a_loaded[t % RING], (n * (BT // RING) + t // RING + 1) * 16)
                act.wait_ge(i_ready, SET_FREE + n * BT + t - RING + 1)
                nc.scalar.activation(a_hi[:, t % RING, :], a_raw[:, t % RING, :], ACT.Copy).then_inc(a_hi_ready, 1)

            def take(n, t):
                act.wait_ge(stored[t % RING], (n * (BT // RING) + t // RING) * 16 + 16)
                act.wait_ge(r_ready, n * BT + t + 1)
                nc.scalar.activation(out[:, t % RING, 0, :], acc[t % RING][0][:, :], ACT.Copy).then_inc(r_taken, 1)

            def store(n, t):
                act.wait_ge(r_taken, RING + n * BT + t + 1)
                act.wait_ge(i_taken, RING + n * BT + t + 1)
                act.dma_start(ri_dram[t, :, n], out[:, t % RING, :, :].rearrange("p j d -> p (j d)")
                              ).then_inc(stored[t % RING], 16)

            act.sem_inc(i_ready, SET_FREE)
            for slot in range(RING):
                act.sem_inc(stored[slot], STORED)
            with act.Fori(0, N // PAIR) as i:
                for u in range(PAIR):
                    n = state(i, u)
                    split_w(n, u)
                    for t in range(2):
                        split_a(n, t)
                    for t in range(BT):
                        if t + 2 < BT:
                            split_a(n, t + 2)
                        take(n, t)
                        if t:
                            store(n, t - 1)
                    store(n, BT - 1)
            for slot in range(RING):
                act.wait_ge(stored[slot], STORED + 16 * N * BT // RING)

        @block.vector
        def _(dve):
            with dve.Fori(0, N // PAIR) as i:
                for u in range(PAIR):
                    n = state(i, u)
                    for j in range(2):
                        dve.wait_ge(w_hi_ready, n * 2 + j + 1)
                        nc.vector.tensor_tensor(w_lo[:, u, j, :], w_raw[:, j, :], w_hi[:, u, j, :].bitcast(F32),
                                                ALU.subtract).then_inc(w_split, 1)

                    def split_a(t):
                        dve.wait_ge(a_hi_ready, n * BT + t + 1)
                        nc.vector.tensor_tensor(a_lo[:, t % RING, :], a_raw[:, t % RING, :],
                                                a_hi[:, t % RING, :].bitcast(F32), ALU.subtract).then_inc(a_split, 1)

                    split_a(0)
                    split_a(1)
                    for t in range(BT):
                        if t + 2 < BT:
                            split_a(t + 2)
                        dve.wait_ge(stored[t % RING], (n * (BT // RING) + t // RING) * 16 + 16)
                        dve.wait_ge(i_ready, SET_FREE + n * BT + t + 1)
                        nc.vector.tensor_copy(out[:, t % RING, 1, :], acc[t % RING][1][:, :]).then_inc(i_taken, 1)

        @block.tensor
        def _(pe):
            pe.sem_inc(r_taken, RING)
            pe.sem_inc(i_taken, RING)
            with pe.Fori(0, N // PAIR) as i:
                for u in range(PAIR):
                    n = state(i, u)
                    pe.wait_ge(w_ready, (n + 1) * 2)
                    for t in range(BT):
                        pe.wait_ge(a_split, A_FREE + n * BT + t + 1)
                        for j, taken, ready in ((0, r_taken, r_ready), (1, i_taken, i_ready)):
                            pe.wait_ge(taken, n * BT + t + 1)
                            for e in range(2):
                                which = ((0, 2), (1, 0))[j][e]
                                for c in range(DC):
                                    x = slice((e * DC + c) * P, (e * DC + c + 1) * P)
                                    y = slice(c * D, (c + 1) * D)
                                    last = split_product(
                                        nc, acc[t % RING][j][:, :], (a_hi[:, t % RING, x], a_lo[:, t % RING, x]),
                                        (w_hi[:, u, which, y], w_lo[:, u, which, y]),
                                        e == 0 and c == 0, e == 1 and c == DC - 1)
                            last.then_inc(ready, 1)


def superpose(nc, keep, ids, tables, ri_dram, ident, sup_t):
    PAIRS = [(n, n + gap) for gap in range(1, N) for n in range(N - gap)]
    with ExitStack() as ctx:
        def sb(name, shape, dt=F32):
            return ctx.enter_context(nc.sbuf_tensor(name, shape, dt))
        idx = sb("idx", [P, BT, N], I32)
        strength = sb("strength", [P, BT, N, N])
        ri = sb("ri_rows", [P, 2, N, 2, D])
        uv = sb("uv", [P, N, 2, D])
        size = sb("size", [P, N, D])
        zero = sb("zero", [P, N, D])
        cos = sb("cos", [P, len(PAIRS), D])
        gain = sb("gain", [P, N, D])
        prod = sb("prodD", [P, N, 2, D])
        sup = sb("sup", [P, 2, 2, D])
        norm = sb("norm", [P, BT, 4])
        tr = [ctx.enter_context(nc.psum_tensor(f"turnD{i}", [P, DC * P], F32)) for i in range(2)]
        s = Sems(nc, keep, ctx, "D")
        ids_loaded, gathered = s.dma("ids_loaded"), s.dma("gathered")
        loaded = s.ring("loaded", 2)
        squared, rooted, normed, lengths = s.one("squared"), s.one("rooted"), s.one("normed"), s.one("lengths")
        step = s.one("step")
        turned, copied = s.one("turned"), s.one("copied")
        STEPS = 32
        block = s.block()

        @block.sync
        def _(sp):
            sp.dma_start(idx[:, :, :], ids).then_inc(ids_loaded, 16)
            for t in range(BT):
                if t >= 2:
                    sp.wait_ge(step, (t - 1) * STEPS)
                sp.dma_start(ri[:, t % 2].rearrange("p n j d -> p (n j d)"),
                             ri_dram[t].rearrange("p n x -> p (n x)")).then_inc(loaded[t % 2], 16)

        @block.gpsimd
        def _(pool):
            pool.wait_ge(ids_loaded, 16)
            for t in range(BT):
                for i in range(N):
                    pool.indirect_dma_start(
                        out=strength[:, t, i, :], out_offset=None, in_=tables[i],
                        in_offset=bass.IndirectOffsetOnAxis(ap=idx[:, t, i:i + 1], axis=0)).then_inc(gathered, 16)

        @block.scalar
        def _(act):
            for t in range(BT):
                act.wait_ge(loaded[t % 2], (t // 2 + 1) * 16)
                if t:
                    act.wait_ge(step, t * STEPS)
                nc.scalar.activation(uv[:, :, :, :], ri[:, t % 2], ACT.Square).then_inc(squared, 1)
                act.wait_ge(step, t * STEPS + 2)
                nc.scalar.activation(size[:, :, :], size[:, :, :], ACT.Sqrt).then_inc(rooted, 1)
                act.wait_ge(step, (t + 1) * STEPS)
                junk = prod[:, 0, :, :]
                nc.scalar.activation(junk, sup[:, t % 2], ACT.Square, accum_out=norm[:, t, 0:1]).then_inc(lengths, 1)
                act.wait_ge(normed, t * 3 + 1)
                nc.scalar.activation(norm[:, t, 2:3], norm[:, t, 1:2], ACT.Sqrt).then_inc(lengths, 1)
                act.wait_ge(normed, t * 3 + 3)
                for j in range(2):
                    act.wait_ge(turned, t * 2 + j + 1)
                    nc.scalar.activation(sup_t[:, j, :, t * P:(t + 1) * P],
                                         tr[j][:, :].rearrange("p (c b) -> p c b", b=P), ACT.Copy).then_inc(copied, 1)

        @block.tensor
        def _(pe):
            for t in range(BT):
                pe.wait_ge(normed, t * 3 + 3)
                for j in range(2):
                    if t:
                        pe.wait_ge(copied, (t - 1) * 2 + j + 1)
                    for c in range(DC):
                        last = nc.tensor.transpose(tr[j][:, c * P:(c + 1) * P],
                                                   sup[:, t % 2, j, c * P:(c + 1) * P], ident[:, :])
                    last.then_inc(turned, 1)

        @block.vector
        def _(dve):
            dve.wait_ge(gathered, 16 * BT * N)
            for t in range(BT):
                done = [t * STEPS]

                def then(instruction, wait=True):
                    instruction.then_inc(step, 1)
                    done[0] += 1
                    if wait:
                        dve.wait_ge(step, done[0])

                x, st = ri[:, t % 2], strength[:, t]
                dve.wait_ge(squared, t + 1)
                then(nc.vector.tensor_tensor(size[:, :, :], uv[:, :, 0, :], uv[:, :, 1, :], ALU.add))
                then(nc.vector.tensor_scalar(zero[:, :, :], size[:, :, :], 0.0, None, ALU.is_equal), False)
                dve.wait_ge(rooted, t + 1)
                then(nc.vector.tensor_scalar(size[:, :, :], size[:, :, :], 1e-30, None, ALU.max))
                then(nc.vector.reciprocal(size[:, :, :], size[:, :, :]))
                then(nc.vector.tensor_tensor(uv[:, :, :, :], x, size[:, :, :].unsqueeze(2).to_broadcast([P, N, 2, D]),
                                             ALU.mult))
                at = 0
                for gap in range(1, N):
                    k = N - gap
                    then(nc.vector.tensor_tensor(prod[:, 0:k], uv[:, 0:k], uv[:, gap:N], ALU.mult))
                    then(nc.vector.tensor_tensor(cos[:, at:at + k, :], prod[:, 0:k, 0, :], prod[:, 0:k, 1, :], ALU.add))
                    for z in (zero[:, 0:k, :], zero[:, gap:N, :]):
                        then(nc.vector.tensor_tensor(cos[:, at:at + k, :], cos[:, at:at + k, :], z, ALU.add))
                    at += k
                terms = [[(q, i) for q, pair in enumerate(PAIRS) if m in pair for i in pair if i != m]
                         for m in range(N)]
                begun = done[0]
                for n in range(N - 1):
                    for m in range(N):
                        q, i = terms[m][n]
                        if n == 0:
                            then(nc.vector.tensor_scalar(gain[:, m, :], cos[:, q, :], st[:, i, m:m + 1],
                                                         st[:, m, m:m + 1], ALU.mult, ALU.add), False)
                        else:
                            dve.wait_ge(step, begun + (n - 1) * N + m + 1)
                            then(nc.vector.scalar_tensor_tensor(gain[:, m, :], cos[:, q, :], st[:, i, m:m + 1],
                                                                gain[:, m, :], ALU.mult, ALU.add), False)
                dve.wait_ge(step, done[0])
                then(nc.vector.tensor_tensor(prod[:, :, :, :], x, gain[:, :, :].unsqueeze(2).to_broadcast([P, N, 2, D]),
                                             ALU.mult))
                then(nc.vector.tensor_tensor(prod[:, 0:2], prod[:, 0:2], prod[:, 2:4], ALU.add))
                if t >= 2:
                    dve.wait_ge(turned, (t - 1) * 2)
                then(nc.vector.tensor_tensor(sup[:, t % 2], prod[:, 0], prod[:, 1], ALU.add))
                assert done[0] == (t + 1) * STEPS, done[0] - t * STEPS
                dve.wait_ge(lengths, t * 2 + 1)
                nc.vector.tensor_scalar(norm[:, t, 1:2], norm[:, t, 0:1], 1e-8, None, ALU.add).then_inc(normed, 1)
                dve.wait_ge(lengths, t * 2 + 2)
                nc.vector.reciprocal(norm[:, t, 3:4], norm[:, t, 2:3]).then_inc(normed, 1)
                dve.wait_ge(normed, t * 3 + 2)
                nc.vector.tensor_scalar(sup[:, t % 2], sup[:, t % 2], norm[:, t, 3:4], None, ALU.mult).then_inc(normed, 1)
            dve.wait_ge(normed, BT * 3)


def measure_and_top(nc, keep, sup_t, h_dram, wm, wpost, wz, w2, w3, b_post, b_top2, norm_post, ident, out):
    HALF = B // 2
    HT = BT // 2
    F2 = 256 // P
    with ExitStack() as ctx:
        def sb(name, shape, dt=F32):
            return ctx.enter_context(nc.sbuf_tensor(name, shape, dt))
        m_w = sb("meas_w", [P, 3, DC * OUT])
        post_w = sb("post_w", [P, DC * OUT])
        z_w = sb("top1_w", [P, DC * CH])
        w2_sb = sb("top2_w", [P, DC * F2 * P])
        w3_sb = sb("top3_w", [P, F2])
        post_b = sb("post_b", [P, OUT])
        par = sb("post_norm", [P, 2, DC])
        b2_sb = sb("top2_b", [P, F2])
        squares = sb("squares", [P, 2, 2, HALF])
        amp = sb("amp", [P, DC, B])
        z = sb("z_rows", [P, BT, OUT])
        r1 = sb("top1_rows", [P, BT, CH])
        r2 = sb("top2_t", [P, F2, B])
        stats = sb("post_stats", [P, BT, 6])
        mv = sb("post_mv", [P, BT, 2])
        rstd = sb("post_rstd", [P, 3, BT])
        y = sb("y_row", [P, B])
        z_t, r1_t = sup_t[:, 0], sup_t[:, 1]
        acc = [ctx.enter_context(nc.psum_tensor(f"accT{i}", [P, HALF], F32)) for i in range(6)]
        tr = [ctx.enter_context(nc.psum_tensor(f"turnT{i}", [P, HALF], F32)) for i in range(2)]
        s = Sems(nc, keep, ctx, "T")
        loaded = s.ring("loaded", 8)
        negated, measured, squared, summed, amp_ready = (
            s.one(x) for x in ("negated", "measured", "squared", "summed", "amp_ready"))
        posted, z_ready, stats_ready, std_ready, mv_ready, normed = (
            s.one(x) for x in ("posted", "z_ready", "stats_ready", "std_ready", "mv_ready", "normed"))
        turned, z_t_ready, top1_done, r1_ready = (
            s.one(x) for x in ("turned", "z_t_ready", "top1_done", "r1_ready"))
        r1_turned, r1_t_ready, top2_done, r2_ready, top3_done, y_ready = (
            s.one(x) for x in ("r1_turned", "r1_t_ready", "top2_done", "r2_ready", "top3_done", "y_ready"))
        stored = s.dma("stored")
        LOADS = ((m_w[:, 0:2, :], wm), (post_w[:, :], wpost), (post_b[:, :], b_post.to_broadcast([P, OUT])),
                 (par[:, :, :], norm_post), (z_w[:, :], wz), (r1[:, :, :], h_dram[NCH - 1].rearrange("t p f -> p t f")),
                 (w2_sb[:, :], w2), (b2_sb[:, :], b_top2))
        M_W, POST_W, POST_B, PAR, Z_W, X_PART, W2, B2 = range(8)
        block = s.block()

        @block.sync
        def _(sp):
            for i, (to, what) in enumerate(LOADS):
                sp.dma_start(to, what).then_inc(loaded[i], 16)
            sp.dma_start(w3_sb[:, :], w3).then_inc(loaded[W2], 16)
            sp.wait_ge(y_ready, 2)
            sp.dma_start(out, y[0:1, :]).then_inc(stored, 16)
            sp.wait_ge(stored, 16)

        @block.scalar
        def _(act):
            act.wait_ge(loaded[M_W], 16)
            nc.scalar.activation(m_w[:, 2, :], m_w[:, 1, :], ACT.Copy, scale=-1.0).then_inc(negated, 1)
            for half in range(2):
                for c in range(DC):
                    i = half * DC + c
                    for j in range(2):
                        act.wait_ge(measured, 2 * i + j + 1)
                        if i >= 2:
                            act.wait_ge(summed, i - 1)
                        nc.scalar.activation(squares[:, i % 2, j, :], acc[2 * (i % 2) + j][:, :],
                                             ACT.Square).then_inc(squared, 1)
                    act.wait_ge(summed, i + 1)
                    nc.scalar.activation(amp[:, c, half * HALF:(half + 1) * HALF], squares[:, i % 2, 0, :],
                                         ACT.Sqrt).then_inc(amp_ready, 1)
            act.wait_ge(stats_ready, BT + 2)
            nc.scalar.activation(rstd[:, 0, :], rstd[:, 1, :], ACT.Sqrt).then_inc(std_ready, 1)
            act.wait_ge(loaded[PAR], 16)
            for half in range(2):
                for c in range(DC):
                    i = half * DC + c
                    act.wait_ge(turned, i + 1)
                    nc.scalar.activation(z_t[:, c, half * HALF:(half + 1) * HALF], tr[i % 2][:, :], ACT.Gelu,
                                         bias=par[:, 1, c:c + 1], scale=par[:, 0, c:c + 1]).then_inc(z_t_ready, 1)
            for half in range(2):
                for c in range(DC):
                    i = half * DC + c
                    act.wait_ge(r1_turned, i + 1)
                    nc.scalar.activation(r1_t[:, c, half * HALF:(half + 1) * HALF], tr[i % 2][:, :],
                                         ACT.Copy).then_inc(r1_t_ready, 1)
            act.wait_ge(loaded[B2], 16)
            for half in range(2):
                for f in range(F2):
                    act.wait_ge(top2_done, half * F2 + f + 1)
                    nc.scalar.activation(r2[:, f, half * HALF:(half + 1) * HALF], acc[f][:, :], ACT.Relu,
                                         bias=b2_sb[:, f:f + 1]).then_inc(r2_ready, 1)

        @block.vector
        def _(dve):
            for i in range(2 * DC):
                dve.wait_ge(squared, 2 * i + 2)
                nc.vector.tensor_tensor(squares[:, i % 2, 0, :], squares[:, i % 2, 0, :], squares[:, i % 2, 1, :],
                                        ALU.add).then_inc(summed, 1)
            dve.wait_ge(loaded[POST_B], 16)
            for t in range(BT):
                dve.wait_ge(posted, t + 1)
                nc.vector.tensor_tensor(z[:, t, :], acc[t % 6][:, :], post_b[:, :], ALU.add).then_inc(z_ready, 1)
                dve.wait_ge(z_ready, t + 1)
                nc.vector.bn_stats(stats[:, t, :], z[:, t, :]).then_inc(stats_ready, 1)
            dve.wait_ge(stats_ready, BT)
            for t in range(BT):
                last = nc.vector.bn_aggr(mv[:, t, :], stats[:, t, :])
            last.then_inc(stats_ready, 1)
            dve.wait_ge(stats_ready, BT + 1)
            nc.vector.tensor_scalar(rstd[:, 1, :], mv[:, :, 1], LN_EPS, None, ALU.add).then_inc(stats_ready, 1)
            dve.wait_ge(std_ready, 1)
            nc.vector.reciprocal(rstd[:, 2, :], rstd[:, 0, :]).then_inc(mv_ready, 1)
            dve.wait_ge(mv_ready, 1)
            for t in range(BT):
                nc.vector.tensor_scalar(z[:, t, :], z[:, t, :], mv[:, t, 0:1], rstd[:, 2, t:t + 1],
                                        ALU.subtract, ALU.mult).then_inc(normed, 1)
            dve.wait_ge(loaded[X_PART], 16)
            for t in range(BT):
                dve.wait_ge(top1_done, t + 1)
                nc.vector.tensor_tensor(r1[:, t, :], acc[t % 6][:, :], r1[:, t, :], ALU.add).then_inc(r1_ready, 1)
                dve.wait_ge(r1_ready, 2 * t + 1)
                nc.vector.tensor_scalar(r1[:, t, :], r1[:, t, :], 0.0, None, ALU.max).then_inc(r1_ready, 1)
            for half in range(2):
                dve.wait_ge(top3_done, half + 1)
                nc.vector.tensor_copy(y[0:1, half * HALF:(half + 1) * HALF], acc[4 + half][0:1, :]).then_inc(y_ready, 1)

        @block.tensor
        def _(pe):
            pe.wait_ge(loaded[M_W], 16)
            pe.wait_ge(negated, 1)
            for half in range(2):
                cols = slice(half * HALF, (half + 1) * HALF)
                for c in range(DC):
                    i = half * DC + c
                    if i >= 2:
                        pe.wait_ge(squared, 2 * (i - 1))
                    for j in range(2):
                        for e in range(2):
                            which = ((0, 2), (1, 0))[j][e]
                            for k in range(DC):
                                last = nc.tensor.matmul(
                                    acc[2 * (i % 2) + j][:, :], m_w[:, which, k * OUT + c * P:k * OUT + (c + 1) * P],
                                    sup_t[:, e, k, cols], start=e == 0 and k == 0, stop=e == 1 and k == DC - 1)
                        last.then_inc(measured, 1)
            pe.wait_ge(loaded[POST_W], 16)
            pe.wait_ge(squared, 4 * DC)
            for t in range(BT):
                pe.wait_ge(amp_ready, (t // HT + 1) * DC)
                if t >= 6:
                    pe.wait_ge(z_ready, t - 5)
                for k in range(DC):
                    last = nc.tensor.matmul(acc[t % 6][:, :], amp[:, k, t * P:(t + 1) * P],
                                            post_w[:, k * OUT:(k + 1) * OUT], start=k == 0, stop=k == DC - 1)
                last.then_inc(posted, 1)
            for half in range(2):
                pe.wait_ge(normed, (half + 1) * HT)
                for c in range(DC):
                    i = half * DC + c
                    if i >= 2:
                        pe.wait_ge(z_t_ready, i - 1)
                    for t in range(HT):
                        last = nc.tensor.transpose(tr[i % 2][:, t * P:(t + 1) * P],
                                                   z[:, half * HT + t, c * P:(c + 1) * P], ident[:, :])
                    last.then_inc(turned, 1)
            pe.wait_ge(loaded[Z_W], 16)
            pe.wait_ge(z_ready, BT)
            for t in range(BT):
                pe.wait_ge(z_t_ready, (t // HT + 1) * DC)
                if t >= 6:
                    pe.wait_ge(r1_ready, 2 * (t - 6) + 1)
                for k in range(DC):
                    last = nc.tensor.matmul(acc[t % 6][:, :], z_t[:, k, t * P:(t + 1) * P],
                                            z_w[:, k * CH:(k + 1) * CH], start=k == 0, stop=k == DC - 1)
                last.then_inc(top1_done, 1)
            for half in range(2):
                pe.wait_ge(r1_ready, 2 * (half + 1) * HT)
                for c in range(DC):
                    i = half * DC + c
                    pe.wait_ge(r1_t_ready, i - 1) if i >= 2 else pe.wait_ge(z_t_ready, 2 * DC)
                    for t in range(HT):
                        last = nc.tensor.transpose(tr[i % 2][:, t * P:(t + 1) * P],
                                                   r1[:, half * HT + t, c * P:(c + 1) * P], ident[:, :])
                    last.then_inc(r1_turned, 1)
            pe.wait_ge(loaded[W2], 32)
            for half in range(2):
                cols = slice(half * HALF, (half + 1) * HALF)
                pe.wait_ge(r1_t_ready, (half + 1) * DC)
                if half:
                    pe.wait_ge(r2_ready, F2)
                for f in range(F2):
                    for k in range(DC):
                        at = (k * F2 + f) * P
                        last = nc.tensor.matmul(acc[f][:, :], w2_sb[:, at:at + P], r1_t[:, k, cols],
                                                start=k == 0, stop=k == DC - 1)
                    last.then_inc(top2_done, 1)
            for half in range(2):
                pe.wait_ge(r2_ready, (half + 1) * F2)
                for f in range(F2):
                    last = nc.tensor.matmul(acc[4 + half][0:1, :], w3_sb[:, f:f + 1],
                                            r2[:, f, half * HALF:(half + 1) * HALF], start=f == 0, stop=f == F2 - 1)
                last.then_inc(top3_done, 1)


def build(nc, a, out):
    h_dram = nc.dram_tensor("h_rows", [NCH, BT, P, CH], F32, kind="Internal").ap()
    s_dram = nc.dram_tensor("s_feats", [BT, N, P, 2, DC, P], F32, kind="Internal").ap()
    a_dram = nc.dram_tensor("attn_feats", [BT, N, P, 2, DC, P], F32, kind="Internal").ap()
    ri_dram = nc.dram_tensor("ri_states", [BT, P, N, 2 * D], F32, kind="Internal").ap()
    s_flat = s_dram.rearrange("t n p e c b -> t n p (e c b)")
    a_flat = a_dram.rearrange("t n p e c b -> t n p (e c b)")
    with ExitStack() as keep:
        ident = keep.enter_context(nc.sbuf_tensor("ident", [P, P], F32))
        ident_ready = keep.enter_context(nc.semaphore("ident_ready"))
        with nc.Block(no_gpsimd_drain=True) as block:
            @block.sync
            def _(sp):
                sp.dma_start(ident[:, :], a["ident"]).then_inc(ident_ready, 16)
                sp.wait_ge(ident_ready, 16)
        with nc.sbuf_tensor("h_stats", [P, NCH, BT, 6], F32) as stats:
            products_with_x(nc, keep, a["xT"], a["wA"], a["bA"], h_dram, stats)
            for e in range(2):
                second_products(nc, keep, e, h_dram, a["w2"], a["b2"], a["norm2"], stats, ident, s_dram)
        with nc.sbuf_tensor("power", [P, BT, N * N * HEADS], F32) as power:
            scores(nc, keep, s_flat, a["wqk"], a["bqk"], power)
            mix_values(nc, keep, power, s_flat, a["wvo"], a["bv"], a["bo"], ident, a_dram)
        mix_states(nc, keep, a_flat, a["wint"], ri_dram)
        with nc.sbuf_tensor("sup_t", [P, 2, DC, B], F32) as sup_t:
            superpose(nc, keep, a["ids"], [a[f"tbl_{i}"] for i in range(N)], ri_dram, ident, sup_t)
            measure_and_top(nc, keep, sup_t, h_dram, a["wm"], a["wpost"], a["wz"], a["wt2"], a["wt3"],
                            a["b_post"], a["b_top2"], a["norm_post"], ident, out)


def kernel(**inputs):
    import numpy as np
    import concourse.bacc as bacc
    from concourse.bass_utils import run_bass_kernel_spmd

    x = {k.removeprefix("L0_rec_"): np.asarray(v) for k, v in inputs.items()}

    def moving(*names):
        return np.stack([x[n].T.reshape(DC, P, -1).transpose(1, 0, 2).reshape(P, -1) for n in names])

    def columns(a):
        return a.reshape(-1, P).T

    w1 = np.concatenate([x["er_W1"].T, x["ei_W1"].T, x["W_top1"][OUT:]], axis=1)
    arrays = {
        "xT": x["r_x"].T.reshape(KT, P, B),
        "wA": w1.reshape(KT // 2, 2, P, NCH, CH).transpose(3, 0, 2, 1, 4).reshape(NCH, KT // 2, P, 2 * CH),
        "bA": np.concatenate([x["er_b1"], x["ei_b1"], x["b_top1"]])[None],
        "w2": np.stack([x[e + "_W2"].reshape(N, DC, P, 4, 4, P).transpose(0, 1, 3, 5, 4, 2).reshape(N, DC, 4, P, 4 * P)
                        for e in ("er", "ei")]),
        "b2": np.stack([columns(x[e + "_b2"]) for e in ("er", "ei")]),
        "norm2": np.stack([np.stack([columns(x[e + "_g1"]), columns(x[e + "_be1"])], axis=1) for e in ("er", "ei")]),
        "wqk": moving("Wq_r", "Wq_i", "Wk_r", "Wk_i"),
        "bqk": np.stack([x["bq_r"], x["bq_i"], x["bk_r"], x["bk_i"]])[None],
        "wvo": moving("Wv_r", "Wv_i", "Wo_r", "Wo_i"),
        "bv": np.stack([x["bv_r"], x["bv_i"]])[None],
        "bo": np.stack([columns(x["bo_r"]), columns(x["bo_i"])], axis=1),
        "wint": np.stack([x["int_Wr"], x["int_Wi"]], axis=1).transpose(0, 1, 3, 2)
                .reshape(N, 2, DC, P, D).transpose(0, 1, 3, 2, 4).reshape(N, 2, P, DC * D),
        "ids": x["ids"].reshape(BT, P, N).transpose(1, 0, 2),
        "tbl_0": x["tbl_0"], "tbl_1": x["tbl_1"], "tbl_2": x["tbl_2"], "tbl_3": x["tbl_3"],
        "wm": moving("meas_Mr", "meas_Mi").transpose(1, 0, 2),
        "wpost": moving("post_W")[0],
        "wz": x["W_top1"][:OUT].reshape(DC, P, CH).transpose(1, 0, 2).reshape(P, -1),
        "wt2": x["W_top2"].reshape(DC, P, 256).transpose(1, 0, 2).reshape(P, -1),
        "wt3": columns(x["W_top3"][:, 0]),
        "b_post": x["post_b"][None],
        "b_top2": columns(x["b_top2"]),
        "norm_post": np.stack([columns(x["post_g"]), columns(x["post_be"])], axis=1),
        "ident": np.eye(P, dtype=np.float32),
    }
    nc = bacc.Bacc("TRN2", target_bir_lowering=False, num_devices=1)
    arrays = {f"in_{k}": np.ascontiguousarray(v) for k, v in arrays.items()}
    aps = {k[3:]: nc.dram_tensor(k, v.shape, mybir.dt.from_np(v.dtype), kind="ExternalInput").ap()
           for k, v in arrays.items()}
    y = nc.dram_tensor("y", (B, 1), F32, kind="ExternalOutput").ap()
    build(nc, aps, y.rearrange("b one -> one b"))
    r = run_bass_kernel_spmd(nc, [arrays], core_ids=[0])
    return r.results[0]["y"]
```

```python
import concourse.bass as bass
from concourse import mybir
from contextlib import ExitStack

F32 = mybir.dt.float32
F32R = mybir.dt.float32r
I32 = mybir.dt.int32
ALU = mybir.AluOpType
ACT = mybir.ActivationFunctionType
AX = mybir.AxisListType

P = 128
B = 1024
BT = B // P
IN = 2048
HID = 2048
D = 512
N = 4
HEADS = 8
HD = D // HEADS
OUT = 512
KT = IN // P
DC = D // P
CH = 512
NCH = 2 * HID // CH + 1
ECH = HID // CH
LN_EPS = 1e-5


def split_product(nc, out, stat, move, start, stop):
    (sh, sl), (mh, ml) = stat, move
    nc.tensor.matmul(out, sh, mh, start=start, stop=False)
    nc.tensor.matmul(out, sh, ml, start=False, stop=False)
    return nc.tensor.matmul(out, sl, mh, start=False, stop=stop)


class Sems:

    def __init__(self, nc, keep, ctx, phase):
        self.nc, self.keep, self.ctx, self.phase, self.engines_own = nc, keep, ctx, phase, []

    def one(self, name):
        self.engines_own.append(self.ctx.enter_context(self.nc.semaphore(f"{self.phase}_{name}")))
        return self.engines_own[-1]

    def dma(self, name):
        return self.keep.enter_context(self.nc.semaphore(f"{self.phase}_{name}"))

    def ring(self, name, n):
        return [self.dma(f"{name}{i}") for i in range(n)]

    def block(self):
        self.ctx.callback(self.clear)
        return self.ctx.enter_context(self.nc.Block(no_gpsimd_drain=True))

    def clear(self):
        with self.nc.Block(no_gpsimd_drain=True) as block:
            @block.sync
            def _(sp):
                for sem in self.engines_own:
                    sp.sem_clear(sem)


def products_with_x(nc, keep, xT, wA, bA, h_dram, stats):
    PAIR, PAIRS = 2, KT // 2
    RAW, SPL, XRAW, HO = 4, 2, 2, BT
    AHEAD = 1
    with ExitStack() as ctx:
        def sb(name, shape, dt=F32):
            return ctx.enter_context(nc.sbuf_tensor(name, shape, dt))
        x_raw = sb("x_raw", [P, XRAW, B])
        x_hi = sb("x_hi", [P, KT, B], F32R)
        x_lo = sb("x_lo", [P, KT, B], F32R)
        w_raw = sb("wA_raw", [P, RAW, PAIR * CH])
        w_hi = sb("wA_hi", [P, SPL, PAIR * CH], F32R)
        w_lo = sb("wA_lo", [P, SPL, PAIR * CH], F32R)
        bias = sb("bA_all", [P, NCH * CH])
        h_out = sb("h_out", [P, HO, CH])
        acc = [ctx.enter_context(nc.psum_tensor(f"accA{t}", [P, CH], F32)) for t in range(BT)]
        s = Sems(nc, keep, ctx, "A")
        x_loaded = s.ring("x_loaded", XRAW)
        w_loaded = s.ring("w_loaded", RAW)
        bias_loaded = s.dma("bias_loaded")
        x_hi_ready, x_split = s.one("x_hi_ready"), s.one("x_split")
        w_hi_ready, w_split = s.one("w_hi_ready"), s.one("w_split")
        w_used = s.one("w_used")
        acc_ready, acc_taken = s.one("acc_ready"), s.one("acc_taken")
        stats_done = s.one("stats_done")
        h_stored = s.ring("h_stored", HO)
        block = s.block()

        @block.sync
        def _(sp):
            def load_w(c, j):
                if not (isinstance(c, int) and c * PAIRS + j < RAW):
                    sp.wait_ge(w_split, c * PAIRS + j - RAW + 1)
                sp.dma_start(w_raw[:, j % RAW, :], wA[c, j]).then_inc(w_loaded[j % RAW], 16)

            for j in range(PAIRS):
                for k in range(PAIR * j, PAIR * j + PAIR):
                    if k >= XRAW:
                        sp.wait_ge(x_split, k - XRAW + 1)
                    sp.dma_start(x_raw[:, k % XRAW, :], xT[k]).then_inc(x_loaded[k % XRAW], 16)
                load_w(0, j)
            sp.dma_start(bias[:, :], bA.to_broadcast([P, NCH * CH])).then_inc(bias_loaded, 16)
            with sp.Fori(1, NCH) as c:
                for j in range(PAIRS):
                    load_w(c, j)

        @block.scalar
        def _(act):
            def split_w(c, j):
                act.wait_ge(w_loaded[j % RAW], (c * (PAIRS // RAW) + j // RAW + 1) * 16)
                if j >= SPL:
                    act.wait_ge(w_used, c * (PAIRS - 1) + j - SPL + 1)
                elif not (isinstance(c, int) and c == 0):
                    if j == SPL - 1:
                        act.wait_ge(acc_ready, c * BT)
                    else:
                        act.wait_ge(w_used, c * (PAIRS - 1) + j - SPL + 2)
                nc.scalar.activation(w_hi[:, j % SPL, :], w_raw[:, j % RAW, :], ACT.Copy).then_inc(w_hi_ready, 1)

            for j in range(PAIRS):
                for k in range(PAIR * j, PAIR * j + PAIR):
                    act.wait_ge(x_loaded[k % XRAW], (k // XRAW + 1) * 16)
                    nc.scalar.activation(x_hi[:, k, :], x_raw[:, k % XRAW, :], ACT.Copy).then_inc(x_hi_ready, 1)
                split_w(0, j)
            with act.Fori(1, NCH) as c:
                for j in range(PAIRS):
                    split_w(c, j)

        @block.vector
        def _(dve):
            def split_w(c, j):
                dve.wait_ge(w_hi_ready, c * PAIRS + j + 1)
                nc.vector.tensor_tensor(w_lo[:, j % SPL, :], w_raw[:, j % RAW, :],
                                        w_hi[:, j % SPL, :].bitcast(F32), ALU.subtract).then_inc(w_split, 1)

            def take(c):
                for t in range(BT):
                    dve.wait_ge(acc_ready, c * BT + t + 1)
                    if not (isinstance(c, int) and c == 0):
                        dve.wait_ge(h_stored[t], c * 16)
                    nc.vector.tensor_tensor(h_out[:, t, :], acc[t][:, :], bias[:, bass.ts(c, CH)],
                                            ALU.add).then_inc(acc_taken, 1)
                for t in range(BT):
                    dve.wait_ge(acc_taken, c * BT + t + 1)
                    nc.vector.bn_stats(stats[:, c, t, :], h_out[:, t, :]).then_inc(stats_done, 1)

            for j in range(PAIRS):
                for k in range(PAIR * j, PAIR * j + PAIR):
                    dve.wait_ge(x_hi_ready, k + 1)
                    nc.vector.tensor_tensor(x_lo[:, k, :], x_raw[:, k % XRAW, :],
                                            x_hi[:, k, :].bitcast(F32), ALU.subtract).then_inc(x_split, 1)
                split_w(0, j)
            for j in range(AHEAD):
                split_w(1, j)
            dve.wait_ge(bias_loaded, 16)
            take(0)
            for j in range(AHEAD, PAIRS):
                split_w(1, j)
            with dve.Fori(2, NCH) as c:
                for j in range(AHEAD):
                    split_w(c, j)
                take(c - 1)
                for j in range(AHEAD, PAIRS):
                    split_w(c, j)
            take(NCH - 1)

        @block.tensor
        def _(pe):
            def chunk(c):
                first = isinstance(c, int)
                for j in range(PAIRS):
                    if first:
                        pe.wait_ge(x_split, PAIR * (j + 1))
                    pe.wait_ge(w_split, c * PAIRS + j + 1)
                    for kk in range(PAIR):
                        k = PAIR * j + kk
                        cols = slice(kk * CH, (kk + 1) * CH)
                        for t in range(BT):
                            if k == 0 and not first:
                                pe.wait_ge(acc_taken, (c - 1) * BT + t + 1)
                            rows = slice(t * P, (t + 1) * P)
                            last = split_product(
                                nc, acc[t][:, :], (x_hi[:, k, rows], x_lo[:, k, rows]),
                                (w_hi[:, j % SPL, cols], w_lo[:, j % SPL, cols]), k == 0, k == KT - 1)
                            if k == KT - 1:
                                last.then_inc(acc_ready, 1)
                    if j < PAIRS - 1:
                        last.then_inc(w_used, 1)

            chunk(0)
            with pe.Fori(1, NCH) as c:
                chunk(c)

        @block.gpsimd
        def _(pool):
            def store(c):
                for t in range(BT):
                    pool.wait_ge(acc_taken, c * BT + t + 1)
                    pool.dma_start(h_dram[c, t], h_out[:, t, :]).then_inc(h_stored[t], 16)

            with pool.Fori(0, NCH) as c:
                store(c)
            for t in range(BT):
                pool.wait_ge(h_stored[t], 16 * NCH)
            pool.wait_ge(stats_done, NCH * BT)


def second_products(nc, keep, e, h_dram, w2, b2, norm2, stats, ident, s_dram):
    QK = 4
    QS = KT // QK
    HALF = B // 2
    HT = BT // 2
    with ExitStack() as ctx:
        def sb(name, shape, dt=F32):
            return ctx.enter_context(nc.sbuf_tensor(f"{name}_{e}", shape, dt))
        g_hi = sb("g_hi", [P, KT, B], F32R)
        g_lo = sb("g_lo", [P, KT, B], F32R)
        h_raw = sb("h_raw", [P, 2, HT, CH])
        gelu = sb("gelu", [P, 2, HALF])
        w_raw = sb("w2_raw", [P, QS, QK * P])
        w_hi = sb("w2_hi", [P, QS, QK * P], F32R)
        w_lo = sb("w2_lo", [P, QS, QK * P], F32R)
        s_out = sb("s_out", [P, 4, HALF])
        par = sb("norm2", [P, 2, KT])
        bias = sb("b2", [P, KT])
        mv = sb("mv", [P, BT, 2])
        rstd = sb("rstd", [P, 3, BT])
        tr = [ctx.enter_context(nc.psum_tensor(f"turn{e}{i}", [P, HALF], F32)) for i in range(4)]
        acc = [ctx.enter_context(nc.psum_tensor(f"accS{e}{i}", [P, HALF], F32)) for i in range(4)]
        s = Sems(nc, keep, ctx, f"E{e}")
        par_loaded = s.dma("par_loaded")
        h_loaded = s.ring("h_loaded", 2)
        w_loaded = s.ring("w_loaded", QS)
        var_ready, std_ready, mv_ready = s.one("var_ready"), s.one("std_ready"), s.one("mv_ready")
        normed, turned = s.one("normed"), s.one("turned")
        gelu_ready, g_hi_ready, g_split = s.one("gelu_ready"), s.one("g_hi_ready"), s.one("g_split")
        w_hi_ready, w_split, w_used = s.one("w_hi_ready"), s.one("w_split"), s.one("w_used")
        acc_ready, s_ready = s.one("acc_ready"), s.one("s_ready")
        s_stored = s.ring("s_stored", 4)
        block = s.block()

        @block.sync
        def _(sp):
            def load_w(n, u, q):
                if not (isinstance(n, int) and u == 0):
                    sp.wait_ge(w_split, (n * DC + u - 1) * QS + q + 1)
                sp.dma_start(w_raw[:, q, :], w2[e, n, u, q]).then_inc(w_loaded[q], 16)

            for i in range(2 * ECH):
                c, half = i // 2, i % 2
                if i >= 2:
                    sp.wait_ge(turned, (i - 1) * QK)
                sp.dma_start(h_raw[:, half, :, :], h_dram[e * ECH + c, half * HT:(half + 1) * HT]
                             .rearrange("t p f -> p t f")).then_inc(h_loaded[half], 16)
                if i == 0:
                    sp.dma_start(par[:, :, :], norm2[e]).then_inc(par_loaded, 16)
                    sp.dma_start(bias[:, :], b2[e]).then_inc(par_loaded, 16)
                if i == 1:
                    for q in range(QS):
                        load_w(0, 0, q)
            for u in range(1, DC):
                for q in range(QS):
                    load_w(0, u, q)
            with sp.Fori(1, N) as n:
                for u in range(DC):
                    for q in range(QS):
                        load_w(n, u, q)

        @block.scalar
        def _(act):
            def split_w(n, u, q):
                act.wait_ge(w_loaded[q], (n * DC + u + 1) * 16)
                if not (isinstance(n, int) and u == 0):
                    if q < QS - 1:
                        act.wait_ge(w_used, (n * DC + u - 1) * (QS - 1) + q + 1)
                    else:
                        act.wait_ge(acc_ready, (n * DC + u) * 2)
                nc.scalar.activation(w_hi[:, q, :], w_raw[:, q, :], ACT.Copy).then_inc(w_hi_ready, 1)

            act.wait_ge(var_ready, 1)
            nc.scalar.activation(rstd[:, 0, :], rstd[:, 1, :], ACT.Sqrt).then_inc(std_ready, 1)
            act.wait_ge(par_loaded, 32)
            for i in range(2 * ECH):
                c, half = i // 2, i % 2
                for kk in range(QK):
                    k, m = c * QK + kk, i * QK + kk
                    act.wait_ge(turned, m + 1)
                    if m >= 2:
                        act.wait_ge(g_split, m - 1)
                    nc.scalar.activation(gelu[:, m % 2, :], tr[m % 4][:, :], ACT.Gelu,
                                         bias=par[:, 1, k:k + 1], scale=par[:, 0, k:k + 1]).then_inc(gelu_ready, 1)
                if half == 0:
                    split_w(0, 0, c)
            for u in range(1, DC):
                for q in range(QS):
                    split_w(0, u, q)
            with act.Fori(1, N) as n:
                for u in range(DC):
                    for q in range(QS):
                        split_w(n, u, q)

        @block.vector
        def _(dve):
            def split_w(n, u, q):
                dve.wait_ge(w_hi_ready, (n * DC + u) * QS + q + 1)
                nc.vector.tensor_tensor(w_lo[:, q, :], w_raw[:, q, :], w_hi[:, q, :].bitcast(F32),
                                        ALU.subtract).then_inc(w_split, 1)

            def take(n, u):
                for half in range(2):
                    slot = 2 * (u % 2) + half
                    dve.wait_ge(acc_ready, (n * DC + u) * 2 + half + 1)
                    if not (isinstance(n, int) and u < 2):
                        dve.wait_ge(s_stored[slot], (n * 2 + u // 2) * 16)
                    nc.vector.tensor_scalar(s_out[:, slot, :], acc[slot][:, :],
                                            bias[:, bass.ds(n * DC + u, 1)], None, ALU.add).then_inc(s_ready, 1)

            for t in range(BT):
                last = nc.vector.bn_aggr(mv[:, t, :], stats[:, e * ECH:(e + 1) * ECH, t, :])
            last.then_inc(mv_ready, 1)
            dve.wait_ge(mv_ready, 1)
            nc.vector.tensor_scalar(rstd[:, 1, :], mv[:, :, 1], LN_EPS, None, ALU.add).then_inc(var_ready, 1)
            dve.wait_ge(std_ready, 1)
            nc.vector.reciprocal(rstd[:, 2, :], rstd[:, 0, :]).then_inc(mv_ready, 1)
            dve.wait_ge(mv_ready, 2)

            def norm(i):
                half = i % 2
                dve.wait_ge(h_loaded[half], (i // 2 + 1) * 16)
                for t in range(HT):
                    row = half * HT + t
                    nc.vector.tensor_scalar(h_raw[:, half, t, :], h_raw[:, half, t, :], mv[:, row, 0:1],
                                            rstd[:, 2, row:row + 1], ALU.subtract, ALU.mult).then_inc(normed, 1)

            norm(0)
            for i in range(2 * ECH):
                c, half = i // 2, i % 2
                if i + 1 < 2 * ECH:
                    norm(i + 1)
                for kk in range(QK):
                    k, m = c * QK + kk, i * QK + kk
                    rows = slice(half * HALF, (half + 1) * HALF)
                    dve.wait_ge(gelu_ready, m + 1)
                    nc.vector.tensor_copy(g_hi[:, k, rows], gelu[:, m % 2, :]).then_inc(g_hi_ready, 1)
                    dve.wait_ge(g_hi_ready, m + 1)
                    nc.vector.tensor_tensor(g_lo[:, k, rows], gelu[:, m % 2, :], g_hi[:, k, rows].bitcast(F32),
                                            ALU.subtract).then_inc(g_split, 1)
                if half == 0:
                    split_w(0, 0, c)
            dve.wait_ge(par_loaded, 32)
            for u in range(1, DC):
                for q in range(QS):
                    split_w(0, u, q)
                take(0, u - 1)
            with dve.Fori(1, N) as n:
                for u in range(DC):
                    for q in range(QS):
                        split_w(n, u, q)
                    if u == 0:
                        take(n - 1, DC - 1)
                    else:
                        take(n, u - 1)
            take(N - 1, DC - 1)

        @block.tensor
        def _(pe):
            def turn(i):
                half = i % 2
                pe.wait_ge(normed, (i + 1) * HT)
                for kk in range(QK):
                    m = i * QK + kk
                    if m >= 4:
                        pe.wait_ge(gelu_ready, m - 3)
                    for t in range(HT):
                        last = nc.tensor.transpose(tr[m % 4][:, t * P:(t + 1) * P],
                                                   h_raw[:, half, t, kk * P:(kk + 1) * P], ident[:, :])
                    last.then_inc(turned, 1)

            def products(n, u, q):
                pe.wait_ge(w_split, (n * DC + u) * QS + q + 1)
                for kk in range(QK):
                    k = q * QK + kk
                    cols = slice(kk * P, (kk + 1) * P)
                    for half in range(2):
                        if k == 0 and not (isinstance(n, int) and u < 2):
                            pe.wait_ge(s_ready, (n * DC + u - 2) * 2 + half + 1)
                        rows = slice(half * HALF, (half + 1) * HALF)
                        last = split_product(nc, acc[2 * (u % 2) + half][:, :],
                                             (w_hi[:, q, cols], w_lo[:, q, cols]),
                                             (g_hi[:, k, rows], g_lo[:, k, rows]), k == 0, k == KT - 1)
                        if k == KT - 1 and half == 0:
                            last.then_inc(acc_ready, 1)
                if q < QS - 1:
                    last.then_inc(w_used, 1)
                else:
                    last.then_inc(acc_ready, 1)

            for c in range(ECH):
                turn(2 * c)
                turn(2 * c + 1)
                if c >= 1:
                    pe.wait_ge(g_split, c * 2 * QK)
                    products(0, 0, c - 1)
            pe.wait_ge(g_split, ECH * 2 * QK)
            products(0, 0, QS - 1)
            for u in range(1, DC):
                for q in range(QS):
                    products(0, u, q)
            with pe.Fori(1, N) as n:
                for u in range(DC):
                    for q in range(QS):
                        products(n, u, q)

        @block.gpsimd
        def _(pool):
            def store(n):
                for u in range(DC):
                    for half in range(2):
                        slot = 2 * (u % 2) + half
                        pool.wait_ge(s_ready, (n * DC + u) * 2 + half + 1)
                        pool.dma_start(
                            s_dram[half * HT:(half + 1) * HT, n, :, e, u].rearrange("t p b -> p t b"),
                            s_out[:, slot, :].rearrange("p (t b) -> p t b", b=P)).then_inc(s_stored[slot], 16)
            with pool.Fori(0, N) as n:
                store(n)
            for slot in range(4):
                pool.wait_ge(s_stored[slot], 16 * 2 * N)


def scores(nc, keep, s_dram, wqk, bqk, power):
    MATS = 4
    W = N * N * HEADS
    SLOTS = 3
    with ExitStack() as ctx:
        def sb(name, shape, dt=F32):
            return ctx.enter_context(nc.sbuf_tensor(name, shape, dt))
        w_hi = sb("wqk_hi", [P, MATS, DC, D], F32R)
        w_lo = sb("wqk_lo", [P, MATS, DC, D], F32R)
        bias = sb("bqk_parts", [P, MATS, D], F32R)
        picks = sb("picks", [P, P], F32R)
        s_raw = sb("sB_raw", [P, 2, 2, DC * P])
        s_hi = sb("sB_hi", [P, 2, 2, DC * P], F32R)
        s_lo = sb("sB_lo", [P, 2, 2, DC * P], F32R)
        q = sb("q_parts", [P, N, 3, D])
        k = sb("k_parts", [P, 2, N, 3, D])
        prod = sb("prod", [P, SLOTS, N, D])
        part = sb("part", [P, 2, 3, W])
        both = sb("both", [P, 2, 2, W])
        picks_raw = sb("picks_raw", [P, P])
        w_raw = k[:, 1].rearrange("p n i d -> p (n i d)")[:, 0:2 * DC * D].rearrange("p (s x) -> p s x", s=2)
        b_raw = q[:, :, 0, :]
        acc = [[ctx.enter_context(nc.psum_tensor(f"accB{i}{m}", [P, D], F32)) for m in range(MATS)] for i in range(2)]
        s = Sems(nc, keep, ctx, "B")
        w_loaded, bias_loaded = s.ring("w_loaded", 2), s.dma("bias_loaded")
        w_hi_ready, w_split = s.one("w_hi_ready"), s.one("w_split")
        zeroed, bias_ready = s.one("zeroed"), s.one("bias_ready")
        s_loaded = s.ring("s_loaded", 2)
        s_hi_ready, s_split = s.one("s_hi_ready"), s.one("s_split")
        acc_ready, copied, k_ready, q_ready = s.one("acc_ready"), s.one("copied"), s.one("k_ready"), s.one("q_ready")
        multiplied, summed = s.one("multiplied"), s.one("summed")
        small = s.one("small")
        PRODS = 3 * N
        SMALL = 5
        block = s.block()

        def first(t, n=0, m=0):
            return isinstance(t, int) and t * N + n < m

        @block.sync
        def _(sp):
            def load_s(t, n):
                if not first(t, n, 2):
                    sp.wait_ge(s_split, t * N + n - 1)
                sp.dma_start(s_raw[:, n % 2, :, :].rearrange("p e x -> p (e x)"), s_dram[t, n]).then_inc(s_loaded[n % 2], 16)

            sp.wait_ge(zeroed, 2)
            for r in (0, 32):
                sp.dma_start(b_raw[r:r + 1, :, :], bqk).then_inc(bias_loaded, 16)
            for m in range(2):
                sp.dma_start(w_raw[:, m, :], wqk[m]).then_inc(w_loaded[m], 16)
            load_s(0, 0)
            for m in range(2, MATS):
                sp.wait_ge(w_split, m - 1)
                sp.dma_start(w_raw[:, m % 2, :], wqk[m]).then_inc(w_loaded[m % 2], 16)
            for n in range(1, N):
                load_s(0, n)
            for n in range(N):
                load_s(1, n)
            with sp.Fori(2, BT) as t:
                for n in range(N):
                    load_s(t, n)

        @block.scalar
        def _(act):
            def split_s(t, n):
                act.wait_ge(s_loaded[n % 2], (t * 2 + n // 2 + 1) * 16)
                if not first(t, n, 2):
                    act.wait_ge(acc_ready, (t * N + n - 1) * MATS)
                nc.scalar.activation(s_hi[:, n % 2, :, :], s_raw[:, n % 2, :, :], ACT.Copy).then_inc(s_hi_ready, 1)

            def copy(t, u, n):
                if not first(t, 0, 1):
                    act.wait_ge(multiplied, (t - 1) * PRODS + 3 * (n + 1))
                for m, to in enumerate((q[:, n, 0, :], q[:, n, 1, :], k[:, u, n, 0, :])):
                    act.wait_ge(acc_ready, (t * N + n) * MATS + m + 1)
                    nc.scalar.activation(to, acc[n % 2][m][:, :], ACT.Copy).then_inc(copied, 1)

            for m in range(MATS):
                act.wait_ge(w_loaded[m % 2], 16 * (m // 2 + 1))
                nc.scalar.activation(w_hi[:, m, :, :], w_raw[:, m % 2, :], ACT.Copy).then_inc(w_hi_ready, 1)
                if m == 0:
                    split_s(0, 0)
            act.wait_ge(bias_ready, 3)

            def tile(t, u):
                for n in range(N):
                    if n < N - 1:
                        split_s(t, n + 1)
                    elif not (isinstance(t, int) and t == BT - 1):
                        split_s(t + 1, 0)
                    copy(t, u, n)

            tile(0, 0)
            tile(1, 1)
            with act.Fori(1, BT // 2 - 1) as i:
                tile(i * 2, 0)
                tile(i * 2 + 1, 1)
            tile(BT - 2, 0)
            tile(BT - 1, 1)

        @block.gpsimd
        def _(pool):
            nc.gpsimd.memset(b_raw, 0.0).then_inc(zeroed, 1)
            nc.gpsimd.memset(picks_raw[:, :], 0.0).then_inc(zeroed, 1)
            pool.wait_ge(zeroed, 2)
            for r in (0, 32):
                nc.gpsimd.memset(picks_raw[r:r + 1, :], 1.0).then_inc(zeroed, 1)
            pool.wait_ge(zeroed, 4)

            def split_s(t, n):
                pool.wait_ge(s_hi_ready, t * N + n + 1)
                nc.gpsimd.tensor_tensor(s_lo[:, n % 2, :, :], s_raw[:, n % 2, :, :],
                                        s_hi[:, n % 2, :, :].bitcast(F32), ALU.subtract).then_inc(s_split, 1)

            def add_q(t, n):
                pool.wait_ge(copied, (t * N + n) * 3 + 2)
                nc.gpsimd.tensor_tensor(q[:, n, 2, :], q[:, n, 0, :], q[:, n, 1, :], ALU.add).then_inc(q_ready, 1)

            def combine(t, u):
                pool.wait_ge(summed, (t + 1) * PRODS)
                m1, m2, m3 = (part[:, u, i, :] for i in range(3))
                re, im = both[:, u, 0, :], both[:, u, 1, :]
                nc.gpsimd.tensor_tensor(re, m1, m3, ALU.add).then_inc(small, 1)
                nc.gpsimd.tensor_tensor(im, m1, m2, ALU.subtract).then_inc(small, 1)
                pool.wait_ge(small, t * SMALL + 2)
                nc.gpsimd.tensor_tensor(re, re, re, ALU.mult).then_inc(small, 1)
                nc.gpsimd.tensor_tensor(im, im, im, ALU.mult).then_inc(small, 1)
                pool.wait_ge(small, t * SMALL + 4)
                nc.gpsimd.tensor_tensor(power[:, t, :], re, im, ALU.add).then_inc(small, 1)

            split_s(0, 0)

            def tile(t, u):
                for n in range(N):
                    if n < N - 1:
                        split_s(t, n + 1)
                    elif not (isinstance(t, int) and t == BT - 1):
                        split_s(t + 1, 0)
                    add_q(t, n)
                    if n == N - 1 and not first(t, 0, 1):
                        combine(t - 1, 1 - u)

            tile(0, 0)
            tile(1, 1)
            with pool.Fori(1, BT // 2 - 1) as i:
                tile(i * 2, 0)
                tile(i * 2 + 1, 1)
            tile(BT - 2, 0)
            tile(BT - 1, 1)
            combine(BT - 1, 1)
            pool.wait_ge(small, BT * SMALL)

        @block.vector
        def _(dve):
            dve.wait_ge(zeroed, 4)
            nc.vector.tensor_copy(picks[:, :], picks_raw[:, :]).then_inc(bias_ready, 1)
            dve.wait_ge(bias_loaded, 32)
            nc.vector.tensor_copy(bias[:, :, :], b_raw).then_inc(bias_ready, 1)
            dve.wait_ge(bias_ready, 2)
            nc.vector.tensor_tensor(bias[32:33, :, :], b_raw[32:33], bias[32:33, :, :].bitcast(F32),
                                    ALU.subtract).then_inc(bias_ready, 1)
            for m in range(MATS):
                dve.wait_ge(w_hi_ready, m + 1)
                nc.vector.tensor_tensor(w_lo[:, m, :, :].rearrange("p c d -> p (c d)"), w_raw[:, m % 2, :],
                                        w_hi[:, m, :, :].rearrange("p c d -> p (c d)").bitcast(F32),
                                        ALU.subtract).then_inc(w_split, 1)

            def finish_k(t, u, n):
                dve.wait_ge(copied, (t * N + n + 1) * 3)
                dve.wait_ge(acc_ready, (t * N + n + 1) * MATS)
                ki = acc[n % 2][3][:, :]
                nc.vector.tensor_tensor(k[:, u, n, 1, :], ki, k[:, u, n, 0, :], ALU.add)
                nc.vector.tensor_tensor(k[:, u, n, 2, :], ki, k[:, u, n, 0, :], ALU.subtract).then_inc(k_ready, 1)

            def tile(t, u, more):
                dve.wait_ge(k_ready, (t + 1) * N)
                pairs = ((2, 0), (0, 1), (1, 2))

                def add_up(r):
                    n, i = r // 3, r % 3
                    dve.wait_ge(multiplied, t * PRODS + r + 1)
                    nc.vector.tensor_reduce(part[:, u, i, n * N * HEADS:(n + 1) * N * HEADS],
                                            prod[:, r % SLOTS, :, :].rearrange("p m (h d) -> p (m h) d", d=HD),
                                            AX.X, ALU.add).then_inc(summed, 1)

                for n in range(N):
                    dve.wait_ge(q_ready, t * N + n + 1)
                    for i, (a, b) in enumerate(pairs):
                        r = 3 * n + i
                        if not first(t, 0, 1) or r >= SLOTS:
                            dve.wait_ge(summed, t * PRODS + r - SLOTS + 1)
                        nc.vector.tensor_tensor(prod[:, r % SLOTS, :, :], k[:, u, :, b, :],
                                                q[:, n, a, :].unsqueeze(1).to_broadcast([P, N, D]),
                                                ALU.mult).then_inc(multiplied, 1)
                        if r:
                            add_up(r - 1)
                    if n == N - 1:
                        add_up(PRODS - 1)
                    if more:
                        finish_k(t + 1, 1 - u, n)

            for n in range(N):
                finish_k(0, 0, n)
            tile(0, 0, True)
            tile(1, 1, True)
            with dve.Fori(1, BT // 2 - 1) as i:
                tile(i * 2, 0, True)
                tile(i * 2 + 1, 1, True)
            tile(BT - 2, 0, True)
            tile(BT - 1, 1, False)

        @block.tensor
        def _(pe):
            pe.wait_ge(bias_ready, 3)

            def tile(t):
                for n in range(N):
                    pe.wait_ge(s_split, t * N + n + 1)
                    if not first(t, n, 2):
                        pe.wait_ge(copied, (t * N + n - 1) * 3)
                        pe.wait_ge(k_ready, t * N + n - 1)
                    for m in range(MATS):
                        e = m % 2
                        if first(t, n, 1):
                            pe.wait_ge(w_split, m + 1)
                        out = acc[n % 2][m][:, :]
                        nc.tensor.matmul(out, picks[:, :], bias[:, m, :], start=True, stop=False)
                        for c in range(DC):
                            x = slice(c * P, (c + 1) * P)
                            last = split_product(nc, out, (s_hi[:, n % 2, e, x], s_lo[:, n % 2, e, x]),
                                                 (w_hi[:, m, c, :], w_lo[:, m, c, :]), False, c == DC - 1)
                        last.then_inc(acc_ready, 1)

            tile(0)
            with pe.Fori(1, BT) as t:
                tile(t)


def mix_values(nc, keep, power, s_dram, wvo, bv, bo, ident, a_dram):
    MATS = 4
    W = N * N * HEADS
    with ExitStack() as ctx:
        def sb(name, shape, dt=F32):
            return ctx.enter_context(nc.sbuf_tensor(name, shape, dt))
        w_hi = sb("wvo_hi", [P, MATS, DC, D], F32R)
        w_lo = sb("wvo_lo", [P, MATS, DC, D], F32R)
        s_raw = sb("sV_raw", [P, 2, 2, DC * P])
        s_hi = sb("sV_hi", [P, 2, 2, DC * P], F32R)
        s_lo = sb("sV_lo", [P, 2, 2, DC * P], F32R)
        bias_v = sb("bv_all", [P, 2, D])
        bias_o = sb("bo_cols", [P, 2, DC])
        v = sb("v_rows", [P, 2, 2, N, D])
        prod = sb("prodV", [P, 2, N, D])
        o = sb("mixed", [P, 2, N, D])
        ot_hi = sb("ot_hi", [P, DC, N * P], F32R)
        ot_lo = sb("ot_lo", [P, DC, N * P], F32R)
        a_out = sb("a_out", [P, 2, N, DC, P])
        top = sb("softmax_top", [P, BT, N, HEADS])
        w_raw = v[:, 1].rearrange("p e n d -> p (e n d)").rearrange("p (s x) -> p s x", s=2)
        vb = [[ctx.enter_context(nc.psum_tensor(f"accV{i}{e}", [P, D], F32)) for e in range(2)] for i in range(2)]
        tr = [ctx.enter_context(nc.psum_tensor(f"turnV{i}", [P, N * P], F32)) for i in range(2)]
        ob = [ctx.enter_context(nc.psum_tensor(f"accO{i}", [P, N * P], F32)) for i in range(2)]
        s = Sems(nc, keep, ctx, "V")
        w_loaded, bias_loaded = s.ring("w_loaded", 2), s.dma("bias_loaded")
        w_hi_ready, w_split = s.one("w_hi_ready"), s.one("w_split")
        s_loaded = s.ring("s_loaded", 2)
        s_hi_ready, s_split = s.one("s_hi_ready"), s.one("s_split")
        soft, root, exped, prob_ready = s.one("soft"), s.one("root"), s.one("exped"), s.one("prob_ready")
        v_ready, v_taken = s.one("v_ready"), s.one("v_taken")
        multiplied, halved, o_ready = s.one("multiplied"), s.one("halved"), s.one("o_ready")
        turned, ot_hi_ready, ot_split = s.one("turned"), s.one("ot_hi_ready"), s.one("ot_split")
        out_ready, out_taken = s.one("out_ready"), s.one("out_taken")
        stored = s.ring("stored", 2)
        block = s.block()

        def first(t, n=0, m=0):
            return isinstance(t, int) and t * N + n < m

        @block.sync
        def _(sp):
            def load_s(t, n):
                if not first(t, n, 2):
                    sp.wait_ge(s_split, t * N + n - 1)
                sp.dma_start(s_raw[:, n % 2, :, :].rearrange("p e x -> p (e x)"), s_dram[t, n]).then_inc(s_loaded[n % 2], 16)

            for m in range(2):
                sp.dma_start(w_raw[:, m, :], wvo[m]).then_inc(w_loaded[m], 16)
            load_s(0, 0)
            sp.dma_start(bias_v[:, :, :], bv.to_broadcast([P, 2, D])).then_inc(bias_loaded, 16)
            sp.dma_start(bias_o[:, :, :], bo).then_inc(bias_loaded, 16)
            for m in range(2, MATS):
                sp.wait_ge(w_split, m - 1)
                sp.dma_start(w_raw[:, m % 2, :], wvo[m]).then_inc(w_loaded[m % 2], 16)
            for n in range(1, N):
                load_s(0, n)
            with sp.Fori(1, BT) as t:
                for n in range(N):
                    load_s(t, n)

        @block.scalar
        def _(act):
            def split_s(t, n):
                act.wait_ge(s_loaded[n % 2], (t * 2 + n // 2 + 1) * 16)
                if not first(t, n, 2):
                    act.wait_ge(v_ready, (t * N + n - 1) * 2)
                nc.scalar.activation(s_hi[:, n % 2, :, :], s_raw[:, n % 2, :, :], ACT.Copy).then_inc(s_hi_ready, 1)

            def split_w(m):
                act.wait_ge(w_loaded[m % 2], 16 * (m // 2 + 1))
                nc.scalar.activation(w_hi[:, m, :, :], w_raw[:, m % 2, :], ACT.Copy).then_inc(w_hi_ready, 1)

            def split_o(t, e):
                for c in range(DC):
                    r = (t * 2 + e) * DC + c
                    act.wait_ge(turned, r + 1)
                    if not (isinstance(t, int) and t == 0 and e == 0):
                        act.wait_ge(out_ready, (t * 2 + e) * DC)
                    nc.scalar.activation(ot_hi[:, c, :], tr[c % 2][:, :], ACT.Copy).then_inc(ot_hi_ready, 1)

            def take_out(t, e):
                if not (isinstance(t, int) and t == 0):
                    act.wait_ge(stored[e], t * 16)
                for c in range(DC):
                    act.wait_ge(out_ready, (t * 2 + e) * DC + c + 1)
                    nc.scalar.activation(a_out[:, e, :, c, :], ob[c % 2][:, :].rearrange("p (n b) -> p n b", b=P),
                                         ACT.Identity, bias=bias_o[:, e, c:c + 1]).then_inc(out_taken, 1)

            split_w(0)
            split_s(0, 0)
            split_w(1)
            act.wait_ge(soft, 1)
            nc.scalar.activation(power[:, :, :], power[:, :, :], ACT.Sqrt).then_inc(root, 1)
            split_w(2)
            act.wait_ge(soft, 3)
            nc.scalar.activation(power[:, :, :], power[:, :, :], ACT.Exp, scale=HD ** -0.5).then_inc(exped, 1)
            split_w(3)
            for n in range(1, N):
                split_s(0, n)
            act.wait_ge(bias_loaded, 32)

            def step(t, splits):
                for e in range(2):
                    for half in range(2):
                        if 2 * e + half < splits:
                            split_s(t + 1 + e, 2 * (1 - e) + half)
                        if half == 0:
                            split_o(t, e)
                        else:
                            take_out(t, e)

            split_s(1, 0)
            split_s(1, 1)
            step(0, 4)
            with act.Fori(1, BT - 2) as t:
                step(t, 4)
            step(BT - 2, 2)
            step(BT - 1, 0)

        @block.gpsimd
        def _(pool):
            def split_s(t, n):
                pool.wait_ge(s_hi_ready, t * N + n + 1)
                nc.gpsimd.tensor_tensor(s_lo[:, n % 2, :, :], s_raw[:, n % 2, :, :],
                                        s_hi[:, n % 2, :, :].bitcast(F32), ALU.subtract).then_inc(s_split, 1)

            def store(t, e):
                pool.wait_ge(out_taken, (t * 2 + e + 1) * DC)
                pool.dma_start(a_dram[t, :, :, e].rearrange("n p c b -> p n (c b)"),
                               a_out[:, e].rearrange("p n c b -> p n (c b)")).then_inc(stored[e], 16)

            for n in range(N):
                split_s(0, n)
            split_s(1, 0)
            split_s(1, 1)

            def step(t, splits):
                for e in range(2):
                    for half in range(2):
                        if 2 * e + half < splits:
                            split_s(t + 1 + e, 2 * (1 - e) + half)
                    store(t, e)

            step(0, 4)
            with pool.Fori(1, BT - 2) as t:
                step(t, 4)
            step(BT - 2, 2)
            step(BT - 1, 0)
            for e in range(2):
                pool.wait_ge(stored[e], 16 * BT)

        @block.vector
        def _(dve):
            def split_w(m):
                dve.wait_ge(w_hi_ready, m + 1)
                nc.vector.tensor_tensor(w_lo[:, m, :, :].rearrange("p c d -> p (c d)"), w_raw[:, m % 2, :],
                                        w_hi[:, m, :, :].rearrange("p c d -> p (c d)").bitcast(F32),
                                        ALU.subtract).then_inc(w_split, 1)

            def take_v(t, u, n):
                for e in range(2):
                    dve.wait_ge(v_ready, (t * N + n) * 2 + e + 1)
                    nc.vector.tensor_tensor(v[:, u, e, n, :], vb[n % 2][e][:, :], bias_v[:, e, :],
                                            ALU.add).then_inc(v_taken, 1)

            def mix(t, u, e, n):
                r = (t * 2 + e) * N + n
                slot = n % 2
                if not (isinstance(t, int) and t == 0 and e == 0 and n < 2):
                    dve.wait_ge(o_ready, r - 1)
                if not (isinstance(t, int) and t == 0):
                    dve.wait_ge(turned, (t * 2 + e - 1) * DC)
                prob = power[:, bass.ds(t, 1), n * N * HEADS:(n + 1) * N * HEADS]
                nc.vector.tensor_tensor(
                    prod[:, slot, :, :].rearrange("p m (h d) -> p (m h) d", d=HD),
                    v[:, u, e, :, :].rearrange("p m (h d) -> p (m h) d", d=HD),
                    prob.rearrange("p t x -> p (t x)").unsqueeze(2).to_broadcast([P, N * HEADS, HD]),
                    ALU.mult).then_inc(multiplied, 1)
                dve.wait_ge(multiplied, r + 1)
                nc.vector.tensor_tensor(prod[:, slot, 0:2, :], prod[:, slot, 0:2, :], prod[:, slot, 2:4, :],
                                        ALU.add).then_inc(halved, 1)
                dve.wait_ge(halved, r + 1)
                nc.vector.tensor_tensor(o[:, e, n, :], prod[:, slot, 0, :], prod[:, slot, 1, :],
                                        ALU.add).then_inc(o_ready, 1)

            def split_o(t, e):
                for c in range(DC):
                    dve.wait_ge(ot_hi_ready, (t * 2 + e) * DC + c + 1)
                    nc.vector.tensor_tensor(ot_lo[:, c, :], tr[c % 2][:, :], ot_hi[:, c, :].bitcast(F32),
                                            ALU.subtract).then_inc(ot_split, 1)

            def step(t, u, more):
                dve.wait_ge(v_taken, (t + 1) * N * 2)
                for e in range(2):
                    for n in range(N):
                        mix(t, u, e, n)
                    for n in range(2 * e, 2 * e + 2):
                        if more:
                            take_v(t + 1, 1 - u, n)
                    split_o(t, e)

            split_w(0)
            nc.vector.tensor_scalar(power[:, :, :], power[:, :, :], 1e-8, None, ALU.add).then_inc(soft, 1)
            split_w(1)
            dve.wait_ge(root, 1)
            by_m = power[:, :, :].rearrange("p t (n m h) -> p (t n) h m", n=N, m=N)
            plain = power[:, :, :].rearrange("p t (n m h) -> p (t n) m h", n=N, m=N)
            heads = top[:, :, :, :].rearrange("p t n h -> p (t n) h")
            over_m = heads.unsqueeze(2).to_broadcast([P, BT * N, N, HEADS])
            nc.vector.tensor_reduce(heads, by_m, AX.X, ALU.max).then_inc(soft, 1)
            dve.wait_ge(soft, 2)
            nc.vector.tensor_tensor(plain, plain, over_m, ALU.subtract).then_inc(soft, 1)
            split_w(2)
            dve.wait_ge(exped, 1)
            nc.vector.tensor_reduce(heads, by_m, AX.X, ALU.add).then_inc(soft, 1)
            dve.wait_ge(soft, 4)
            nc.vector.reciprocal(heads, heads).then_inc(soft, 1)
            dve.wait_ge(soft, 5)
            nc.vector.tensor_tensor(plain, plain, over_m, ALU.mult).then_inc(prob_ready, 1)
            split_w(3)
            dve.wait_ge(bias_loaded, 32)
            for n in range(N):
                take_v(0, 0, n)
            dve.wait_ge(prob_ready, 1)
            step(0, 0, True)
            step(1, 1, True)
            with dve.Fori(1, BT // 2 - 1) as i:
                step(i * 2, 0, True)
                step(i * 2 + 1, 1, True)
            step(BT - 2, 0, True)
            step(BT - 1, 1, False)

        @block.tensor
        def _(pe):
            def values(t, n):
                pe.wait_ge(s_split, t * N + n + 1)
                for e in range(2):
                    if first(t, n, 1):
                        pe.wait_ge(w_split, e + 1)
                    if not first(t, n, 2):
                        pe.wait_ge(v_taken, (t * N + n - 2) * 2 + e + 1)
                    for c in range(DC):
                        x = slice(c * P, (c + 1) * P)
                        last = split_product(nc, vb[n % 2][e][:, :], (s_hi[:, n % 2, e, x], s_lo[:, n % 2, e, x]),
                                             (w_hi[:, e, c, :], w_lo[:, e, c, :]), c == 0, c == DC - 1)
                    last.then_inc(v_ready, 1)

            def project(t, e):
                pe.wait_ge(o_ready, (t * 2 + e + 1) * N)
                for c in range(DC):
                    if not (isinstance(t, int) and t == 0 and e == 0 and c < 2):
                        pe.wait_ge(ot_split, (t * 2 + e) * DC + c - 1)
                    for n in range(N):
                        last = nc.tensor.transpose(tr[c % 2][:, n * P:(n + 1) * P],
                                                   o[:, e, n, c * P:(c + 1) * P], ident[:, :])
                    last.then_inc(turned, 1)
                for to in range(DC):
                    if not (isinstance(t, int) and t == 0 and e == 0 and to < 2):
                        pe.wait_ge(out_taken, (t * 2 + e) * DC + to - 1)
                    for c in range(DC):
                        if to == 0:
                            pe.wait_ge(ot_split, (t * 2 + e) * DC + c + 1)
                        cols = slice(to * P, (to + 1) * P)
                        last = split_product(nc, ob[to % 2][:, :], (w_hi[:, 2 + e, c, cols], w_lo[:, 2 + e, c, cols]),
                                             (ot_hi[:, c, :], ot_lo[:, c, :]), c == 0, c == DC - 1)
                    last.then_inc(out_ready, 1)

            def step(t):
                for e in range(2):
                    values(t + 1, 2 * e)
                    values(t + 1, 2 * e + 1)
                    project(t, e)

            for n in range(N):
                values(0, n)
            pe.wait_ge(w_split, MATS)
            step(0)
            with pe.Fori(1, BT - 1) as t:
                step(t)
            for e in range(2):
                project(BT - 1, e)



def mix_states(nc, keep, a_dram, wint, ids, tables, strength, ri_dram):
    SETS = 3
    WR, WI, DIFF, SUM = range(4)
    RAW_OF = (WR, DIFF, SUM)
    PARTS = 3
    PART_OF = (2, 0, 1)
    RING, SPL = 4, 2
    AHEAD = 2
    LAST = N * BT
    with ExitStack() as ctx:
        def sb(name, shape, dt=F32):
            return ctx.enter_context(nc.sbuf_tensor(name, shape, dt))
        w_raw = sb("wint_raw", [P, 4, DC * D])
        w_hi = sb("wint_hi", [P, 2, SETS, DC * D], F32R)
        w_lo = sb("wint_lo", [P, 2, SETS, DC * D], F32R)
        a_raw = sb("a_raw", [P, RING, PARTS, DC * P])
        a_hi = sb("a_hi", [P, SPL, PARTS, DC * P], F32R)
        a_lo = sb("a_lo", [P, SPL, PARTS, DC * P], F32R)
        out = sb("ri_out", [P, RING, 2, D])
        idx = sb("idx", [P, BT, N], I32)
        acc = [[ctx.enter_context(nc.psum_tensor(f"accM{i}{m}", [P, D], F32)) for m in range(SETS)] for i in range(SPL)]
        s = Sems(nc, keep, ctx, "M")
        w_loaded, a_loaded = s.ring("w_loaded", 2), s.ring("a_loaded", RING)
        ids_loaded, gathered = s.dma("ids_loaded"), s.dma("gathered")
        w_combined, w_hi_ready, w_split = s.one("w_combined"), s.one("w_hi_ready"), s.one("w_split")
        a_summed, a_hi_ready, a_split = s.one("a_summed"), s.one("a_hi_ready"), s.one("a_split")
        m1_ready, m2_ready, m3_ready = s.one("m1_ready"), s.one("m2_ready"), s.one("m3_ready")
        m1_taken, r_ready, i_ready = s.one("m1_taken"), s.one("r_ready"), s.one("i_ready")
        stored = s.ring("stored", RING)
        block = s.block()

        @block.sync
        def _(sp):
            def load_w(n):
                for j in range(2):
                    if n:
                        sp.wait_ge(w_split, n * SETS)
                    sp.dma_start(w_raw[:, j, :], wint[n, j]).then_inc(w_loaded[j], 16)

            load_w(0)
            for g in range(LAST):
                if g >= RING:
                    sp.wait_ge(a_split, g - RING + 1)
                sp.dma_start(a_raw[:, g % RING, 0:2, :].rearrange("p e x -> p (e x)"),
                             a_dram[g % BT, g // BT]).then_inc(a_loaded[g % RING], 16)
                if g == 0:
                    sp.dma_start(idx[:, :, :], ids).then_inc(ids_loaded, 16)
                if g % BT == 2 and g // BT < N - 1:
                    load_w(g // BT + 1)

        @block.gpsimd
        def _(pool):
            for g in range(LAST):
                pool.wait_ge(a_loaded[g % RING], (g // RING + 1) * 16)
                nc.gpsimd.tensor_tensor(a_raw[:, g % RING, 2, :], a_raw[:, g % RING, 0, :], a_raw[:, g % RING, 1, :],
                                        ALU.add).then_inc(a_summed, 1)
                if g == 0:
                    pool.wait_ge(ids_loaded, 16)
                t, i = g // N, g % N
                pool.indirect_dma_start(
                    out=strength[:, t, i, :], out_offset=None, in_=tables[i],
                    in_offset=bass.IndirectOffsetOnAxis(ap=idx[:, t, i:i + 1], axis=0)).then_inc(gathered, 16)
            pool.wait_ge(gathered, 16 * BT * N)

        @block.scalar
        def _(act):
            def split_w(n, m):
                if m == 0:
                    act.wait_ge(w_loaded[0], (n + 1) * 16)
                    if n >= 2:
                        act.wait_ge(m3_ready, (n - 1) * BT)
                else:
                    act.wait_ge(w_combined, n * 2 + m)
                nc.scalar.activation(w_hi[:, n % 2, m, :], w_raw[:, RAW_OF[m], :], ACT.Copy).then_inc(w_hi_ready, 1)

            def split_a(g):
                act.wait_ge(a_summed, g + 1)
                if g >= SPL:
                    act.wait_ge(m3_ready, g - SPL + 1)
                nc.scalar.activation(a_hi[:, g % SPL], a_raw[:, g % RING], ACT.Copy).then_inc(a_hi_ready, 1)

            def take(g):
                if g >= RING:
                    act.wait_ge(stored[g % RING], g // RING * 16)
                act.wait_ge(m1_ready, g + 1)
                nc.scalar.activation(out[:, g % RING, 1, :], acc[g % SPL][0][:, :], ACT.Copy).then_inc(m1_taken, 1)

            def store(g):
                act.wait_ge(i_ready, g + 1)
                act.dma_start(ri_dram[g % BT, :, g // BT], out[:, g % RING, :, :].rearrange("p j d -> p (j d)")
                              ).then_inc(stored[g % RING], 16)

            split_w(0, 0)
            split_a(0)
            for m in range(1, SETS):
                split_w(0, m)
            for g in range(1, AHEAD):
                split_a(g)
            for g in range(LAST):
                n, t = g // BT, g % BT
                take(g)
                if g + AHEAD < LAST:
                    split_a(g + AHEAD)
                if g:
                    store(g - 1)
                if n < N - 1 and 3 <= t < 3 + SETS:
                    split_w(n + 1, t - 3)
            store(LAST - 1)
            for slot in range(RING):
                act.wait_ge(stored[slot], 16 * LAST // RING)

        @block.vector
        def _(dve):
            def combine_w(n):
                for j in range(2):
                    dve.wait_ge(w_loaded[j], (n + 1) * 16)
                nc.vector.tensor_tensor(w_raw[:, DIFF, :], w_raw[:, WI, :], w_raw[:, WR, :], ALU.subtract).then_inc(w_combined, 1)
                nc.vector.tensor_tensor(w_raw[:, SUM, :], w_raw[:, WR, :], w_raw[:, WI, :], ALU.add).then_inc(w_combined, 1)

            def split_w(n, m):
                dve.wait_ge(w_hi_ready, n * SETS + m + 1)
                if m:
                    dve.wait_ge(w_combined, n * 2 + m)
                nc.vector.tensor_tensor(w_lo[:, n % 2, m, :], w_raw[:, RAW_OF[m], :], w_hi[:, n % 2, m, :].bitcast(F32),
                                        ALU.subtract).then_inc(w_split, 1)

            def split_a(g):
                dve.wait_ge(a_hi_ready, g + 1)
                nc.vector.tensor_tensor(a_lo[:, g % SPL], a_raw[:, g % RING], a_hi[:, g % SPL].bitcast(F32),
                                        ALU.subtract).then_inc(a_split, 1)

            def take(g):
                dve.wait_ge(m1_taken, g + 1)
                r, i = out[:, g % RING, 0, :], out[:, g % RING, 1, :]
                dve.wait_ge(m3_ready, g + 1)
                nc.vector.tensor_tensor(r, i, acc[g % SPL][2][:, :], ALU.subtract).then_inc(r_ready, 1)
                nc.vector.tensor_tensor(i, i, acc[g % SPL][1][:, :], ALU.add).then_inc(i_ready, 1)

            combine_w(0)
            split_w(0, 0)
            split_a(0)
            for m in range(1, SETS):
                split_w(0, m)
            for g in range(1, AHEAD):
                split_a(g)
            for g in range(LAST):
                n, t = g // BT, g % BT
                take(g)
                if g + AHEAD < LAST:
                    split_a(g + AHEAD)
                if n < N - 1 and t == 2:
                    combine_w(n + 1)
                if n < N - 1 and 3 <= t < 3 + SETS:
                    split_w(n + 1, t - 3)

        @block.tensor
        def _(pe):
            def products(n, u, t, first=False):
                pe.wait_ge(a_split, n * BT + t + 1)
                slot = t % SPL
                for m, (ready, taken) in enumerate(((m1_ready, m1_taken), (m2_ready, i_ready), (m3_ready, r_ready))):
                    if t == 0:
                        pe.wait_ge(w_split, n * SETS + m + 1)
                    if not first:
                        pe.wait_ge(taken, n * BT + t - SPL + 1)
                    for c in range(DC):
                        x, y = slice(c * P, (c + 1) * P), slice(c * D, (c + 1) * D)
                        last = split_product(nc, acc[slot][m][:, :], (a_hi[:, slot, PART_OF[m], x], a_lo[:, slot, PART_OF[m], x]),
                                             (w_hi[:, u, m, y], w_lo[:, u, m, y]), c == 0, c == DC - 1)
                    last.then_inc(ready, 1)

            for t in range(BT):
                products(0, 0, t, t < SPL)
            with pe.Fori(0, N // 2 - 1) as i:
                for u in range(2):
                    for t in range(BT):
                        products(i * 2 + 1 + u, 1 - u, t)
            for t in range(BT):
                products(N - 1, 1, t)
        return gathered


def superpose(nc, keep, strength, gathered, ri_dram, ident, sup_t):
    PAIRS = [(n, n + gap) for gap in range(1, N) for n in range(N - gap)]
    NP = len(PAIRS)
    ORDER = [pair if q == 0 else pair[::-1] for q, pair in enumerate(PAIRS)]
    COMPLETE = [[m for m in pair if not any(m in later for later in ORDER[q + 1:])] for q, pair in enumerate(ORDER)]
    DONE = [m for states in COMPLETE for m in states]
    SLOTS, AHEAD = 3, 3
    CB = 4
    UNROLL = 2
    GAINS = 2 * NP
    with ExitStack() as ctx:
        def sb(name, shape, dt=F32):
            return ctx.enter_context(nc.sbuf_tensor(name, shape, dt))
        ri = sb("ri_rows", [P, UNROLL, N, 2, D])
        squares = sb("squaresD", [P, N, 2, D])
        size = sb("size", [P, UNROLL, N, D])
        zero = sb("zero", [P, N, D], F32R)
        uv = sb("uv", [P, N, 2, D])
        prod = sb("pair_products", [P, SLOTS, 2, D])
        gain = sb("gain", [P, N, D])
        term = sb("terms", [P, N, 2, D])
        sup = sb("sup", [P, 2, D])
        norm = sb("norm", [P, BT, 3])
        eps = sb("eps", [P, 1])
        ident_r = sb("ident_r", [P, P], F32R)
        side = [ctx.enter_context(nc.psum_tensor(f"sideD{i}", [P, D], F32)) for i in range(2)]
        cos = [ctx.enter_context(nc.psum_tensor(f"cosD{i}", [P, D], F32)) for i in range(CB)]
        total = ctx.enter_context(nc.psum_tensor("totalD", [P, 2, D], F32))
        s = Sems(nc, keep, ctx, "D")
        loaded = s.ring("loaded", UNROLL)
        constants, eps_ready = s.one("constants"), s.one("eps_ready")
        squared, sized, rooted = s.one("squared"), s.one("sized"), s.one("rooted")
        zeroed, lifted, inverted, directed = s.one("zeroed"), s.one("lifted"), s.one("inverted"), s.one("directed")
        multiplied, cos_ready, gained = s.one("multiplied"), s.one("cos_ready"), s.one("gained")
        term_ready, summed = s.one("term_ready"), s.one("summed")
        length, scale_ready, normed = s.one("length"), s.one("scale_ready"), s.one("normed")
        turned, copied = s.one("turned"), s.one("copied")
        block = s.block()

        @block.sync
        def _(sp):
            def load(t, u, first):
                if not first:
                    sp.wait_ge(term_ready, (t - 1) * N)
                sp.dma_start(ri[:, u].rearrange("p n j d -> p (n j d)"),
                             ri_dram[t].rearrange("p n x -> p (n x)")).then_inc(loaded[u], 16)

            for u in range(UNROLL):
                load(u, u, True)
            with sp.Fori(1, BT // UNROLL) as i:
                for u in range(UNROLL):
                    load(i * UNROLL + u, u, False)

        @block.scalar
        def _(act):
            def square(t):
                act.wait_ge(loaded[t % UNROLL], (t // UNROLL + 1) * 16)
                if t:
                    act.wait_ge(sized, t * N)
                nc.scalar.activation(squares[:, :, :, :], ri[:, t % UNROLL], ACT.Square).then_inc(squared, 1)

            def root(t):
                for n in range(N):
                    act.wait_ge(sized, t * N + n + 1)
                    if t >= UNROLL and n == 0:
                        act.wait_ge(directed, t - UNROLL + 1)
                    nc.scalar.activation(size[:, t % UNROLL, n, :], side[n % 2][:, :], ACT.Sqrt).then_inc(rooted, 1)

            def measure(t):
                act.wait_ge(summed, (t + 1) * 2)
                if t:
                    act.wait_ge(turned, t * 2)
                nc.scalar.activation(sup[:, :, :], total[:, :, :], ACT.Square, accum_out=norm[:, t, 0:1]).then_inc(length, 1)
                act.wait_ge(length, t * 2 + 1)
                nc.scalar.activation(norm[:, t, 1:2], norm[:, t, 0:1], ACT.Sqrt, bias=eps[:, :]).then_inc(length, 1)

            def normalise(t):
                act.wait_ge(scale_ready, t + 1)
                nc.scalar.activation(sup[:, :, :], total[:, :, :], ACT.Copy, scale=norm[:, t, 2:3]).then_inc(normed, 1)

            def copy(t):
                for j in range(2):
                    act.wait_ge(turned, t * 2 + j + 1)
                    nc.scalar.activation(sup_t[:, j, :, t * P:(t + 1) * P],
                                         side[j][:, :].rearrange("p (c b) -> p c b", b=P), ACT.Copy).then_inc(copied, 1)

            nc.scalar.activation(ident_r[:, :], ident[:, :], ACT.Copy).then_inc(constants, 1)
            act.wait_ge(eps_ready, 1)
            square(0)
            root(0)
            for t in range(BT + 1):
                if t + 1 < BT:
                    square(t + 1)
                    root(t + 1)
                if t:
                    measure(t - 1)
                    normalise(t - 1)
                    copy(t - 1)

        @block.tensor
        def _(pe):
            def sizes(t, last_there):
                pe.wait_ge(squared, t + 1)
                for n in range(N):
                    if n >= 2:
                        pe.wait_ge(rooted, t * N + n - 1)
                    elif last_there == "size":
                        pe.wait_ge(rooted, (t - 1) * N + n + 3)
                    elif last_there == "turned":
                        pe.wait_ge(copied, (t - 3) * 2 + n + 1)
                    nc.tensor.matmul(side[n % 2][:, :], ident[:, :], squares[:, n, 0, :], start=True, stop=False)
                    nc.tensor.matmul(side[n % 2][:, :], ident[:, :], squares[:, n, 1, :],
                                     start=False, stop=True).then_inc(sized, 1)

            def cosines(t, u, first):
                for q, (i, j) in enumerate(PAIRS):
                    g = u * NP + q
                    bank = cos[g % CB][:, :]
                    pe.wait_ge(multiplied, t * NP + q + 1)
                    if not (first and q < CB):
                        pe.wait_ge(gained, (t * NP + q - CB + 1) * 2)
                    for part in range(2):
                        nc.tensor.matmul(bank, ident[:, :], prod[:, g % SLOTS, part, :], start=part == 0, stop=False)
                    nc.tensor.matmul(bank, ident_r[:, :], zero[:, i, :], start=False, stop=False)
                    nc.tensor.matmul(bank, ident_r[:, :], zero[:, j, :], start=False, stop=True).then_inc(cos_ready, 1)

            def turn(t, sizes_done):
                pe.wait_ge(normed, t + 1)
                pe.wait_ge(rooted, sizes_done * N)
                for j in range(2):
                    for c in range(DC):
                        last = nc.tensor.transpose(side[j][:, c * P:(c + 1) * P], sup[:, j, c * P:(c + 1) * P],
                                                   ident[:, :])
                    last.then_inc(turned, 1)

            def add_terms(t, first):
                if not first:
                    pe.wait_ge(normed, t)
                for n in range(N):
                    pe.wait_ge(term_ready, t * N + n + 1)
                    for j in range(2):
                        last = nc.tensor.matmul(total[:, j, :], ident[:, :], term[:, DONE[n], j, :],
                                                start=n == 0, stop=n == N - 1)
                        if n == N - 1:
                            last.then_inc(summed, 1)

            def step(t, u):
                sizes(t + 1, "turned")
                cosines(t, u, False)
                turn(t - 1, t + 2)
                add_terms(t, False)

            pe.wait_ge(constants, 1)
            sizes(0, None)
            sizes(1, "size")
            cosines(0, 0, True)
            add_terms(0, True)
            sizes(2, "size")
            cosines(1, 1, False)
            turn(0, 3)
            add_terms(1, False)
            with pe.Fori(1, BT // UNROLL - 1) as i:
                for u in range(UNROLL):
                    step(i * UNROLL + u, u)
            step(BT - 2, 0)
            cosines(BT - 1, 1, False)
            turn(BT - 2, BT)
            add_terms(BT - 1, False)
            turn(BT - 1, BT)

        @block.vector
        def _(dve):
            def directions(t, u):
                here = size[:, u, :, :]
                dve.wait_ge(rooted, (t + 1) * N)
                nc.vector.tensor_scalar(zero[:, :, :], here, 0.0, None, ALU.is_equal).then_inc(zeroed, 1)
                nc.vector.tensor_scalar(here, here, 1e-30, None, ALU.max).then_inc(lifted, 1)
                dve.wait_ge(lifted, t + 1)
                nc.vector.reciprocal(here, here).then_inc(inverted, 1)
                dve.wait_ge(inverted, t + 1)
                nc.vector.tensor_tensor(uv[:, :, :, :], ri[:, u], here.unsqueeze(2).to_broadcast([P, N, 2, D]),
                                        ALU.mult).then_inc(directed, 1)

            def scale(t):
                dve.wait_ge(length, t * 2 + 2)
                nc.vector.reciprocal(norm[:, bass.ds(t, 1), 2:3], norm[:, bass.ds(t, 1), 1:2]).then_inc(scale_ready, 1)

            def multiply(t, u, q):
                i, j = PAIRS[q]
                nc.vector.tensor_tensor(prod[:, (u * NP + q) % SLOTS], uv[:, i], uv[:, j], ALU.mult).then_inc(multiplied, 1)

            def strengths(t, i, m):
                return strength[:, bass.ds(t, 1), i, m:m + 1].rearrange("p t x -> p (t x)")

            def collect(t, u, q):
                dve.wait_ge(cos_ready, t * NP + q + 1)
                for m in ORDER[q]:
                    i = sum(PAIRS[q]) - m
                    bank = cos[(u * NP + q) % CB][:, :]
                    k = last_gain.get(m)
                    if k is None:
                        ins = nc.vector.tensor_scalar(gain[:, m, :], bank, strengths(t, i, m), strengths(t, m, m),
                                                      ALU.mult, ALU.add)
                    else:
                        dve.wait_ge(gained, t * GAINS + k)
                        ins = nc.vector.scalar_tensor_tensor(gain[:, m, :], bank, strengths(t, i, m), gain[:, m, :],
                                                             ALU.mult, ALU.add)
                    ins.then_inc(gained, 1)
                    last_gain[m] = last_gain["count"] = last_gain["count"] + 1

            def step(t, u, first=False):
                directions(t, u)
                dve.wait_ge(directed, t + 1)
                last_gain.clear()
                last_gain["count"] = 0
                for q in range(AHEAD):
                    multiply(t, u, q)
                if not first:
                    scale(t - 1)
                for q in range(NP):
                    collect(t, u, q)
                    if q + AHEAD < NP:
                        multiply(t, u, q + AHEAD)
                    for m in COMPLETE[q]:
                        dve.wait_ge(gained, t * GAINS + last_gain[m])
                        nc.vector.tensor_tensor(term[:, m], ri[:, u, m], gain[:, m:m + 1, :].to_broadcast([P, 2, D]),
                                                ALU.mult).then_inc(term_ready, 1)

            last_gain = {}
            nc.vector.memset(eps[:, :], 1e-8).then_inc(eps_ready, 1)
            dve.wait_ge(gathered, 16 * BT * N)
            step(0, 0, True)
            with dve.Fori(0, BT // UNROLL - 1) as i:
                step(i * UNROLL + 1, 1)
                step(i * UNROLL + 2, 0)
            step(BT - 1, 1)
            scale(BT - 1)


def measure_and_top(nc, keep, sup_t, h_dram, wm, wpost, wz, w2, w3, b_post, b_top2, norm_post, ident, out):
    HALF = B // 2
    HT = BT // 2
    F2 = 256 // P
    with ExitStack() as ctx:
        def sb(name, shape, dt=F32):
            return ctx.enter_context(nc.sbuf_tensor(name, shape, dt))
        m_w = sb("meas_w", [P, 3, DC * OUT])
        post_w = sb("post_w", [P, DC * OUT])
        z_w = sb("top1_w", [P, DC * CH])
        w2_sb = sb("top2_w", [P, DC * F2 * P])
        w3_sb = sb("top3_w", [P, F2])
        post_b = sb("post_b", [P, OUT])
        par = sb("post_norm", [P, 2, DC])
        b2_sb = sb("top2_b", [P, F2])
        squares = sb("squares", [P, 2, 2, HALF])
        amp = sb("amp", [P, DC, B])
        z = sb("z_rows", [P, BT, OUT])
        r1 = sb("top1_rows", [P, BT, CH])
        r2 = sb("top2_t", [P, F2, B])
        stats = sb("post_stats", [P, BT, 6])
        mv = sb("post_mv", [P, BT, 2])
        rstd = sb("post_rstd", [P, 3, BT])
        y = sb("y_row", [P, B])
        z_t, r1_t = sup_t[:, 0], sup_t[:, 1]
        acc = [ctx.enter_context(nc.psum_tensor(f"accT{i}", [P, HALF], F32)) for i in range(6)]
        tr = [ctx.enter_context(nc.psum_tensor(f"turnT{i}", [P, HALF], F32)) for i in range(2)]
        s = Sems(nc, keep, ctx, "T")
        loaded = s.ring("loaded", 8)
        negated, measured, squared, summed, amp_ready = (
            s.one(x) for x in ("negated", "measured", "squared", "summed", "amp_ready"))
        posted, z_ready, stats_ready, std_ready, mv_ready, normed = (
            s.one(x) for x in ("posted", "z_ready", "stats_ready", "std_ready", "mv_ready", "normed"))
        turned, z_t_ready, top1_done, r1_ready = (
            s.one(x) for x in ("turned", "z_t_ready", "top1_done", "r1_ready"))
        r1_turned, r1_t_ready, top2_done, r2_ready, top3_done, y_ready = (
            s.one(x) for x in ("r1_turned", "r1_t_ready", "top2_done", "r2_ready", "top3_done", "y_ready"))
        stored = s.dma("stored")
        LOADS = ((m_w[:, 0:2, :], wm), (post_w[:, :], wpost), (post_b[:, :], b_post.to_broadcast([P, OUT])),
                 (par[:, :, :], norm_post), (z_w[:, :], wz), (r1[:, :, :], h_dram[NCH - 1].rearrange("t p f -> p t f")),
                 (w2_sb[:, :], w2), (b2_sb[:, :], b_top2))
        M_W, POST_W, POST_B, PAR, Z_W, X_PART, W2, B2 = range(8)
        block = s.block()

        @block.sync
        def _(sp):
            for i, (to, what) in enumerate(LOADS):
                sp.dma_start(to, what).then_inc(loaded[i], 16)
            sp.dma_start(w3_sb[:, :], w3).then_inc(loaded[W2], 16)
            sp.wait_ge(y_ready, 2)
            sp.dma_start(out, y[0:1, :]).then_inc(stored, 16)
            sp.wait_ge(stored, 16)

        @block.scalar
        def _(act):
            act.wait_ge(loaded[M_W], 16)
            nc.scalar.activation(m_w[:, 2, :], m_w[:, 1, :], ACT.Copy, scale=-1.0).then_inc(negated, 1)
            for half in range(2):
                for c in range(DC):
                    i = half * DC + c
                    for j in range(2):
                        act.wait_ge(measured, 2 * i + j + 1)
                        if i >= 2:
                            act.wait_ge(summed, i - 1)
                        nc.scalar.activation(squares[:, i % 2, j, :], acc[2 * (i % 2) + j][:, :],
                                             ACT.Square).then_inc(squared, 1)
                    act.wait_ge(summed, i + 1)
                    nc.scalar.activation(amp[:, c, half * HALF:(half + 1) * HALF], squares[:, i % 2, 0, :],
                                         ACT.Sqrt).then_inc(amp_ready, 1)
            act.wait_ge(stats_ready, BT + 2)
            nc.scalar.activation(rstd[:, 0, :], rstd[:, 1, :], ACT.Sqrt).then_inc(std_ready, 1)
            act.wait_ge(loaded[PAR], 16)
            for half in range(2):
                for c in range(DC):
                    i = half * DC + c
                    act.wait_ge(turned, i + 1)
                    nc.scalar.activation(z_t[:, c, half * HALF:(half + 1) * HALF], tr[i % 2][:, :], ACT.Gelu,
                                         bias=par[:, 1, c:c + 1], scale=par[:, 0, c:c + 1]).then_inc(z_t_ready, 1)
            for half in range(2):
                for c in range(DC):
                    i = half * DC + c
                    act.wait_ge(r1_turned, i + 1)
                    nc.scalar.activation(r1_t[:, c, half * HALF:(half + 1) * HALF], tr[i % 2][:, :],
                                         ACT.Copy).then_inc(r1_t_ready, 1)
            act.wait_ge(loaded[B2], 16)
            for half in range(2):
                for f in range(F2):
                    act.wait_ge(top2_done, half * F2 + f + 1)
                    nc.scalar.activation(r2[:, f, half * HALF:(half + 1) * HALF], acc[f][:, :], ACT.Relu,
                                         bias=b2_sb[:, f:f + 1]).then_inc(r2_ready, 1)

        @block.vector
        def _(dve):
            for i in range(2 * DC):
                dve.wait_ge(squared, 2 * i + 2)
                nc.vector.tensor_tensor(squares[:, i % 2, 0, :], squares[:, i % 2, 0, :], squares[:, i % 2, 1, :],
                                        ALU.add).then_inc(summed, 1)
            dve.wait_ge(loaded[POST_B], 16)
            for t in range(BT):
                dve.wait_ge(posted, t + 1)
                nc.vector.tensor_tensor(z[:, t, :], acc[t % 6][:, :], post_b[:, :], ALU.add).then_inc(z_ready, 1)
                dve.wait_ge(z_ready, t + 1)
                nc.vector.bn_stats(stats[:, t, :], z[:, t, :]).then_inc(stats_ready, 1)
            dve.wait_ge(stats_ready, BT)
            for t in range(BT):
                last = nc.vector.bn_aggr(mv[:, t, :], stats[:, t, :])
            last.then_inc(stats_ready, 1)
            dve.wait_ge(stats_ready, BT + 1)
            nc.vector.tensor_scalar(rstd[:, 1, :], mv[:, :, 1], LN_EPS, None, ALU.add).then_inc(stats_ready, 1)
            dve.wait_ge(std_ready, 1)
            nc.vector.reciprocal(rstd[:, 2, :], rstd[:, 0, :]).then_inc(mv_ready, 1)
            dve.wait_ge(mv_ready, 1)
            for t in range(BT):
                nc.vector.tensor_scalar(z[:, t, :], z[:, t, :], mv[:, t, 0:1], rstd[:, 2, t:t + 1],
                                        ALU.subtract, ALU.mult).then_inc(normed, 1)
            dve.wait_ge(loaded[X_PART], 16)
            for t in range(BT):
                dve.wait_ge(top1_done, t + 1)
                nc.vector.tensor_tensor(r1[:, t, :], acc[t % 6][:, :], r1[:, t, :], ALU.add).then_inc(r1_ready, 1)
                dve.wait_ge(r1_ready, 2 * t + 1)
                nc.vector.tensor_scalar(r1[:, t, :], r1[:, t, :], 0.0, None, ALU.max).then_inc(r1_ready, 1)
            for half in range(2):
                dve.wait_ge(top3_done, half + 1)
                nc.vector.tensor_copy(y[0:1, half * HALF:(half + 1) * HALF], acc[4 + half][0:1, :]).then_inc(y_ready, 1)

        @block.tensor
        def _(pe):
            pe.wait_ge(loaded[M_W], 16)
            pe.wait_ge(negated, 1)
            for half in range(2):
                cols = slice(half * HALF, (half + 1) * HALF)
                for c in range(DC):
                    i = half * DC + c
                    if i >= 2:
                        pe.wait_ge(squared, 2 * (i - 1))
                    for j in range(2):
                        for e in range(2):
                            which = ((0, 2), (1, 0))[j][e]
                            for k in range(DC):
                                last = nc.tensor.matmul(
                                    acc[2 * (i % 2) + j][:, :], m_w[:, which, k * OUT + c * P:k * OUT + (c + 1) * P],
                                    sup_t[:, e, k, cols], start=e == 0 and k == 0, stop=e == 1 and k == DC - 1)
                        last.then_inc(measured, 1)
            pe.wait_ge(loaded[POST_W], 16)
            pe.wait_ge(squared, 4 * DC)
            for t in range(BT):
                pe.wait_ge(amp_ready, (t // HT + 1) * DC)
                if t >= 6:
                    pe.wait_ge(z_ready, t - 5)
                for k in range(DC):
                    last = nc.tensor.matmul(acc[t % 6][:, :], amp[:, k, t * P:(t + 1) * P],
                                            post_w[:, k * OUT:(k + 1) * OUT], start=k == 0, stop=k == DC - 1)
                last.then_inc(posted, 1)
            for half in range(2):
                pe.wait_ge(normed, (half + 1) * HT)
                for c in range(DC):
                    i = half * DC + c
                    if i >= 2:
                        pe.wait_ge(z_t_ready, i - 1)
                    for t in range(HT):
                        last = nc.tensor.transpose(tr[i % 2][:, t * P:(t + 1) * P],
                                                   z[:, half * HT + t, c * P:(c + 1) * P], ident[:, :])
                    last.then_inc(turned, 1)
            pe.wait_ge(loaded[Z_W], 16)
            pe.wait_ge(z_ready, BT)
            for t in range(BT):
                pe.wait_ge(z_t_ready, (t // HT + 1) * DC)
                if t >= 6:
                    pe.wait_ge(r1_ready, 2 * (t - 6) + 1)
                for k in range(DC):
                    last = nc.tensor.matmul(acc[t % 6][:, :], z_t[:, k, t * P:(t + 1) * P],
                                            z_w[:, k * CH:(k + 1) * CH], start=k == 0, stop=k == DC - 1)
                last.then_inc(top1_done, 1)
            for half in range(2):
                pe.wait_ge(r1_ready, 2 * (half + 1) * HT)
                for c in range(DC):
                    i = half * DC + c
                    pe.wait_ge(r1_t_ready, i - 1) if i >= 2 else pe.wait_ge(z_t_ready, 2 * DC)
                    for t in range(HT):
                        last = nc.tensor.transpose(tr[i % 2][:, t * P:(t + 1) * P],
                                                   r1[:, half * HT + t, c * P:(c + 1) * P], ident[:, :])
                    last.then_inc(r1_turned, 1)
            pe.wait_ge(loaded[W2], 32)
            for half in range(2):
                cols = slice(half * HALF, (half + 1) * HALF)
                pe.wait_ge(r1_t_ready, (half + 1) * DC)
                if half:
                    pe.wait_ge(r2_ready, F2)
                for f in range(F2):
                    for k in range(DC):
                        at = (k * F2 + f) * P
                        last = nc.tensor.matmul(acc[f][:, :], w2_sb[:, at:at + P], r1_t[:, k, cols],
                                                start=k == 0, stop=k == DC - 1)
                    last.then_inc(top2_done, 1)
            for half in range(2):
                pe.wait_ge(r2_ready, (half + 1) * F2)
                for f in range(F2):
                    last = nc.tensor.matmul(acc[4 + half][0:1, :], w3_sb[:, f:f + 1],
                                            r2[:, f, half * HALF:(half + 1) * HALF], start=f == 0, stop=f == F2 - 1)
                last.then_inc(top3_done, 1)


def build(nc, a, out):
    h_dram = nc.dram_tensor("h_rows", [NCH, BT, P, CH], F32, kind="Internal").ap()
    s_dram = nc.dram_tensor("s_feats", [BT, N, P, 2, DC, P], F32, kind="Internal").ap()
    a_dram = nc.dram_tensor("attn_feats", [BT, N, P, 2, DC, P], F32, kind="Internal").ap()
    ri_dram = nc.dram_tensor("ri_states", [BT, P, N, 2 * D], F32, kind="Internal").ap()
    s_flat = s_dram.rearrange("t n p e c b -> t n p (e c b)")
    a_flat = a_dram.rearrange("t n p e c b -> t n p (e c b)")
    with ExitStack() as keep:
        ident = keep.enter_context(nc.sbuf_tensor("ident", [P, P], F32))
        ident_ready = keep.enter_context(nc.semaphore("ident_ready"))
        with nc.Block(no_gpsimd_drain=True) as block:
            @block.sync
            def _(sp):
                sp.dma_start(ident[:, :], a["ident"]).then_inc(ident_ready, 16)
                sp.wait_ge(ident_ready, 16)
        with nc.sbuf_tensor("h_stats", [P, NCH, BT, 6], F32) as stats:
            products_with_x(nc, keep, a["xT"], a["wA"], a["bA"], h_dram, stats)
            for e in range(2):
                second_products(nc, keep, e, h_dram, a["w2"], a["b2"], a["norm2"], stats, ident, s_dram)
        with nc.sbuf_tensor("power", [P, BT, N * N * HEADS], F32) as power:
            scores(nc, keep, s_flat, a["wqk"], a["bqk"], power)
            mix_values(nc, keep, power, s_flat, a["wvo"], a["bv"], a["bo"], ident, a_dram)
        with nc.sbuf_tensor("strength", [P, BT, N, N], F32) as strength:
            gathered = mix_states(nc, keep, a_flat, a["wint"], a["ids"], [a[f"tbl_{i}"] for i in range(N)],
                                  strength, ri_dram)
            with nc.sbuf_tensor("sup_t", [P, 2, DC, B], F32) as sup_t:
                superpose(nc, keep, strength, gathered, ri_dram, ident, sup_t)
                measure_and_top(nc, keep, sup_t, h_dram, a["wm"], a["wpost"], a["wz"], a["wt2"], a["wt3"],
                                a["b_post"], a["b_top2"], a["norm_post"], ident, out)


def kernel(**inputs):
    import numpy as np
    import concourse.bacc as bacc
    from concourse.bass_utils import run_bass_kernel_spmd

    x = {k.removeprefix("L0_rec_"): np.asarray(v) for k, v in inputs.items()}

    def moving(*names):
        return np.stack([x[n].T.reshape(DC, P, -1).transpose(1, 0, 2).reshape(P, -1) for n in names])

    def columns(a):
        return a.reshape(-1, P).T

    w1 = np.concatenate([x["er_W1"].T, x["ei_W1"].T, x["W_top1"][OUT:]], axis=1)
    arrays = {
        "xT": x["r_x"].T.reshape(KT, P, B),
        "wA": w1.reshape(KT // 2, 2, P, NCH, CH).transpose(3, 0, 2, 1, 4).reshape(NCH, KT // 2, P, 2 * CH),
        "bA": np.concatenate([x["er_b1"], x["ei_b1"], x["b_top1"]])[None],
        "w2": np.stack([x[e + "_W2"].reshape(N, DC, P, 4, 4, P).transpose(0, 1, 3, 5, 4, 2).reshape(N, DC, 4, P, 4 * P)
                        for e in ("er", "ei")]),
        "b2": np.stack([columns(x[e + "_b2"]) for e in ("er", "ei")]),
        "norm2": np.stack([np.stack([columns(x[e + "_g1"]), columns(x[e + "_be1"])], axis=1) for e in ("er", "ei")]),
        "wqk": moving("Wq_r", "Wq_i", "Wk_r", "Wk_i"),
        "bqk": np.stack([x["bq_r"], x["bq_i"], x["bk_r"], x["bk_i"]])[None],
        "wvo": moving("Wv_r", "Wv_i", "Wo_r", "Wo_i"),
        "bv": np.stack([x["bv_r"], x["bv_i"]])[None],
        "bo": np.stack([columns(x["bo_r"]), columns(x["bo_i"])], axis=1),
        "wint": np.stack([x["int_Wr"], x["int_Wi"]], axis=1).transpose(0, 1, 3, 2)
                .reshape(N, 2, DC, P, D).transpose(0, 1, 3, 2, 4).reshape(N, 2, P, DC * D),
        "ids": x["ids"].reshape(BT, P, N).transpose(1, 0, 2),
        "tbl_0": x["tbl_0"], "tbl_1": x["tbl_1"], "tbl_2": x["tbl_2"], "tbl_3": x["tbl_3"],
        "wm": moving("meas_Mr", "meas_Mi").transpose(1, 0, 2),
        "wpost": moving("post_W")[0],
        "wz": x["W_top1"][:OUT].reshape(DC, P, CH).transpose(1, 0, 2).reshape(P, -1),
        "wt2": x["W_top2"].reshape(DC, P, 256).transpose(1, 0, 2).reshape(P, -1),
        "wt3": columns(x["W_top3"][:, 0]),
        "b_post": x["post_b"][None],
        "b_top2": columns(x["b_top2"]),
        "norm_post": np.stack([columns(x["post_g"]), columns(x["post_be"])], axis=1),
        "ident": np.eye(P, dtype=np.float32),
    }
    nc = bacc.Bacc("TRN2", target_bir_lowering=False, num_devices=1)
    arrays = {f"in_{k}": np.ascontiguousarray(v) for k, v in arrays.items()}
    aps = {k[3:]: nc.dram_tensor(k, v.shape, mybir.dt.from_np(v.dtype), kind="ExternalInput").ap()
           for k, v in arrays.items()}
    y = nc.dram_tensor("y", (B, 1), F32, kind="ExternalOutput").ap()
    build(nc, aps, y.rearrange("b one -> one b"))
    r = run_bass_kernel_spmd(nc, [arrays], core_ids=[0])
    return r.results[0]["y"]
```

```python
import concourse.bass as bass
from concourse import mybir
from contextlib import ExitStack

F32 = mybir.dt.float32
F32R = mybir.dt.float32r
I32 = mybir.dt.int32
ALU = mybir.AluOpType
ACT = mybir.ActivationFunctionType
AX = mybir.AxisListType

P = 128
B = 1024
BT = B // P
IN = 2048
HID = 2048
D = 512
N = 4
HEADS = 8
HD = D // HEADS
OUT = 512
KT = IN // P
DC = D // P
CH = 512
NCH = 2 * HID // CH + 1
ECH = HID // CH
LN_EPS = 1e-5


def split_product(nc, out, stat, move, start, stop):
    (sh, sl), (mh, ml) = stat, move
    nc.tensor.matmul(out, sh, mh, start=start, stop=False)
    nc.tensor.matmul(out, sh, ml, start=False, stop=False)
    return nc.tensor.matmul(out, sl, mh, start=False, stop=stop)


class Sems:

    def __init__(self, nc, keep, ctx, phase):
        self.nc, self.keep, self.ctx, self.phase, self.engines_own = nc, keep, ctx, phase, []

    def one(self, name):
        self.engines_own.append(self.ctx.enter_context(self.nc.semaphore(f"{self.phase}_{name}")))
        return self.engines_own[-1]

    def dma(self, name):
        return self.keep.enter_context(self.nc.semaphore(f"{self.phase}_{name}"))

    def ring(self, name, n):
        return [self.dma(f"{name}{i}") for i in range(n)]

    def block(self):
        self.ctx.callback(self.clear)
        return self.ctx.enter_context(self.nc.Block(no_gpsimd_drain=True))

    def clear(self):
        with self.nc.Block(no_gpsimd_drain=True) as block:
            @block.sync
            def _(sp):
                for sem in self.engines_own:
                    sp.sem_clear(sem)


def products_with_x(nc, keep, xT, wA, bA, h_dram, stats):
    PAIR, PAIRS = 2, KT // 2
    RAW, SPL, XRAW, HO = 4, 2, 2, BT
    AHEAD = 1
    with ExitStack() as ctx:
        def sb(name, shape, dt=F32):
            return ctx.enter_context(nc.sbuf_tensor(name, shape, dt))
        x_raw = sb("x_raw", [P, XRAW, B])
        x_hi = sb("x_hi", [P, KT, B], F32R)
        x_lo = sb("x_lo", [P, KT, B], F32R)
        w_raw = sb("wA_raw", [P, RAW, PAIR * CH])
        w_hi = sb("wA_hi", [P, SPL, PAIR * CH], F32R)
        w_lo = sb("wA_lo", [P, SPL, PAIR * CH], F32R)
        bias = sb("bA_all", [P, NCH * CH])
        h_out = sb("h_out", [P, HO, CH])
        acc = [ctx.enter_context(nc.psum_tensor(f"accA{t}", [P, CH], F32)) for t in range(BT)]
        s = Sems(nc, keep, ctx, "A")
        x_loaded = s.ring("x_loaded", XRAW)
        w_loaded = s.ring("w_loaded", RAW)
        bias_loaded = s.dma("bias_loaded")
        x_hi_ready, x_split = s.one("x_hi_ready"), s.one("x_split")
        w_hi_ready, w_split = s.one("w_hi_ready"), s.one("w_split")
        w_used = s.one("w_used")
        acc_ready, acc_taken = s.one("acc_ready"), s.one("acc_taken")
        stats_done = s.one("stats_done")
        h_stored = s.ring("h_stored", HO)
        block = s.block()

        @block.sync
        def _(sp):
            def load_w(c, j):
                if not (isinstance(c, int) and c * PAIRS + j < RAW):
                    sp.wait_ge(w_split, c * PAIRS + j - RAW + 1)
                sp.dma_start(w_raw[:, j % RAW, :], wA[c, j]).then_inc(w_loaded[j % RAW], 16)

            for j in range(PAIRS):
                for k in range(PAIR * j, PAIR * j + PAIR):
                    if k >= XRAW:
                        sp.wait_ge(x_split, k - XRAW + 1)
                    sp.dma_start(x_raw[:, k % XRAW, :], xT[k]).then_inc(x_loaded[k % XRAW], 16)
                load_w(0, j)
            sp.dma_start(bias[:, :], bA.to_broadcast([P, NCH * CH])).then_inc(bias_loaded, 16)
            with sp.Fori(1, NCH) as c:
                for j in range(PAIRS):
                    load_w(c, j)

        @block.scalar
        def _(act):
            def split_w(c, j):
                act.wait_ge(w_loaded[j % RAW], (c * (PAIRS // RAW) + j // RAW + 1) * 16)
                if j >= SPL:
                    act.wait_ge(w_used, c * (PAIRS - 1) + j - SPL + 1)
                elif not (isinstance(c, int) and c == 0):
                    if j == SPL - 1:
                        act.wait_ge(acc_ready, c * BT)
                    else:
                        act.wait_ge(w_used, c * (PAIRS - 1) + j - SPL + 2)
                nc.scalar.activation(w_hi[:, j % SPL, :], w_raw[:, j % RAW, :], ACT.Copy).then_inc(w_hi_ready, 1)

            for j in range(PAIRS):
                for k in range(PAIR * j, PAIR * j + PAIR):
                    act.wait_ge(x_loaded[k % XRAW], (k // XRAW + 1) * 16)
                    nc.scalar.activation(x_hi[:, k, :], x_raw[:, k % XRAW, :], ACT.Copy).then_inc(x_hi_ready, 1)
                split_w(0, j)
            with act.Fori(1, NCH) as c:
                for j in range(PAIRS):
                    split_w(c, j)

        @block.vector
        def _(dve):
            def split_w(c, j):
                dve.wait_ge(w_hi_ready, c * PAIRS + j + 1)
                nc.vector.tensor_tensor(w_lo[:, j % SPL, :], w_raw[:, j % RAW, :],
                                        w_hi[:, j % SPL, :].bitcast(F32), ALU.subtract).then_inc(w_split, 1)

            def take(c):
                for t in range(BT):
                    dve.wait_ge(acc_ready, c * BT + t + 1)
                    if not (isinstance(c, int) and c == 0):
                        dve.wait_ge(h_stored[t], c * 16)
                    nc.vector.tensor_tensor(h_out[:, t, :], acc[t][:, :], bias[:, bass.ts(c, CH)],
                                            ALU.add).then_inc(acc_taken, 1)
                for t in range(BT):
                    dve.wait_ge(acc_taken, c * BT + t + 1)
                    nc.vector.bn_stats(stats[:, c, t, :], h_out[:, t, :]).then_inc(stats_done, 1)

            for j in range(PAIRS):
                for k in range(PAIR * j, PAIR * j + PAIR):
                    dve.wait_ge(x_hi_ready, k + 1)
                    nc.vector.tensor_tensor(x_lo[:, k, :], x_raw[:, k % XRAW, :],
                                            x_hi[:, k, :].bitcast(F32), ALU.subtract).then_inc(x_split, 1)
                split_w(0, j)
            for j in range(AHEAD):
                split_w(1, j)
            dve.wait_ge(bias_loaded, 16)
            take(0)
            for j in range(AHEAD, PAIRS):
                split_w(1, j)
            with dve.Fori(2, NCH) as c:
                for j in range(AHEAD):
                    split_w(c, j)
                take(c - 1)
                for j in range(AHEAD, PAIRS):
                    split_w(c, j)
            take(NCH - 1)

        @block.tensor
        def _(pe):
            def chunk(c):
                first = isinstance(c, int)
                for j in range(PAIRS):
                    if first:
                        pe.wait_ge(x_split, PAIR * (j + 1))
                    pe.wait_ge(w_split, c * PAIRS + j + 1)
                    for kk in range(PAIR):
                        k = PAIR * j + kk
                        cols = slice(kk * CH, (kk + 1) * CH)
                        for t in range(BT):
                            if k == 0 and not first:
                                pe.wait_ge(acc_taken, (c - 1) * BT + t + 1)
                            rows = slice(t * P, (t + 1) * P)
                            last = split_product(
                                nc, acc[t][:, :], (x_hi[:, k, rows], x_lo[:, k, rows]),
                                (w_hi[:, j % SPL, cols], w_lo[:, j % SPL, cols]), k == 0, k == KT - 1)
                            if k == KT - 1:
                                last.then_inc(acc_ready, 1)
                    if j < PAIRS - 1:
                        last.then_inc(w_used, 1)

            chunk(0)
            with pe.Fori(1, NCH) as c:
                chunk(c)

        @block.gpsimd
        def _(pool):
            def store(c):
                for t in range(BT):
                    pool.wait_ge(acc_taken, c * BT + t + 1)
                    pool.dma_start(h_dram[c, t], h_out[:, t, :]).then_inc(h_stored[t], 16)

            with pool.Fori(0, NCH) as c:
                store(c)
            for t in range(BT):
                pool.wait_ge(h_stored[t], 16 * NCH)
            pool.wait_ge(stats_done, NCH * BT)


def second_products(nc, keep, e, h_dram, w2, b2, norm2, stats, ident, s_dram):
    QK = 4
    QS = KT // QK
    HALF = B // 2
    HT = BT // 2
    GELUS = 4
    BY_ACT = HT // 2
    with ExitStack() as ctx:
        def sb(name, shape, dt=F32):
            return ctx.enter_context(nc.sbuf_tensor(f"{name}_{e}", shape, dt))
        g_hi = sb("g_hi", [P, KT, B], F32R)
        g_lo = sb("g_lo", [P, KT, B], F32R)
        h_raw = sb("h_raw", [P, 2, HT, CH])
        gelu = sb("gelu", [P, GELUS, HALF])
        w_raw = sb("w2_raw", [P, QS, QK * P])
        w_hi = sb("w2_hi", [P, QS, QK * P], F32R)
        w_lo = sb("w2_lo", [P, QS, QK * P], F32R)
        s_out = sb("s_out", [P, 4, HALF])
        par = sb("norm2", [P, 2, KT])
        bias = sb("b2", [P, KT])
        mv = sb("mv", [P, BT, 2])
        rstd = sb("rstd", [P, 4, BT])
        tr = [ctx.enter_context(nc.psum_tensor(f"turn{e}{i}", [P, HALF], F32)) for i in range(4)]
        acc = [ctx.enter_context(nc.psum_tensor(f"accS{e}{i}", [P, HALF], F32)) for i in range(4)]
        s = Sems(nc, keep, ctx, f"E{e}")
        par_loaded = s.dma("par_loaded")
        h_loaded = s.ring("h_loaded", 2)
        w_loaded = s.ring("w_loaded", QS)
        var_ready, std_ready, mv_ready = s.one("var_ready"), s.one("std_ready"), s.one("mv_ready")
        normed, normed_act, turned = s.one("normed"), s.one("normed_act"), s.one("turned")
        gelu_ready, g_hi_ready, g_split = s.one("gelu_ready"), s.one("g_hi_ready"), s.one("g_split")
        w_hi_ready, w_split, w_used = s.one("w_hi_ready"), s.one("w_split"), s.one("w_used")
        acc_ready, s_ready = s.one("acc_ready"), s.one("s_ready")
        s_stored = s.ring("s_stored", 4)
        block = s.block()

        @block.sync
        def _(sp):
            def load_w(n, u, q):
                if not (isinstance(n, int) and u == 0):
                    sp.wait_ge(w_split, (n * DC + u - 1) * QS + q + 1)
                sp.dma_start(w_raw[:, q, :], w2[e, n, u, q]).then_inc(w_loaded[q], 16)

            for i in range(2 * ECH):
                c, half = i // 2, i % 2
                if i >= 2:
                    sp.wait_ge(turned, (i - 1) * QK)
                sp.dma_start(h_raw[:, half, :, :], h_dram[e * ECH + c, half * HT:(half + 1) * HT]
                             .rearrange("t p f -> p t f")).then_inc(h_loaded[half], 16)
                if i == 0:
                    sp.dma_start(par[:, :, :], norm2[e]).then_inc(par_loaded, 16)
                    sp.dma_start(bias[:, :], b2[e]).then_inc(par_loaded, 16)
                if i == 1:
                    for q in range(QS):
                        load_w(0, 0, q)
            for u in range(1, DC):
                for q in range(QS):
                    load_w(0, u, q)
            with sp.Fori(1, N) as n:
                for u in range(DC):
                    for q in range(QS):
                        load_w(n, u, q)

        @block.scalar
        def _(act):
            def split_w(n, u, q):
                act.wait_ge(w_loaded[q], (n * DC + u + 1) * 16)
                if not (isinstance(n, int) and u == 0):
                    if q < QS - 1:
                        act.wait_ge(w_used, (n * DC + u - 1) * (QS - 1) + q + 1)
                    else:
                        act.wait_ge(acc_ready, (n * DC + u) * 2)
                nc.scalar.activation(w_hi[:, q, :], w_raw[:, q, :], ACT.Copy).then_inc(w_hi_ready, 1)

            act.wait_ge(var_ready, 1)
            nc.scalar.activation(rstd[:, 0, :], rstd[:, 1, :], ACT.Sqrt).then_inc(std_ready, 1)

            def norm(i):
                half = i % 2
                act.wait_ge(h_loaded[half], (i // 2 + 1) * 16)
                for t in range(BY_ACT):
                    row = half * HT + t
                    nc.scalar.activation(h_raw[:, half, t, :], h_raw[:, half, t, :], ACT.Identity,
                                         bias=rstd[:, 3, row:row + 1], scale=rstd[:, 2, row:row + 1]
                                         ).then_inc(normed_act, 1)

            act.wait_ge(mv_ready, 3)
            norm(0)
            act.wait_ge(par_loaded, 32)
            for i in range(2 * ECH):
                c, half = i // 2, i % 2
                if i + 1 < 2 * ECH:
                    norm(i + 1)
                for kk in range(QK):
                    k, m = c * QK + kk, i * QK + kk
                    act.wait_ge(turned, m + 1)
                    if m >= GELUS:
                        act.wait_ge(g_split, m - GELUS + 1)
                    nc.scalar.activation(gelu[:, m % GELUS, :], tr[m % 4][:, :], ACT.Gelu,
                                         bias=par[:, 1, k:k + 1], scale=par[:, 0, k:k + 1]).then_inc(gelu_ready, 1)
                if half == 0:
                    split_w(0, 0, c)
            for u in range(1, DC):
                for q in range(QS):
                    split_w(0, u, q)
            with act.Fori(1, N) as n:
                for u in range(DC):
                    for q in range(QS):
                        split_w(n, u, q)

        @block.vector
        def _(dve):
            def split_w(n, u, q):
                dve.wait_ge(w_hi_ready, (n * DC + u) * QS + q + 1)
                nc.vector.tensor_tensor(w_lo[:, q, :], w_raw[:, q, :], w_hi[:, q, :].bitcast(F32),
                                        ALU.subtract).then_inc(w_split, 1)

            def take(n, u):
                for half in range(2):
                    slot = 2 * (u % 2) + half
                    dve.wait_ge(acc_ready, (n * DC + u) * 2 + half + 1)
                    if not (isinstance(n, int) and u < 2):
                        dve.wait_ge(s_stored[slot], (n * 2 + u // 2) * 16)
                    nc.vector.tensor_scalar(s_out[:, slot, :], acc[slot][:, :],
                                            bias[:, bass.ds(n * DC + u, 1)], None, ALU.add).then_inc(s_ready, 1)

            for t in range(BT):
                last = nc.vector.bn_aggr(mv[:, t, :], stats[:, e * ECH:(e + 1) * ECH, t, :])
            last.then_inc(mv_ready, 1)
            dve.wait_ge(mv_ready, 1)
            nc.vector.tensor_scalar(rstd[:, 1, :], mv[:, :, 1], LN_EPS, None, ALU.add).then_inc(var_ready, 1)
            dve.wait_ge(std_ready, 1)
            nc.vector.reciprocal(rstd[:, 2, :], rstd[:, 0, :]).then_inc(mv_ready, 1)
            dve.wait_ge(mv_ready, 2)
            nc.vector.scalar_tensor_tensor(rstd[:, 3, :], mv[:, :, 0], -1.0, rstd[:, 2, :],
                                           ALU.mult, ALU.mult).then_inc(mv_ready, 1)

            def norm(i):
                half = i % 2
                dve.wait_ge(h_loaded[half], (i // 2 + 1) * 16)
                for t in range(BY_ACT, HT):
                    row = half * HT + t
                    nc.vector.tensor_scalar(h_raw[:, half, t, :], h_raw[:, half, t, :], mv[:, row, 0:1],
                                            rstd[:, 2, row:row + 1], ALU.subtract, ALU.mult).then_inc(normed, 1)

            norm(0)
            for i in range(2 * ECH):
                c, half = i // 2, i % 2
                if i + 1 < 2 * ECH:
                    norm(i + 1)
                for kk in range(QK):
                    k, m = c * QK + kk, i * QK + kk
                    rows = slice(half * HALF, (half + 1) * HALF)
                    dve.wait_ge(gelu_ready, m + 1)
                    nc.vector.tensor_copy(g_hi[:, k, rows], gelu[:, m % GELUS, :]).then_inc(g_hi_ready, 1)
                    dve.wait_ge(g_hi_ready, m + 1)
                    nc.vector.tensor_tensor(g_lo[:, k, rows], gelu[:, m % GELUS, :], g_hi[:, k, rows].bitcast(F32),
                                            ALU.subtract).then_inc(g_split, 1)
                if half == 0:
                    split_w(0, 0, c)
            dve.wait_ge(par_loaded, 32)
            for u in range(1, DC):
                for q in range(QS):
                    split_w(0, u, q)
                take(0, u - 1)
            with dve.Fori(1, N) as n:
                for u in range(DC):
                    for q in range(QS):
                        split_w(n, u, q)
                    if u == 0:
                        take(n - 1, DC - 1)
                    else:
                        take(n, u - 1)
            take(N - 1, DC - 1)

        @block.tensor
        def _(pe):
            def turn(i):
                half = i % 2
                pe.wait_ge(normed, (i + 1) * (HT - BY_ACT))
                pe.wait_ge(normed_act, (i + 1) * BY_ACT)
                for kk in range(QK):
                    m = i * QK + kk
                    if m >= 4:
                        pe.wait_ge(gelu_ready, m - 3)
                    for t in range(HT):
                        last = nc.tensor.transpose(tr[m % 4][:, t * P:(t + 1) * P],
                                                   h_raw[:, half, t, kk * P:(kk + 1) * P], ident[:, :])
                    last.then_inc(turned, 1)

            def products(n, u, q):
                pe.wait_ge(w_split, (n * DC + u) * QS + q + 1)
                for kk in range(QK):
                    k = q * QK + kk
                    cols = slice(kk * P, (kk + 1) * P)
                    for half in range(2):
                        if k == 0 and not (isinstance(n, int) and u < 2):
                            pe.wait_ge(s_ready, (n * DC + u - 2) * 2 + half + 1)
                        rows = slice(half * HALF, (half + 1) * HALF)
                        last = split_product(nc, acc[2 * (u % 2) + half][:, :],
                                             (w_hi[:, q, cols], w_lo[:, q, cols]),
                                             (g_hi[:, k, rows], g_lo[:, k, rows]), k == 0, k == KT - 1)
                        if k == KT - 1 and half == 0:
                            last.then_inc(acc_ready, 1)
                if q < QS - 1:
                    last.then_inc(w_used, 1)
                else:
                    last.then_inc(acc_ready, 1)

            for c in range(ECH):
                turn(2 * c)
                turn(2 * c + 1)
                if c >= 1:
                    pe.wait_ge(g_split, c * 2 * QK)
                    products(0, 0, c - 1)
            pe.wait_ge(g_split, ECH * 2 * QK)
            products(0, 0, QS - 1)
            for u in range(1, DC):
                for q in range(QS):
                    products(0, u, q)
            with pe.Fori(1, N) as n:
                for u in range(DC):
                    for q in range(QS):
                        products(n, u, q)

        @block.gpsimd
        def _(pool):
            def store(n):
                for u in range(DC):
                    for half in range(2):
                        slot = 2 * (u % 2) + half
                        pool.wait_ge(s_ready, (n * DC + u) * 2 + half + 1)
                        pool.dma_start(
                            s_dram[half * HT:(half + 1) * HT, n, :, e, u].rearrange("t p b -> p t b"),
                            s_out[:, slot, :].rearrange("p (t b) -> p t b", b=P)).then_inc(s_stored[slot], 16)
            with pool.Fori(0, N) as n:
                store(n)
            for slot in range(4):
                pool.wait_ge(s_stored[slot], 16 * 2 * N)


def scores(nc, keep, s_dram, wqk, bqk, wvo, w_hi, w_lo, power):
    MATS = 4
    W = N * N * HEADS
    SLOTS = 3
    with ExitStack() as ctx:
        def sb(name, shape, dt=F32):
            return ctx.enter_context(nc.sbuf_tensor(name, shape, dt))
        bias = sb("bqk_parts", [P, MATS, D], F32R)
        picks = sb("picks", [P, P], F32R)
        s_raw = sb("sB_raw", [P, 2, 2, DC * P])
        s_hi = sb("sB_hi", [P, 2, 2, DC * P], F32R)
        s_lo = sb("sB_lo", [P, 2, 2, DC * P], F32R)
        q = sb("q_parts", [P, N, 3, D])
        k = sb("k_parts", [P, 2, N, 3, D])
        prod = sb("prod", [P, SLOTS, N, D])
        part = sb("part", [P, 2, 3, W])
        both = sb("both", [P, 2, 2, W])
        picks_raw = sb("picks_raw", [P, P])
        w_raw = k[:, 1].rearrange("p n i d -> p (n i d)")[:, 0:2 * DC * D].rearrange("p (s x) -> p s x", s=2)
        b_raw = q[:, :, 0, :]
        k_first = k[:, 0].rearrange("p n i d -> p (n i d)")
        next_raw = [k_first[:, m * DC * D:(m + 1) * DC * D] for m in range(3)] + [
            s_raw[:, :, :, :].rearrange("p s e x -> p (s e x)")]
        acc = [[ctx.enter_context(nc.psum_tensor(f"accB{i}{m}", [P, D], F32)) for m in range(MATS)] for i in range(2)]
        s = Sems(nc, keep, ctx, "B")
        w_loaded, bias_loaded = s.ring("w_loaded", 2), s.dma("bias_loaded")
        w_hi_ready, w_split = s.one("w_hi_ready"), s.one("w_split")
        next_loaded, next_hi_ready, next_split = s.ring("next_loaded", MATS), s.one("next_hi_ready"), s.one("next_split")
        zeroed, bias_ready = s.one("zeroed"), s.one("bias_ready")
        s_loaded = s.ring("s_loaded", 2)
        s_hi_ready, s_split = s.one("s_hi_ready"), s.one("s_split")
        acc_ready, copied, k_ready, q_ready = s.one("acc_ready"), s.one("copied"), s.one("k_ready"), s.one("q_ready")
        multiplied, summed, accumulated = s.one("multiplied"), s.one("summed"), s.one("accumulated")
        small = s.one("small")
        PRODS = 3 * N
        SUMS = 2 * N
        SMALL = 5
        block = s.block()

        def first(t, n=0, m=0):
            return isinstance(t, int) and t * N + n < m

        @block.sync
        def _(sp):
            def load_s(t, n):
                if not first(t, n, 2):
                    sp.wait_ge(s_split, t * N + n - 1)
                sp.dma_start(s_raw[:, n % 2, :, :].rearrange("p e x -> p (e x)"), s_dram[t, n]).then_inc(s_loaded[n % 2], 16)

            sp.wait_ge(zeroed, 2)
            for r in (0, 32):
                sp.dma_start(b_raw[r:r + 1, :, :], bqk).then_inc(bias_loaded, 16)
            for m in range(2):
                sp.dma_start(w_raw[:, m, :], wqk[m]).then_inc(w_loaded[m], 16)
            load_s(0, 0)
            for m in range(2, MATS):
                sp.wait_ge(w_split, m - 1)
                sp.dma_start(w_raw[:, m % 2, :], wqk[m]).then_inc(w_loaded[m % 2], 16)
            for n in range(1, N):
                load_s(0, n)
            for n in range(N):
                load_s(1, n)
            with sp.Fori(2, BT) as t:
                for n in range(N):
                    load_s(t, n)
            sp.wait_ge(multiplied, (BT - 1) * PRODS)
            for m in range(MATS):
                if m == 3:
                    sp.wait_ge(s_split, BT * N)
                sp.dma_start(next_raw[m], wvo[m]).then_inc(next_loaded[m], 16)

        @block.scalar
        def _(act):
            def split_s(t, n):
                act.wait_ge(s_loaded[n % 2], (t * 2 + n // 2 + 1) * 16)
                if not first(t, n, 2):
                    act.wait_ge(acc_ready, (t * N + n - 1) * MATS)
                nc.scalar.activation(s_hi[:, n % 2, :, :], s_raw[:, n % 2, :, :], ACT.Copy).then_inc(s_hi_ready, 1)

            def copy(t, u, n):
                if not first(t, 0, 1):
                    act.wait_ge(multiplied, (t - 1) * PRODS + 3 * (n + 1))
                for m, to in enumerate((q[:, n, 0, :], q[:, n, 1, :], k[:, u, n, 0, :])):
                    act.wait_ge(acc_ready, (t * N + n) * MATS + m + 1)
                    nc.scalar.activation(to, acc[n % 2][m][:, :], ACT.Copy).then_inc(copied, 1)

            def accumulate(t, u, n, heads):
                act.wait_ge(multiplied, t * PRODS + 3 * (n + 1))
                for m in range(N):
                    for h in heads:
                        x = prod[:, 2, m, h * HD:(h + 1) * HD]
                        at = (n * N + m) * HEADS + h
                        last = nc.scalar.activation(x, x, ACT.Copy, accum_out=part[:, u, 2, at:at + 1])
                if heads[-1] == HEADS - 1:
                    last.then_inc(accumulated, 1)

            for m in range(MATS):
                act.wait_ge(w_loaded[m % 2], 16 * (m // 2 + 1))
                nc.scalar.activation(w_hi[:, m, :, :], w_raw[:, m % 2, :], ACT.Copy).then_inc(w_hi_ready, 1)
                if m == 0:
                    split_s(0, 0)
            split_s(0, 1)
            act.wait_ge(bias_ready, 3)

            def tile(t, u):
                last_t = isinstance(t, int) and t == BT - 1
                for n in range(N):
                    copy(t, u, n)
                    if not first(t, 0, 1):
                        accumulate(t - 1, 1 - u, n, range(HEADS // 2))
                    if n + 2 < N:
                        split_s(t, n + 2)
                    elif not last_t:
                        split_s(t + 1, n + 2 - N)
                    if not first(t, 0, 1):
                        accumulate(t - 1, 1 - u, n, range(HEADS // 2, HEADS))

            tile(0, 0)
            tile(1, 1)
            with act.Fori(1, BT // 2 - 1) as i:
                tile(i * 2, 0)
                tile(i * 2 + 1, 1)
            tile(BT - 2, 0)
            tile(BT - 1, 1)
            act.wait_ge(acc_ready, BT * N * MATS)
            for m in range(MATS):
                act.wait_ge(next_loaded[m], 16)
                nc.scalar.activation(w_hi[:, m, :, :], next_raw[m], ACT.Copy).then_inc(next_hi_ready, 1)
                accumulate(BT - 1, 1, m, range(HEADS))

        @block.gpsimd
        def _(pool):
            nc.gpsimd.memset(b_raw, 0.0).then_inc(zeroed, 1)
            nc.gpsimd.memset(picks_raw[:, :], 0.0).then_inc(zeroed, 1)
            pool.wait_ge(zeroed, 2)
            for r in (0, 32):
                nc.gpsimd.memset(picks_raw[r:r + 1, :], 1.0).then_inc(zeroed, 1)
            pool.wait_ge(zeroed, 4)

            def split_s(t, n):
                pool.wait_ge(s_hi_ready, t * N + n + 1)
                nc.gpsimd.tensor_tensor(s_lo[:, n % 2, :, :], s_raw[:, n % 2, :, :],
                                        s_hi[:, n % 2, :, :].bitcast(F32), ALU.subtract).then_inc(s_split, 1)

            def add_q(t, n):
                pool.wait_ge(copied, (t * N + n) * 3 + 2)
                nc.gpsimd.tensor_tensor(q[:, n, 2, :], q[:, n, 0, :], q[:, n, 1, :], ALU.add).then_inc(q_ready, 1)

            def combine(t, u):
                pool.wait_ge(summed, (t + 1) * SUMS)
                pool.wait_ge(accumulated, (t + 1) * N)
                m1, m2, m3 = (part[:, u, i, :] for i in range(3))
                re, im = both[:, u, 0, :], both[:, u, 1, :]
                nc.gpsimd.tensor_tensor(re, m1, m3, ALU.add).then_inc(small, 1)
                nc.gpsimd.tensor_tensor(im, m1, m2, ALU.subtract).then_inc(small, 1)
                pool.wait_ge(small, t * SMALL + 2)
                nc.gpsimd.tensor_tensor(re, re, re, ALU.mult).then_inc(small, 1)
                nc.gpsimd.tensor_tensor(im, im, im, ALU.mult).then_inc(small, 1)
                pool.wait_ge(small, t * SMALL + 4)
                nc.gpsimd.tensor_tensor(power[:, t, :], re, im, ALU.add).then_inc(small, 1)

            split_s(0, 0)
            split_s(0, 1)

            def tile(t, u):
                for n in range(N):
                    add_q(t, n)
                    if n + 2 < N:
                        split_s(t, n + 2)
                    elif not (isinstance(t, int) and t == BT - 1):
                        split_s(t + 1, n + 2 - N)
                    if n == N - 1 and not first(t, 0, 1):
                        combine(t - 1, 1 - u)

            tile(0, 0)
            tile(1, 1)
            with pool.Fori(1, BT // 2 - 1) as i:
                tile(i * 2, 0)
                tile(i * 2 + 1, 1)
            tile(BT - 2, 0)
            tile(BT - 1, 1)
            for m in range(MATS):
                pool.wait_ge(next_hi_ready, m + 1)
                nc.gpsimd.tensor_tensor(w_lo[:, m, :, :].rearrange("p c d -> p (c d)"), next_raw[m],
                                        w_hi[:, m, :, :].rearrange("p c d -> p (c d)").bitcast(F32),
                                        ALU.subtract).then_inc(next_split, 1)
            combine(BT - 1, 1)
            pool.wait_ge(small, BT * SMALL)
            pool.wait_ge(next_split, MATS)

        @block.vector
        def _(dve):
            dve.wait_ge(zeroed, 4)
            nc.vector.tensor_copy(picks[:, :], picks_raw[:, :]).then_inc(bias_ready, 1)
            dve.wait_ge(bias_loaded, 32)
            nc.vector.tensor_copy(bias[:, :, :], b_raw).then_inc(bias_ready, 1)
            dve.wait_ge(bias_ready, 2)
            nc.vector.tensor_tensor(bias[32:33, :, :], b_raw[32:33], bias[32:33, :, :].bitcast(F32),
                                    ALU.subtract).then_inc(bias_ready, 1)
            for m in range(MATS):
                dve.wait_ge(w_hi_ready, m + 1)
                nc.vector.tensor_tensor(w_lo[:, m, :, :].rearrange("p c d -> p (c d)"), w_raw[:, m % 2, :],
                                        w_hi[:, m, :, :].rearrange("p c d -> p (c d)").bitcast(F32),
                                        ALU.subtract).then_inc(w_split, 1)

            def finish_k(t, u, n):
                dve.wait_ge(copied, (t * N + n + 1) * 3)
                dve.wait_ge(acc_ready, (t * N + n + 1) * MATS)
                ki = acc[n % 2][3][:, :]
                nc.vector.tensor_tensor(k[:, u, n, 1, :], ki, k[:, u, n, 0, :], ALU.add)
                nc.vector.tensor_tensor(k[:, u, n, 2, :], ki, k[:, u, n, 0, :], ALU.subtract).then_inc(k_ready, 1)

            def tile(t, u, more):
                dve.wait_ge(k_ready, (t + 1) * N)
                pairs = ((2, 0), (0, 1), (1, 2))

                def add_up(n, i):
                    dve.wait_ge(multiplied, t * PRODS + 3 * n + i + 1)
                    nc.vector.tensor_reduce(part[:, u, i, n * N * HEADS:(n + 1) * N * HEADS],
                                            prod[:, i, :, :].rearrange("p m (h d) -> p (m h) d", d=HD),
                                            AX.X, ALU.add).then_inc(summed, 1)

                for n in range(N):
                    dve.wait_ge(q_ready, t * N + n + 1)
                    for i, (a, b) in enumerate(pairs):
                        if not first(t, n, 1):
                            if i < 2:
                                dve.wait_ge(summed, t * SUMS + 2 * n - 1 + i)
                            else:
                                dve.wait_ge(accumulated, t * N + n)
                        nc.vector.tensor_tensor(prod[:, i, :, :], k[:, u, :, b, :],
                                                q[:, n, a, :].unsqueeze(1).to_broadcast([P, N, D]),
                                                ALU.mult).then_inc(multiplied, 1)
                        if i:
                            add_up(n, i - 1)
                    if more:
                        finish_k(t + 1, 1 - u, n)

            for n in range(N):
                finish_k(0, 0, n)
            tile(0, 0, True)
            tile(1, 1, True)
            with dve.Fori(1, BT // 2 - 1) as i:
                tile(i * 2, 0, True)
                tile(i * 2 + 1, 1, True)
            tile(BT - 2, 0, True)
            tile(BT - 1, 1, False)

        @block.tensor
        def _(pe):
            pe.wait_ge(bias_ready, 3)

            def tile(t):
                for n in range(N):
                    pe.wait_ge(s_split, t * N + n + 1)
                    if not first(t, n, 2):
                        pe.wait_ge(copied, (t * N + n - 1) * 3)
                        pe.wait_ge(k_ready, t * N + n - 1)
                    for m in range(MATS):
                        e = m % 2
                        if first(t, n, 1):
                            pe.wait_ge(w_split, m + 1)
                        out = acc[n % 2][m][:, :]
                        nc.tensor.matmul(out, picks[:, :], bias[:, m, :], start=True, stop=False)
                        for c in range(DC):
                            x = slice(c * P, (c + 1) * P)
                            last = split_product(nc, out, (s_hi[:, n % 2, e, x], s_lo[:, n % 2, e, x]),
                                                 (w_hi[:, m, c, :], w_lo[:, m, c, :]), False, c == DC - 1)
                        last.then_inc(acc_ready, 1)

            tile(0)
            with pe.Fori(1, BT) as t:
                tile(t)


def mix_values(nc, keep, power, s_dram, w_hi, w_lo, bv, bo, ident, a_dram):
    W = N * N * HEADS
    with ExitStack() as ctx:
        def sb(name, shape, dt=F32):
            return ctx.enter_context(nc.sbuf_tensor(name, shape, dt))
        s_raw = sb("sV_raw", [P, 2, 2, DC * P])
        s_hi = sb("sV_hi", [P, 2, 2, DC * P], F32R)
        s_lo = sb("sV_lo", [P, 2, 2, DC * P], F32R)
        bias_v = sb("bv_all", [P, 2, D])
        bias_o = sb("bo_cols", [P, 2, DC])
        v = sb("v_rows", [P, 2, 2, N, D])
        prod = sb("prodV", [P, 2, N, D])
        o = sb("mixed", [P, 2, N, D])
        ot_hi = sb("ot_hi", [P, DC, N * P], F32R)
        ot_lo = sb("ot_lo", [P, DC, N * P], F32R)
        a_out = sb("a_out", [P, 2, N, DC, P])
        top = sb("softmax_top", [P, BT, N, HEADS])
        vb = [[ctx.enter_context(nc.psum_tensor(f"accV{i}{e}", [P, D], F32)) for e in range(2)] for i in range(2)]
        tr = [ctx.enter_context(nc.psum_tensor(f"turnV{i}", [P, N * P], F32)) for i in range(2)]
        ob = [ctx.enter_context(nc.psum_tensor(f"accO{i}", [P, N * P], F32)) for i in range(2)]
        s = Sems(nc, keep, ctx, "V")
        bias_loaded = s.dma("bias_loaded")
        s_loaded = s.ring("s_loaded", 2)
        s_hi_ready, s_split = s.one("s_hi_ready"), s.one("s_split")
        soft, root, exped, prob_ready = s.one("soft"), s.one("root"), s.one("exped"), s.one("prob_ready")
        v_ready, v_taken = s.one("v_ready"), s.one("v_taken")
        multiplied, halved, o_ready = s.one("multiplied"), s.one("halved"), s.one("o_ready")
        turned, ot_hi_ready, ot_split = s.one("turned"), s.one("ot_hi_ready"), s.one("ot_split")
        out_ready, out_taken = s.one("out_ready"), s.one("out_taken")
        stored = s.ring("stored", 2)
        block = s.block()

        def first(t, n=0, m=0):
            return isinstance(t, int) and t * N + n < m

        @block.sync
        def _(sp):
            def load_s(t, n):
                if not first(t, n, 2):
                    sp.wait_ge(s_split, t * N + n - 1)
                sp.dma_start(s_raw[:, n % 2, :, :].rearrange("p e x -> p (e x)"), s_dram[t, n]).then_inc(s_loaded[n % 2], 16)

            load_s(0, 0)
            load_s(0, 1)
            sp.dma_start(bias_v[:, :, :], bv.to_broadcast([P, 2, D])).then_inc(bias_loaded, 16)
            sp.dma_start(bias_o[:, :, :], bo).then_inc(bias_loaded, 16)
            for n in range(2, N):
                load_s(0, n)
            with sp.Fori(1, BT) as t:
                for n in range(N):
                    load_s(t, n)

        @block.scalar
        def _(act):
            def split_s(t, n):
                act.wait_ge(s_loaded[n % 2], (t * 2 + n // 2 + 1) * 16)
                if not first(t, n, 2):
                    act.wait_ge(v_ready, (t * N + n - 1) * 2)
                nc.scalar.activation(s_hi[:, n % 2, :, :], s_raw[:, n % 2, :, :], ACT.Copy).then_inc(s_hi_ready, 1)

            def split_o(t, e):
                for c in range(DC):
                    r = (t * 2 + e) * DC + c
                    act.wait_ge(turned, r + 1)
                    if not (isinstance(t, int) and t == 0 and e == 0):
                        act.wait_ge(out_ready, (t * 2 + e) * DC)
                    nc.scalar.activation(ot_hi[:, c, :], tr[c % 2][:, :], ACT.Copy).then_inc(ot_hi_ready, 1)

            def take_out(t, e):
                if not (isinstance(t, int) and t == 0):
                    act.wait_ge(stored[e], t * 16)
                for c in range(DC):
                    act.wait_ge(out_ready, (t * 2 + e) * DC + c + 1)
                    nc.scalar.activation(a_out[:, e, :, c, :], ob[c % 2][:, :].rearrange("p (n b) -> p n b", b=P),
                                         ACT.Identity, bias=bias_o[:, e, c:c + 1]).then_inc(out_taken, 1)

            act.wait_ge(soft, 1)
            nc.scalar.activation(power[:, :, :], power[:, :, :], ACT.Sqrt).then_inc(root, 1)
            split_s(0, 0)
            split_s(0, 1)
            act.wait_ge(soft, 3)
            nc.scalar.activation(power[:, :, :], power[:, :, :], ACT.Exp, scale=HD ** -0.5).then_inc(exped, 1)
            for n in range(2, N):
                split_s(0, n)
            act.wait_ge(bias_loaded, 32)

            def step(t, splits):
                for e in range(2):
                    for half in range(2):
                        if 2 * e + half < splits:
                            split_s(t + 1 + e, 2 * (1 - e) + half)
                        if half == 0:
                            split_o(t, e)
                        else:
                            take_out(t, e)

            split_s(1, 0)
            split_s(1, 1)
            step(0, 4)
            with act.Fori(1, BT - 2) as t:
                step(t, 4)
            step(BT - 2, 2)
            step(BT - 1, 0)

        @block.gpsimd
        def _(pool):
            def split_s(t, n):
                pool.wait_ge(s_hi_ready, t * N + n + 1)
                nc.gpsimd.tensor_tensor(s_lo[:, n % 2, :, :], s_raw[:, n % 2, :, :],
                                        s_hi[:, n % 2, :, :].bitcast(F32), ALU.subtract).then_inc(s_split, 1)

            def store(t, e):
                pool.wait_ge(out_taken, (t * 2 + e + 1) * DC)
                pool.dma_start(a_dram[t, :, :, e].rearrange("n p c b -> p n (c b)"),
                               a_out[:, e].rearrange("p n c b -> p n (c b)")).then_inc(stored[e], 16)

            for n in range(N):
                split_s(0, n)
            split_s(1, 0)
            split_s(1, 1)

            def step(t, splits):
                for e in range(2):
                    for half in range(2):
                        if 2 * e + half < splits:
                            split_s(t + 1 + e, 2 * (1 - e) + half)
                    store(t, e)

            step(0, 4)
            with pool.Fori(1, BT - 2) as t:
                step(t, 4)
            step(BT - 2, 2)
            step(BT - 1, 0)
            for e in range(2):
                pool.wait_ge(stored[e], 16 * BT)

        @block.vector
        def _(dve):
            def take_v(t, u, n):
                for e in range(2):
                    dve.wait_ge(v_ready, (t * N + n) * 2 + e + 1)
                    nc.vector.tensor_tensor(v[:, u, e, n, :], vb[n % 2][e][:, :], bias_v[:, e, :],
                                            ALU.add).then_inc(v_taken, 1)

            def mix(t, u, e, n):
                r = (t * 2 + e) * N + n
                slot = n % 2
                if not (isinstance(t, int) and t == 0 and e == 0 and n < 2):
                    dve.wait_ge(o_ready, r - 1)
                if not (isinstance(t, int) and t == 0):
                    dve.wait_ge(turned, (t * 2 + e - 1) * DC)
                prob = power[:, bass.ds(t, 1), n * N * HEADS:(n + 1) * N * HEADS]
                nc.vector.tensor_tensor(
                    prod[:, slot, :, :].rearrange("p m (h d) -> p (m h) d", d=HD),
                    v[:, u, e, :, :].rearrange("p m (h d) -> p (m h) d", d=HD),
                    prob.rearrange("p t x -> p (t x)").unsqueeze(2).to_broadcast([P, N * HEADS, HD]),
                    ALU.mult).then_inc(multiplied, 1)
                dve.wait_ge(multiplied, r + 1)
                nc.vector.tensor_tensor(prod[:, slot, 0:2, :], prod[:, slot, 0:2, :], prod[:, slot, 2:4, :],
                                        ALU.add).then_inc(halved, 1)
                dve.wait_ge(halved, r + 1)
                nc.vector.tensor_tensor(o[:, e, n, :], prod[:, slot, 0, :], prod[:, slot, 1, :],
                                        ALU.add).then_inc(o_ready, 1)

            def split_o(t, e):
                for c in range(DC):
                    dve.wait_ge(ot_hi_ready, (t * 2 + e) * DC + c + 1)
                    nc.vector.tensor_tensor(ot_lo[:, c, :], tr[c % 2][:, :], ot_hi[:, c, :].bitcast(F32),
                                            ALU.subtract).then_inc(ot_split, 1)

            def step(t, u, more):
                dve.wait_ge(v_taken, (t + 1) * N * 2)
                for e in range(2):
                    for n in range(N):
                        mix(t, u, e, n)
                    for n in range(2 * e, 2 * e + 2):
                        if more:
                            take_v(t + 1, 1 - u, n)
                    split_o(t, e)

            nc.vector.tensor_scalar(power[:, :, :], power[:, :, :], 1e-8, None, ALU.add).then_inc(soft, 1)
            dve.wait_ge(root, 1)
            by_m = power[:, :, :].rearrange("p t (n m h) -> p (t n) h m", n=N, m=N)
            plain = power[:, :, :].rearrange("p t (n m h) -> p (t n) m h", n=N, m=N)
            heads = top[:, :, :, :].rearrange("p t n h -> p (t n) h")
            over_m = heads.unsqueeze(2).to_broadcast([P, BT * N, N, HEADS])
            nc.vector.tensor_reduce(heads, by_m, AX.X, ALU.max).then_inc(soft, 1)
            dve.wait_ge(soft, 2)
            nc.vector.tensor_tensor(plain, plain, over_m, ALU.subtract).then_inc(soft, 1)
            dve.wait_ge(exped, 1)
            nc.vector.tensor_reduce(heads, by_m, AX.X, ALU.add).then_inc(soft, 1)
            dve.wait_ge(soft, 4)
            nc.vector.reciprocal(heads, heads).then_inc(soft, 1)
            dve.wait_ge(soft, 5)
            nc.vector.tensor_tensor(plain, plain, over_m, ALU.mult).then_inc(prob_ready, 1)
            dve.wait_ge(bias_loaded, 32)
            for n in range(N):
                take_v(0, 0, n)
            dve.wait_ge(prob_ready, 1)
            step(0, 0, True)
            step(1, 1, True)
            with dve.Fori(1, BT // 2 - 1) as i:
                step(i * 2, 0, True)
                step(i * 2 + 1, 1, True)
            step(BT - 2, 0, True)
            step(BT - 1, 1, False)

        @block.tensor
        def _(pe):
            def values(t, n):
                pe.wait_ge(s_split, t * N + n + 1)
                for e in range(2):
                    if not first(t, n, 2):
                        pe.wait_ge(v_taken, (t * N + n - 2) * 2 + e + 1)
                    for c in range(DC):
                        x = slice(c * P, (c + 1) * P)
                        last = split_product(nc, vb[n % 2][e][:, :], (s_hi[:, n % 2, e, x], s_lo[:, n % 2, e, x]),
                                             (w_hi[:, e, c, :], w_lo[:, e, c, :]), c == 0, c == DC - 1)
                    last.then_inc(v_ready, 1)

            def project(t, e):
                pe.wait_ge(o_ready, (t * 2 + e + 1) * N)
                for c in range(DC):
                    if not (isinstance(t, int) and t == 0 and e == 0 and c < 2):
                        pe.wait_ge(ot_split, (t * 2 + e) * DC + c - 1)
                    for n in range(N):
                        last = nc.tensor.transpose(tr[c % 2][:, n * P:(n + 1) * P],
                                                   o[:, e, n, c * P:(c + 1) * P], ident[:, :])
                    last.then_inc(turned, 1)
                for to in range(DC):
                    if not (isinstance(t, int) and t == 0 and e == 0 and to < 2):
                        pe.wait_ge(out_taken, (t * 2 + e) * DC + to - 1)
                    for c in range(DC):
                        if to == 0:
                            pe.wait_ge(ot_split, (t * 2 + e) * DC + c + 1)
                        cols = slice(to * P, (to + 1) * P)
                        last = split_product(nc, ob[to % 2][:, :], (w_hi[:, 2 + e, c, cols], w_lo[:, 2 + e, c, cols]),
                                             (ot_hi[:, c, :], ot_lo[:, c, :]), c == 0, c == DC - 1)
                    last.then_inc(out_ready, 1)

            def step(t):
                for e in range(2):
                    values(t + 1, 2 * e)
                    values(t + 1, 2 * e + 1)
                    project(t, e)

            for n in range(N):
                values(0, n)
            step(0)
            with pe.Fori(1, BT - 1) as t:
                step(t)
            for e in range(2):
                project(BT - 1, e)



def mix_states(nc, keep, a_dram, wint, ids, tables, strength, ri_dram):
    SETS = 3
    WR, WI, DIFF, SUM = range(4)
    RAW_OF = (WR, DIFF, SUM)
    PARTS = 3
    PART_OF = (2, 0, 1)
    RING, SPL = 4, 2
    AHEAD = 2
    LAST = N * BT
    with ExitStack() as ctx:
        def sb(name, shape, dt=F32):
            return ctx.enter_context(nc.sbuf_tensor(name, shape, dt))
        w_raw = sb("wint_raw", [P, 4, DC * D])
        w_hi = sb("wint_hi", [P, 2, SETS, DC * D], F32R)
        w_lo = sb("wint_lo", [P, 2, SETS, DC * D], F32R)
        a_raw = sb("a_raw", [P, RING, PARTS, DC * P])
        a_hi = sb("a_hi", [P, SPL, PARTS, DC * P], F32R)
        a_lo = sb("a_lo", [P, SPL, PARTS, DC * P], F32R)
        out = sb("ri_out", [P, RING, 2, D])
        idx = sb("idx", [P, BT, N], I32)
        acc = [[ctx.enter_context(nc.psum_tensor(f"accM{i}{m}", [P, D], F32)) for m in range(SETS)] for i in range(SPL)]
        s = Sems(nc, keep, ctx, "M")
        w_loaded, a_loaded = s.ring("w_loaded", 2), s.ring("a_loaded", RING)
        ids_loaded, gathered = s.dma("ids_loaded"), s.dma("gathered")
        w_combined, w_hi_ready, w_split = s.one("w_combined"), s.one("w_hi_ready"), s.one("w_split")
        a_summed, a_hi_ready, a_split = s.one("a_summed"), s.one("a_hi_ready"), s.one("a_split")
        m1_ready, m2_ready, m3_ready = s.one("m1_ready"), s.one("m2_ready"), s.one("m3_ready")
        m1_taken, r_ready, i_ready = s.one("m1_taken"), s.one("r_ready"), s.one("i_ready")
        stored = s.ring("stored", RING)
        block = s.block()

        @block.sync
        def _(sp):
            def load_w(n):
                for j in range(2):
                    if n:
                        sp.wait_ge(w_split, n * SETS)
                    sp.dma_start(w_raw[:, j, :], wint[n, j]).then_inc(w_loaded[j], 16)

            load_w(0)
            for g in range(LAST):
                if g >= RING:
                    sp.wait_ge(a_split, g - RING + 1)
                sp.dma_start(a_raw[:, g % RING, 0:2, :].rearrange("p e x -> p (e x)"),
                             a_dram[g % BT, g // BT]).then_inc(a_loaded[g % RING], 16)
                if g == 0:
                    sp.dma_start(idx[:, :, :], ids).then_inc(ids_loaded, 16)
                if g % BT == 2 and g // BT < N - 1:
                    load_w(g // BT + 1)

        @block.gpsimd
        def _(pool):
            for g in range(LAST):
                pool.wait_ge(a_loaded[g % RING], (g // RING + 1) * 16)
                nc.gpsimd.tensor_tensor(a_raw[:, g % RING, 2, :], a_raw[:, g % RING, 0, :], a_raw[:, g % RING, 1, :],
                                        ALU.add).then_inc(a_summed, 1)
                if g == 0:
                    pool.wait_ge(ids_loaded, 16)
                t, i = g // N, g % N
                pool.indirect_dma_start(
                    out=strength[:, t, i, :], out_offset=None, in_=tables[i],
                    in_offset=bass.IndirectOffsetOnAxis(ap=idx[:, t, i:i + 1], axis=0)).then_inc(gathered, 16)
            pool.wait_ge(gathered, 16 * BT * N)

        @block.scalar
        def _(act):
            def split_w(n, m):
                if m == 0:
                    act.wait_ge(w_loaded[0], (n + 1) * 16)
                    if n >= 2:
                        act.wait_ge(m3_ready, (n - 1) * BT)
                else:
                    act.wait_ge(w_combined, n * 2 + m)
                nc.scalar.activation(w_hi[:, n % 2, m, :], w_raw[:, RAW_OF[m], :], ACT.Copy).then_inc(w_hi_ready, 1)

            def split_a(g):
                act.wait_ge(a_summed, g + 1)
                if g >= SPL:
                    act.wait_ge(m3_ready, g - SPL + 1)
                nc.scalar.activation(a_hi[:, g % SPL], a_raw[:, g % RING], ACT.Copy).then_inc(a_hi_ready, 1)

            def take(g):
                if g >= RING:
                    act.wait_ge(stored[g % RING], g // RING * 16)
                act.wait_ge(m1_ready, g + 1)
                nc.scalar.activation(out[:, g % RING, 1, :], acc[g % SPL][0][:, :], ACT.Copy).then_inc(m1_taken, 1)

            def store(g):
                act.wait_ge(i_ready, g + 1)
                act.dma_start(ri_dram[g % BT, :, g // BT], out[:, g % RING, :, :].rearrange("p j d -> p (j d)")
                              ).then_inc(stored[g % RING], 16)

            split_w(0, 0)
            split_a(0)
            for m in range(1, SETS):
                split_w(0, m)
            for g in range(1, AHEAD):
                split_a(g)
            for g in range(LAST):
                n, t = g // BT, g % BT
                take(g)
                if g + AHEAD < LAST:
                    split_a(g + AHEAD)
                if g:
                    store(g - 1)
                if n < N - 1 and 3 <= t < 3 + SETS:
                    split_w(n + 1, t - 3)
            store(LAST - 1)
            for slot in range(RING):
                act.wait_ge(stored[slot], 16 * LAST // RING)

        @block.vector
        def _(dve):
            def combine_w(n):
                for j in range(2):
                    dve.wait_ge(w_loaded[j], (n + 1) * 16)
                nc.vector.tensor_tensor(w_raw[:, DIFF, :], w_raw[:, WI, :], w_raw[:, WR, :], ALU.subtract).then_inc(w_combined, 1)
                nc.vector.tensor_tensor(w_raw[:, SUM, :], w_raw[:, WR, :], w_raw[:, WI, :], ALU.add).then_inc(w_combined, 1)

            def split_w(n, m):
                dve.wait_ge(w_hi_ready, n * SETS + m + 1)
                if m:
                    dve.wait_ge(w_combined, n * 2 + m)
                nc.vector.tensor_tensor(w_lo[:, n % 2, m, :], w_raw[:, RAW_OF[m], :], w_hi[:, n % 2, m, :].bitcast(F32),
                                        ALU.subtract).then_inc(w_split, 1)

            def split_a(g):
                dve.wait_ge(a_hi_ready, g + 1)
                nc.vector.tensor_tensor(a_lo[:, g % SPL], a_raw[:, g % RING], a_hi[:, g % SPL].bitcast(F32),
                                        ALU.subtract).then_inc(a_split, 1)

            def take(g):
                dve.wait_ge(m1_taken, g + 1)
                r, i = out[:, g % RING, 0, :], out[:, g % RING, 1, :]
                dve.wait_ge(m3_ready, g + 1)
                nc.vector.tensor_tensor(r, i, acc[g % SPL][2][:, :], ALU.subtract).then_inc(r_ready, 1)
                nc.vector.tensor_tensor(i, i, acc[g % SPL][1][:, :], ALU.add).then_inc(i_ready, 1)

            combine_w(0)
            split_w(0, 0)
            split_a(0)
            for m in range(1, SETS):
                split_w(0, m)
            for g in range(1, AHEAD):
                split_a(g)
            for g in range(LAST):
                n, t = g // BT, g % BT
                take(g)
                if g + AHEAD < LAST:
                    split_a(g + AHEAD)
                if n < N - 1 and t == 2:
                    combine_w(n + 1)
                if n < N - 1 and 3 <= t < 3 + SETS:
                    split_w(n + 1, t - 3)

        @block.tensor
        def _(pe):
            def products(n, u, t, first=False):
                pe.wait_ge(a_split, n * BT + t + 1)
                slot = t % SPL
                for m, (ready, taken) in enumerate(((m1_ready, m1_taken), (m2_ready, i_ready), (m3_ready, r_ready))):
                    if t == 0:
                        pe.wait_ge(w_split, n * SETS + m + 1)
                    if not first:
                        pe.wait_ge(taken, n * BT + t - SPL + 1)
                    for c in range(DC):
                        x, y = slice(c * P, (c + 1) * P), slice(c * D, (c + 1) * D)
                        last = split_product(nc, acc[slot][m][:, :], (a_hi[:, slot, PART_OF[m], x], a_lo[:, slot, PART_OF[m], x]),
                                             (w_hi[:, u, m, y], w_lo[:, u, m, y]), c == 0, c == DC - 1)
                    last.then_inc(ready, 1)

            for t in range(BT):
                products(0, 0, t, t < SPL)
            with pe.Fori(0, N // 2 - 1) as i:
                for u in range(2):
                    for t in range(BT):
                        products(i * 2 + 1 + u, 1 - u, t)
            for t in range(BT):
                products(N - 1, 1, t)
        return gathered


def superpose(nc, keep, strength, gathered, ri_dram, wm, ident, amp):
    PAIRS = [(0, 1), (2, 3), (1, 2), (0, 2), (1, 3), (0, 3)]
    NP = len(PAIRS)
    ORDER = [pair if q < 2 else pair[::-1] for q, pair in enumerate(PAIRS)]
    COMPLETE = [[m for m in pair if not any(m in later for later in ORDER[q + 1:])] for q, pair in enumerate(ORDER)]
    DONE = [m for states in COMPLETE for m in states]
    BEGINS = {q: ORDER[q] for q in range(N // 2)}
    SLOTS, AHEAD = 3, 3
    CB = 4
    BIG = 1e23
    UNROLL = 2
    GAINS = 2 * NP - N
    with ExitStack() as ctx:
        def sb(name, shape, dt=F32):
            return ctx.enter_context(nc.sbuf_tensor(name, shape, dt))
        ri = sb("ri_rows", [P, UNROLL, N, 2, D])
        squares = sb("squaresD", [P, N, 2, D])
        size = sb("size", [P, UNROLL, N, D])
        zero = sb("zero", [P, N, D], F32R)
        uv = sb("uv", [P, N, 2, D])
        prod = sb("pair_products", [P, SLOTS, 2, D])
        gain = sb("gain", [P, N, D])
        term = sb("terms", [P, N, 2, D])
        sup = sb("sup", [P, 2, D])
        norm = sb("norm", [P, BT, 3])
        eps = sb("eps", [P, 1])
        one = sb("one", [P, 1])
        ident_r = sb("ident_r", [P, P], F32R)
        m_hi = sb("meas_hi", [P, 3, DC * OUT], F32R)
        m_lo = sb("meas_lo", [P, 3, DC * OUT], F32R)
        sup_hi = sb("sup_hi", [P, 2, DC, P], F32R)
        sup_lo = sb("sup_lo", [P, 2, DC, P], F32R)
        m_raw = term[:, :, :, :].rearrange("p (j m) i d -> p j (m i d)", j=2)
        side = [ctx.enter_context(nc.psum_tensor(f"sideD{i}", [P, D], F32)) for i in range(2)]
        cos = [ctx.enter_context(nc.psum_tensor(f"cosD{i}", [P, D], F32)) for i in range(CB)]
        total = ctx.enter_context(nc.psum_tensor("totalD", [P, 2, D], F32))
        s = Sems(nc, keep, ctx, "D")
        loaded, first_loaded = s.ring("loaded", UNROLL), s.ring("first_loaded", N)
        constants, eps_ready = s.one("constants"), s.one("eps_ready")
        squared, sized, rooted = s.one("squared"), s.one("sized"), s.one("rooted")
        zeroed, lifted, inverted, directed = s.one("zeroed"), s.one("lifted"), s.one("inverted"), s.one("directed")
        multiplied, cos_ready = s.one("multiplied"), s.one("cos_ready")
        begun, gained = s.one("begun"), s.one("gained")
        term_ready, summed = s.one("term_ready"), s.one("summed")
        length, scale_ready, normed = s.one("length"), s.one("scale_ready"), s.one("normed")
        turned, sup_hi_ready, sup_split = s.one("turned"), s.one("sup_hi_ready"), s.one("sup_split")
        m_loaded = s.dma("m_loaded")
        m_hi_ready, m_lo_ready, m_ready = s.one("m_hi_ready"), s.one("m_lo_ready"), s.one("m_ready")
        measured, amp_squared, amp_summed, amp_ready = (
            s.one(x) for x in ("measured", "amp_squared", "amp_summed", "amp_ready"))
        block = s.block()

        @block.sync
        def _(sp):
            def load(t, u, first):
                if not first:
                    sp.wait_ge(term_ready, (t - 1) * N)
                sp.dma_start(ri[:, u].rearrange("p n j d -> p (n j d)"),
                             ri_dram[t].rearrange("p n x -> p (n x)")).then_inc(loaded[u], 16)

            for n in range(N):
                sp.dma_start(ri[:, 0, n].rearrange("p j d -> p (j d)"), ri_dram[0, :, n]).then_inc(first_loaded[n], 16)
            sp.dma_start(m_raw, wm).then_inc(m_loaded, 16)
            load(1, 1, True)
            with sp.Fori(1, BT // UNROLL) as i:
                for u in range(UNROLL):
                    load(i * UNROLL + u, u, False)

        @block.scalar
        def _(act):
            def square(t):
                act.wait_ge(loaded[t % UNROLL], (t // UNROLL + t % UNROLL) * 16)
                act.wait_ge(sized, t * N)
                nc.scalar.activation(squares[:, :, :, :], ri[:, t % UNROLL], ACT.Square).then_inc(squared, N)

            def root(t):
                act.wait_ge(sized, (t + 1) * N)
                nc.scalar.activation(size[:, t % UNROLL], size[:, t % UNROLL], ACT.Sqrt).then_inc(rooted, N)

            def find_zeros(t, states=slice(0, N)):
                act.wait_ge(rooted, t * N + states.stop)
                if t:
                    act.wait_ge(cos_ready, t * NP)
                nc.scalar.activation(zero[:, states, :], size[:, t % UNROLL, states, :], ACT.Relu, bias=one[:, :],
                                     scale=-BIG).then_inc(zeroed, states.stop - states.start)

            def begin_gains(t):
                for q, states in BEGINS.items():
                    for m in states:
                        i = sum(PAIRS[q]) - m
                        act.wait_ge(cos_ready, t * NP + q + 1)
                        if t:
                            act.wait_ge(term_ready, t * N)
                        nc.scalar.activation(gain[:, m, :], cos[(t % UNROLL * NP + q) % CB][:, :], ACT.Identity,
                                             bias=strength[:, t, m, m:m + 1],
                                             scale=strength[:, t, i, m:m + 1]).then_inc(begun, 1)

            def first_roots():
                for n in range(N):
                    act.wait_ge(first_loaded[n], 16)
                    nc.scalar.activation(squares[:, n], ri[:, 0, n], ACT.Square).then_inc(squared, 1)
                for n in range(N):
                    act.wait_ge(sized, n + 1)
                    nc.scalar.activation(size[:, 0, n, :], size[:, 0, n, :], ACT.Sqrt).then_inc(rooted, 1)
                    find_zeros(0, slice(n, n + 1))

            def square_amp(t):
                for j in range(2):
                    act.wait_ge(measured, t * 2 + j + 1)
                    nc.scalar.activation(sup[:, j, :], side[j][:, :], ACT.Square).then_inc(amp_squared, 1)

            def root_amp(t):
                act.wait_ge(amp_summed, t + 1)
                nc.scalar.activation(amp[:, t, :], amp[:, t, :], ACT.Sqrt).then_inc(amp_ready, 1)

            def measure(t):
                act.wait_ge(summed, (t + 1) * 2)
                junk = squares[:, 0]
                act.wait_ge(sized, min(t + 2, BT) * N)
                nc.scalar.activation(junk, total[:, :, :], ACT.Square, accum_out=norm[:, t, 0:1]).then_inc(length, 1)
                act.wait_ge(length, t * 2 + 1)
                nc.scalar.activation(norm[:, t, 1:2], norm[:, t, 0:1], ACT.Sqrt, bias=eps[:, :]).then_inc(length, 1)

            def normalise(t):
                act.wait_ge(scale_ready, t + 1)
                if t:
                    act.wait_ge(turned, t * 2)
                    act.wait_ge(amp_summed, t)
                nc.scalar.activation(sup[:, :, :], total[:, :, :], ACT.Copy, scale=norm[:, t, 2:3]).then_inc(normed, 1)

            def split_sup(t):
                for j in range(2):
                    act.wait_ge(turned, t * 2 + j + 1)
                    nc.scalar.activation(sup_hi[:, j, :, :], side[j][:, :].rearrange("p (c b) -> p c b", b=P),
                                         ACT.Copy).then_inc(sup_hi_ready, 1)

            nc.scalar.activation(ident_r[:, :], ident[:, :], ACT.Copy).then_inc(constants, 1)
            act.wait_ge(eps_ready, 2)
            first_roots()
            act.wait_ge(m_loaded, 16)
            for j in range(2):
                nc.scalar.activation(m_hi[:, j, :], m_raw[:, j, :], ACT.Copy).then_inc(m_hi_ready, 1)
            act.wait_ge(m_hi_ready, 2)
            nc.scalar.activation(m_hi[:, 2, :], m_hi[:, 1, :].bitcast(F32), ACT.Copy, scale=-1.0).then_inc(m_ready, 1)
            act.wait_ge(m_lo_ready, 2)
            nc.scalar.activation(m_lo[:, 2, :], m_lo[:, 1, :].bitcast(F32), ACT.Copy, scale=-1.0).then_inc(m_ready, 1)
            act.wait_ge(gathered, 16 * BT * N)
            for t in range(BT + 2):
                if 1 <= t <= BT:
                    measure(t - 1)
                if t + 1 < BT:
                    square(t + 1)
                if t >= 2:
                    square_amp(t - 2)
                if t < BT:
                    begin_gains(t)
                if 1 <= t <= BT:
                    normalise(t - 1)
                if t >= 2:
                    root_amp(t - 2)
                if t + 1 < BT:
                    root(t + 1)
                if 1 <= t <= BT:
                    split_sup(t - 1)
                if t + 1 < BT:
                    find_zeros(t + 1)

        @block.gpsimd
        def _(pool):
            def add_squares(t):
                pool.wait_ge(squared, (t + 1) * N)
                if t >= UNROLL:
                    pool.wait_ge(directed, (t - UNROLL + 1) * N)
                nc.gpsimd.tensor_tensor(size[:, t % UNROLL], squares[:, :, 0, :], squares[:, :, 1, :],
                                        ALU.add).then_inc(sized, N)

            def add_amp(t):
                pool.wait_ge(amp_squared, (t + 1) * 2)
                nc.gpsimd.tensor_tensor(amp[:, t, :], sup[:, 0, :], sup[:, 1, :], ALU.add).then_inc(amp_summed, 1)

            for j in range(2):
                pool.wait_ge(m_hi_ready, j + 1)
                nc.gpsimd.tensor_tensor(m_lo[:, j, :], m_raw[:, j, :], m_hi[:, j, :].bitcast(F32),
                                        ALU.subtract).then_inc(m_lo_ready, 1)
            for t in range(BT + 2):
                if t + 1 < BT:
                    add_squares(t + 1)
                if t >= 2:
                    add_amp(t - 2)
            pool.wait_ge(amp_ready, BT)

        @block.tensor
        def _(pe):
            def cosines(t, u, first, pairs=range(NP)):
                for q in pairs:
                    i, j = PAIRS[q]
                    g = u * NP + q
                    bank = cos[g % CB][:, :]
                    if q == 0:
                        pe.wait_ge(zeroed, (t + 1) * N)
                    pe.wait_ge(multiplied, t * NP + q + 1)
                    if q >= CB:
                        assert q - CB in BEGINS
                        pe.wait_ge(begun, t * N + 2 * (q - CB + 1))
                    elif not first:
                        pe.wait_ge(gained, t * GAINS)
                    for part in range(2):
                        nc.tensor.matmul(bank, ident[:, :], prod[:, g % SLOTS, part, :], start=part == 0, stop=False)
                    nc.tensor.matmul(bank, ident_r[:, :], zero[:, i, :], start=False, stop=False)
                    nc.tensor.matmul(bank, ident_r[:, :], zero[:, j, :], start=False, stop=True).then_inc(cos_ready, 1)

            def turn(t, first=False):
                pe.wait_ge(normed, t + 1)
                for j in range(2):
                    if not first:
                        pe.wait_ge(amp_squared, (t - 1) * 2 + j + 1)
                    for c in range(DC):
                        last = nc.tensor.transpose(side[j][:, c * P:(c + 1) * P], sup[:, j, c * P:(c + 1) * P],
                                                   ident[:, :])
                    last.then_inc(turned, 1)

            def measure(t, j, first=False):
                if first:
                    pe.wait_ge(m_ready, 2)
                pe.wait_ge(sup_split, (t + 1) * 2)
                for e in range(2):
                    which = ((0, 2), (1, 0))[j][e]
                    for c in range(DC):
                        cols = slice(c * OUT, (c + 1) * OUT)
                        last = split_product(nc, side[j][:, :], (sup_hi[:, e, c, :], sup_lo[:, e, c, :]),
                                             (m_hi[:, which, cols], m_lo[:, which, cols]),
                                             e == 0 and c == 0, e == 1 and c == DC - 1)
                last.then_inc(measured, 1)

            def add_terms(t, first):
                if not first:
                    pe.wait_ge(normed, t)
                for n in range(N):
                    pe.wait_ge(term_ready, t * N + n + 1)
                    for j in range(2):
                        last = nc.tensor.matmul(total[:, j, :], ident[:, :], term[:, DONE[n], j, :],
                                                start=n == 0, stop=n == N - 1)
                        if n == N - 1:
                            last.then_inc(summed, 1)

            def step(t, u, first=False):
                measure(t - 2, 0, first)
                cosines(t, u, False, range(1))
                measure(t - 2, 1)
                cosines(t, u, False, range(1, NP))
                turn(t - 1)
                add_terms(t, False)

            pe.wait_ge(constants, 1)
            cosines(0, 0, True)
            add_terms(0, True)
            cosines(1, 1, False)
            turn(0, True)
            add_terms(1, False)
            step(2, 0, True)
            step(3, 1)
            with pe.Fori(UNROLL, BT // UNROLL) as i:
                for u in range(UNROLL):
                    step(i * UNROLL + u, u)
            for t in (BT - 2, BT - 1):
                for j in range(2):
                    measure(t, j)
                if t < BT - 1:
                    turn(t + 1)

        @block.vector
        def _(dve):
            def split_sup(t):
                for j in range(2):
                    dve.wait_ge(sup_hi_ready, t * 2 + j + 1)
                    nc.vector.tensor_tensor(sup_lo[:, j, :, :], side[j][:, :].rearrange("p (c b) -> p c b", b=P),
                                            sup_hi[:, j, :, :].bitcast(F32), ALU.subtract).then_inc(sup_split, 1)

            def directions(t, u, splits, states=slice(0, N)):
                k = states.stop - states.start
                before = t * N + states.start
                here = size[:, u, states, :]
                dve.wait_ge(rooted, before + k)
                dve.wait_ge(zeroed, before + k)
                nc.vector.tensor_scalar(here, here, 1e-30, None, ALU.max).then_inc(lifted, k)
                if splits:
                    split_sup(t - 2)
                dve.wait_ge(lifted, before + k)
                nc.vector.reciprocal(here, here).then_inc(inverted, k)
                dve.wait_ge(inverted, before + k)
                nc.vector.tensor_tensor(uv[:, states, :, :], ri[:, u, states],
                                        here.unsqueeze(2).to_broadcast([P, k, 2, D]), ALU.mult).then_inc(directed, k)

            def scale(t):
                dve.wait_ge(length, t * 2 + 2)
                nc.vector.reciprocal(norm[:, bass.ds(t, 1), 2:3], norm[:, bass.ds(t, 1), 1:2]).then_inc(scale_ready, 1)

            def multiply(t, u, q):
                i, j = PAIRS[q]
                nc.vector.tensor_tensor(prod[:, (u * NP + q) % SLOTS], uv[:, i], uv[:, j], ALU.mult).then_inc(multiplied, 1)

            def strengths(t, i, m):
                return strength[:, bass.ds(t, 1), i, m:m + 1].rearrange("p t x -> p (t x)")

            def collect(t, u, q):
                if q in BEGINS:
                    return
                dve.wait_ge(cos_ready, t * NP + q + 1)
                for m in ORDER[q]:
                    i = sum(PAIRS[q]) - m
                    if m in last_gain:
                        dve.wait_ge(gained, t * GAINS + last_gain[m])
                    else:
                        dve.wait_ge(begun, t * N + m + 1)
                    bank = cos[(u * NP + q) % CB][:, :]
                    nc.vector.scalar_tensor_tensor(gain[:, m, :], bank, strengths(t, i, m), gain[:, m, :],
                                                   ALU.mult, ALU.add).then_inc(gained, 1)
                    last_gain[m] = last_gain["count"] = last_gain["count"] + 1

            def finish_gains(t, u, q, first):
                for m in COMPLETE[q]:
                    dve.wait_ge(gained, t * GAINS + last_gain[m])
                    if first:
                        dve.wait_ge(m_lo_ready, 2)
                    nc.vector.tensor_tensor(term[:, m], ri[:, u, m], gain[:, m:m + 1, :].to_broadcast([P, 2, D]),
                                            ALU.mult).then_inc(term_ready, 1)

            def step(t, u, first=False, splits=True):
                if first:
                    for n in range(N):
                        dve.wait_ge(squared, n + 1)
                        nc.vector.tensor_tensor(size[:, 0, n, :], squares[:, n, 0, :], squares[:, n, 1, :],
                                                ALU.add).then_inc(sized, 1)
                last_gain.clear()
                last_gain["count"] = 0
                for q in range(2):
                    if first:
                        for n in PAIRS[q]:
                            directions(t, u, False, slice(n, n + 1))
                    else:
                        directions(t, u, splits and q == 0, slice(2 * q, 2 * q + 2))
                    dve.wait_ge(directed, t * N + 2 * q + 2)
                    multiply(t, u, q)
                multiply(t, u, 2)
                if not first:
                    scale(t - 1)
                for q in range(NP):
                    collect(t, u, q)
                    if q in BEGINS:
                        dve.wait_ge(cos_ready, t * NP + q + 1)
                    if q + AHEAD < NP:
                        multiply(t, u, q + AHEAD)
                    finish_gains(t, u, q, first)

            last_gain = {}
            nc.vector.memset(eps[:, :], 1e-8).then_inc(eps_ready, 1)
            nc.vector.memset(one[:, :], 1.0).then_inc(eps_ready, 1)
            dve.wait_ge(gathered, 16 * BT * N)
            step(0, 0, True, False)
            step(1, 1, False, False)
            with dve.Fori(1, BT // UNROLL) as i:
                for u in range(UNROLL):
                    step(i * UNROLL + u, u)
            split_sup(BT - 2)
            scale(BT - 1)
            split_sup(BT - 1)


def top_layers(nc, keep, amp, h_dram, wpost, wz, w2, w3, b_post, b_top2, norm_post, ident, out):
    HALF = B // 2
    HT = BT // 2
    F2 = 256 // P
    with ExitStack() as ctx:
        def sb(name, shape, dt=F32):
            return ctx.enter_context(nc.sbuf_tensor(name, shape, dt))
        post_w = sb("post_w", [P, DC * OUT])
        z_w = sb("top1_w", [P, DC * CH])
        w2_sb = sb("top2_w", [P, DC * F2 * P])
        w3_sb = sb("top3_w", [P, F2])
        post_b = sb("post_b", [P, OUT])
        par = sb("post_norm", [P, 2, DC])
        b2_sb = sb("top2_b", [P, F2])
        amp_t = sb("amp_t", [P, DC, B])
        z_t = sb("z_t", [P, DC, B])
        r1_t = sb("top1_t", [P, DC, B])
        z = sb("z_rows", [P, BT, OUT])
        r1 = sb("top1_rows", [P, BT, CH])
        r2 = sb("top2_t", [P, F2, B])
        stats = sb("post_stats", [P, BT, 6])
        mv = sb("post_mv", [P, BT, 2])
        rstd = sb("post_rstd", [P, 3, BT])
        y = sb("y_row", [P, B])
        acc = [ctx.enter_context(nc.psum_tensor(f"accT{i}", [P, HALF], F32)) for i in range(6)]
        tr = [ctx.enter_context(nc.psum_tensor(f"turnT{i}", [P, HALF], F32)) for i in range(2)]
        s = Sems(nc, keep, ctx, "T")
        loaded = s.ring("loaded", 7)
        amp_turned, amp_ready = s.one("amp_turned"), s.one("amp_ready")
        posted, z_ready, stats_ready, std_ready, mv_ready, normed = (
            s.one(x) for x in ("posted", "z_ready", "stats_ready", "std_ready", "mv_ready", "normed"))
        turned, z_t_ready, top1_done, r1_ready = (
            s.one(x) for x in ("turned", "z_t_ready", "top1_done", "r1_ready"))
        r1_turned, r1_t_ready, top2_done, r2_ready, top3_done, y_ready = (
            s.one(x) for x in ("r1_turned", "r1_t_ready", "top2_done", "r2_ready", "top3_done", "y_ready"))
        stored = s.dma("stored")
        LOADS = ((post_w[:, :], wpost), (post_b[:, :], b_post.to_broadcast([P, OUT])),
                 (par[:, :, :], norm_post), (z_w[:, :], wz), (r1[:, :, :], h_dram[NCH - 1].rearrange("t p f -> p t f")),
                 (w2_sb[:, :], w2), (b2_sb[:, :], b_top2))
        POST_W, POST_B, PAR, Z_W, X_PART, W2, B2 = range(7)
        block = s.block()

        @block.sync
        def _(sp):
            for i, (to, what) in enumerate(LOADS):
                sp.dma_start(to, what).then_inc(loaded[i], 16)
            sp.dma_start(w3_sb[:, :], w3).then_inc(loaded[W2], 16)
            sp.wait_ge(y_ready, 2)
            sp.dma_start(out, y[0:1, :]).then_inc(stored, 16)
            sp.wait_ge(stored, 16)

        @block.scalar
        def _(act):
            for half in range(2):
                for c in range(DC):
                    i = half * DC + c
                    act.wait_ge(amp_turned, i + 1)
                    nc.scalar.activation(amp_t[:, c, half * HALF:(half + 1) * HALF], tr[i % 2][:, :],
                                         ACT.Copy).then_inc(amp_ready, 1)
            act.wait_ge(stats_ready, BT + 2)
            nc.scalar.activation(rstd[:, 0, :], rstd[:, 1, :], ACT.Sqrt).then_inc(std_ready, 1)
            act.wait_ge(loaded[PAR], 16)
            for half in range(2):
                for c in range(DC):
                    i = half * DC + c
                    act.wait_ge(turned, i + 1)
                    nc.scalar.activation(z_t[:, c, half * HALF:(half + 1) * HALF], tr[i % 2][:, :], ACT.Gelu,
                                         bias=par[:, 1, c:c + 1], scale=par[:, 0, c:c + 1]).then_inc(z_t_ready, 1)
            for half in range(2):
                for c in range(DC):
                    i = half * DC + c
                    act.wait_ge(r1_turned, i + 1)
                    nc.scalar.activation(r1_t[:, c, half * HALF:(half + 1) * HALF], tr[i % 2][:, :],
                                         ACT.Copy).then_inc(r1_t_ready, 1)
            act.wait_ge(loaded[B2], 16)
            for half in range(2):
                for f in range(F2):
                    act.wait_ge(top2_done, half * F2 + f + 1)
                    nc.scalar.activation(r2[:, f, half * HALF:(half + 1) * HALF], acc[f][:, :], ACT.Relu,
                                         bias=b2_sb[:, f:f + 1]).then_inc(r2_ready, 1)

        @block.vector
        def _(dve):
            dve.wait_ge(loaded[POST_B], 16)
            for t in range(BT):
                dve.wait_ge(posted, t + 1)
                nc.vector.tensor_tensor(z[:, t, :], acc[t % 6][:, :], post_b[:, :], ALU.add).then_inc(z_ready, 1)
                dve.wait_ge(z_ready, t + 1)
                nc.vector.bn_stats(stats[:, t, :], z[:, t, :]).then_inc(stats_ready, 1)
            dve.wait_ge(stats_ready, BT)
            for t in range(BT):
                last = nc.vector.bn_aggr(mv[:, t, :], stats[:, t, :])
            last.then_inc(stats_ready, 1)
            dve.wait_ge(stats_ready, BT + 1)
            nc.vector.tensor_scalar(rstd[:, 1, :], mv[:, :, 1], LN_EPS, None, ALU.add).then_inc(stats_ready, 1)
            dve.wait_ge(std_ready, 1)
            nc.vector.reciprocal(rstd[:, 2, :], rstd[:, 0, :]).then_inc(mv_ready, 1)
            dve.wait_ge(mv_ready, 1)
            for t in range(BT):
                nc.vector.tensor_scalar(z[:, t, :], z[:, t, :], mv[:, t, 0:1], rstd[:, 2, t:t + 1],
                                        ALU.subtract, ALU.mult).then_inc(normed, 1)
            dve.wait_ge(loaded[X_PART], 16)
            for t in range(BT):
                dve.wait_ge(top1_done, t + 1)
                nc.vector.tensor_tensor(r1[:, t, :], acc[t % 6][:, :], r1[:, t, :], ALU.add).then_inc(r1_ready, 1)
                dve.wait_ge(r1_ready, 2 * t + 1)
                nc.vector.tensor_scalar(r1[:, t, :], r1[:, t, :], 0.0, None, ALU.max).then_inc(r1_ready, 1)
            for half in range(2):
                dve.wait_ge(top3_done, half + 1)
                nc.vector.tensor_copy(y[0:1, half * HALF:(half + 1) * HALF], acc[4 + half][0:1, :]).then_inc(y_ready, 1)

        @block.tensor
        def _(pe):
            for half in range(2):
                for c in range(DC):
                    i = half * DC + c
                    if i >= 2:
                        pe.wait_ge(amp_ready, i - 1)
                    for t in range(HT):
                        last = nc.tensor.transpose(tr[i % 2][:, t * P:(t + 1) * P],
                                                   amp[:, half * HT + t, c * P:(c + 1) * P], ident[:, :])
                    last.then_inc(amp_turned, 1)
            pe.wait_ge(loaded[POST_W], 16)
            for t in range(BT):
                pe.wait_ge(amp_ready, (t // HT + 1) * DC)
                if t >= 6:
                    pe.wait_ge(z_ready, t - 5)
                for k in range(DC):
                    last = nc.tensor.matmul(acc[t % 6][:, :], amp_t[:, k, t * P:(t + 1) * P],
                                            post_w[:, k * OUT:(k + 1) * OUT], start=k == 0, stop=k == DC - 1)
                last.then_inc(posted, 1)
            for half in range(2):
                pe.wait_ge(normed, (half + 1) * HT)
                for c in range(DC):
                    i = half * DC + c
                    if i >= 2:
                        pe.wait_ge(z_t_ready, i - 1)
                    for t in range(HT):
                        last = nc.tensor.transpose(tr[i % 2][:, t * P:(t + 1) * P],
                                                   z[:, half * HT + t, c * P:(c + 1) * P], ident[:, :])
                    last.then_inc(turned, 1)
            pe.wait_ge(loaded[Z_W], 16)
            pe.wait_ge(z_ready, BT)
            for t in range(BT):
                pe.wait_ge(z_t_ready, (t // HT + 1) * DC)
                if t >= 6:
                    pe.wait_ge(r1_ready, 2 * (t - 6) + 1)
                for k in range(DC):
                    last = nc.tensor.matmul(acc[t % 6][:, :], z_t[:, k, t * P:(t + 1) * P],
                                            z_w[:, k * CH:(k + 1) * CH], start=k == 0, stop=k == DC - 1)
                last.then_inc(top1_done, 1)
            for half in range(2):
                pe.wait_ge(r1_ready, 2 * (half + 1) * HT)
                for c in range(DC):
                    i = half * DC + c
                    pe.wait_ge(r1_t_ready, i - 1) if i >= 2 else pe.wait_ge(z_t_ready, 2 * DC)
                    for t in range(HT):
                        last = nc.tensor.transpose(tr[i % 2][:, t * P:(t + 1) * P],
                                                   r1[:, half * HT + t, c * P:(c + 1) * P], ident[:, :])
                    last.then_inc(r1_turned, 1)
            pe.wait_ge(loaded[W2], 32)
            for half in range(2):
                cols = slice(half * HALF, (half + 1) * HALF)
                pe.wait_ge(r1_t_ready, (half + 1) * DC)
                if half:
                    pe.wait_ge(r2_ready, F2)
                for f in range(F2):
                    for k in range(DC):
                        at = (k * F2 + f) * P
                        last = nc.tensor.matmul(acc[f][:, :], w2_sb[:, at:at + P], r1_t[:, k, cols],
                                                start=k == 0, stop=k == DC - 1)
                    last.then_inc(top2_done, 1)
            for half in range(2):
                pe.wait_ge(r2_ready, (half + 1) * F2)
                for f in range(F2):
                    last = nc.tensor.matmul(acc[4 + half][0:1, :], w3_sb[:, f:f + 1],
                                            r2[:, f, half * HALF:(half + 1) * HALF], start=f == 0, stop=f == F2 - 1)
                last.then_inc(top3_done, 1)


def build(nc, a, out):
    h_dram = nc.dram_tensor("h_rows", [NCH, BT, P, CH], F32, kind="Internal").ap()
    s_dram = nc.dram_tensor("s_feats", [BT, N, P, 2, DC, P], F32, kind="Internal").ap()
    a_dram = nc.dram_tensor("attn_feats", [BT, N, P, 2, DC, P], F32, kind="Internal").ap()
    ri_dram = nc.dram_tensor("ri_states", [BT, P, N, 2 * D], F32, kind="Internal").ap()
    s_flat = s_dram.rearrange("t n p e c b -> t n p (e c b)")
    a_flat = a_dram.rearrange("t n p e c b -> t n p (e c b)")
    with ExitStack() as keep:
        ident = keep.enter_context(nc.sbuf_tensor("ident", [P, P], F32))
        ident_ready = keep.enter_context(nc.semaphore("ident_ready"))
        with nc.Block(no_gpsimd_drain=True) as block:
            @block.sync
            def _(sp):
                sp.dma_start(ident[:, :], a["ident"]).then_inc(ident_ready, 16)
                sp.wait_ge(ident_ready, 16)
        with nc.sbuf_tensor("h_stats", [P, NCH, BT, 6], F32) as stats:
            products_with_x(nc, keep, a["xT"], a["wA"], a["bA"], h_dram, stats)
            for e in range(2):
                second_products(nc, keep, e, h_dram, a["w2"], a["b2"], a["norm2"], stats, ident, s_dram)
        with nc.sbuf_tensor("power", [P, BT, N * N * HEADS], F32) as power:
            with (nc.sbuf_tensor("wide_hi", [P, 4, DC, D], F32R) as w_hi,
                  nc.sbuf_tensor("wide_lo", [P, 4, DC, D], F32R) as w_lo):
                scores(nc, keep, s_flat, a["wqk"], a["bqk"], a["wvo"], w_hi, w_lo, power)
                mix_values(nc, keep, power, s_flat, w_hi, w_lo, a["bv"], a["bo"], ident, a_dram)
        with nc.sbuf_tensor("strength", [P, BT, N, N], F32) as strength:
            gathered = mix_states(nc, keep, a_flat, a["wint"], a["ids"], [a[f"tbl_{i}"] for i in range(N)],
                                  strength, ri_dram)
            with nc.sbuf_tensor("amp", [P, BT, OUT], F32) as amp:
                superpose(nc, keep, strength, gathered, ri_dram, a["wm"], ident, amp)
                top_layers(nc, keep, amp, h_dram, a["wpost"], a["wz"], a["wt2"], a["wt3"],
                                a["b_post"], a["b_top2"], a["norm_post"], ident, out)


def kernel(**inputs):
    import numpy as np
    import concourse.bacc as bacc
    from concourse.bass_utils import run_bass_kernel_spmd

    x = {k.removeprefix("L0_rec_"): np.asarray(v) for k, v in inputs.items()}

    def moving(*names):
        return np.stack([x[n].T.reshape(DC, P, -1).transpose(1, 0, 2).reshape(P, -1) for n in names])

    def columns(a):
        return a.reshape(-1, P).T

    w1 = np.concatenate([x["er_W1"].T, x["ei_W1"].T, x["W_top1"][OUT:]], axis=1)
    arrays = {
        "xT": x["r_x"].T.reshape(KT, P, B),
        "wA": w1.reshape(KT // 2, 2, P, NCH, CH).transpose(3, 0, 2, 1, 4).reshape(NCH, KT // 2, P, 2 * CH),
        "bA": np.concatenate([x["er_b1"], x["ei_b1"], x["b_top1"]])[None],
        "w2": np.stack([x[e + "_W2"].reshape(N, DC, P, 4, 4, P).transpose(0, 1, 3, 5, 4, 2).reshape(N, DC, 4, P, 4 * P)
                        for e in ("er", "ei")]),
        "b2": np.stack([columns(x[e + "_b2"]) for e in ("er", "ei")]),
        "norm2": np.stack([np.stack([columns(x[e + "_g1"]), columns(x[e + "_be1"])], axis=1) for e in ("er", "ei")]),
        "wqk": moving("Wq_r", "Wq_i", "Wk_r", "Wk_i"),
        "bqk": np.stack([x["bq_r"], x["bq_i"], x["bk_r"], x["bk_i"]])[None],
        "wvo": moving("Wv_r", "Wv_i", "Wo_r", "Wo_i"),
        "bv": np.stack([x["bv_r"], x["bv_i"]])[None],
        "bo": np.stack([columns(x["bo_r"]), columns(x["bo_i"])], axis=1),
        "wint": np.stack([x["int_Wr"], x["int_Wi"]], axis=1).transpose(0, 1, 3, 2)
                .reshape(N, 2, DC, P, D).transpose(0, 1, 3, 2, 4).reshape(N, 2, P, DC * D),
        "ids": x["ids"].reshape(BT, P, N).transpose(1, 0, 2),
        "tbl_0": x["tbl_0"], "tbl_1": x["tbl_1"], "tbl_2": x["tbl_2"], "tbl_3": x["tbl_3"],
        "wm": moving("meas_Mr", "meas_Mi").transpose(1, 0, 2),
        "wpost": moving("post_W")[0],
        "wz": x["W_top1"][:OUT].reshape(DC, P, CH).transpose(1, 0, 2).reshape(P, -1),
        "wt2": x["W_top2"].reshape(DC, P, 256).transpose(1, 0, 2).reshape(P, -1),
        "wt3": columns(x["W_top3"][:, 0]),
        "b_post": x["post_b"][None],
        "b_top2": columns(x["b_top2"]),
        "norm_post": np.stack([columns(x["post_g"]), columns(x["post_be"])], axis=1),
        "ident": np.eye(P, dtype=np.float32),
    }
    nc = bacc.Bacc("TRN2", target_bir_lowering=False, num_devices=1)
    arrays = {f"in_{k}": np.ascontiguousarray(v) for k, v in arrays.items()}
    aps = {k[3:]: nc.dram_tensor(k, v.shape, mybir.dt.from_np(v.dtype), kind="ExternalInput").ap()
           for k, v in arrays.items()}
    y = nc.dram_tensor("y", (B, 1), F32, kind="ExternalOutput").ap()
    build(nc, aps, y.rearrange("b one -> one b"))
    r = run_bass_kernel_spmd(nc, [arrays], core_ids=[0])
    return r.results[0]["y"]
```
